# Optimizing a Trainium2 kernel written in Bass

```python
import numpy as np
import jax
import jax.numpy as jnp

def _softmax(x, axis=-1):
    return jax.nn.softmax(x, axis=axis)

def _gelu(x):
    return jax.nn.gelu(x, approximate=True)

def _silu(x):
    return jax.nn.silu(x)

def _sigmoid(x):
    return jax.nn.sigmoid(x)

def _layernorm(x, axis=-1, eps=1e-05):
    m = jnp.mean(x, axis=axis, keepdims=True)
    v = jnp.var(x, axis=axis, keepdims=True)
    return (x - m) / jnp.sqrt(v + eps)

def _scatter_add(tgt, idx, src, axis=0):
    return tgt.at[idx].add(src)

def _segment_sum(src, seg, n):
    return jax.ops.segment_sum(src, seg, n)
kernel_name = 'mk_gnn_resnorm_d4_gnn_r8_c48c98'

def setup_inputs(seed: int=0):
    np.random.seed(seed)
    _w = jnp.asarray

    def _rec_inputs():
        import jax
        import jax.numpy as jnp
        _gk = jax.random.key(seed)
        x = -0.0003713 + 1 * jax.random.normal(jax.random.fold_in(_gk, 1), (6250, 256), jnp.float32)
        _s = jax.random.randint(jax.random.fold_in(_gk, 2), (50000,), 0, 6250, jnp.int32)
        _d = jax.random.randint(jax.random.fold_in(_gk, 3), (50000,), 0, 6250, jnp.int32)
        _loop = jnp.arange(6250, dtype=jnp.int32)
        src = jnp.concatenate([_s, _d, _loop])
        dst = jnp.concatenate([_d, _s, _loop])
        _o = jnp.argsort(dst, stable=True)
        src = src[_o]
        dst = dst[_o]
        edge_type_64 = jax.random.randint(jax.random.fold_in(_gk, 13), (106250,), 0, 64, jnp.int32)
        return (x, src, dst, edge_type_64)
    x, src, dst, edge_type_64 = _rec_inputs()

    def _L0_gnn_setup():
        import jax, jax.numpy as jnp
        import numpy as np
        N_NODES = 6250
        N_EDGES = 100000
        IN_FEAT = 256
        HEADS = 4
        OUT_FEAT = 64
        NEG_SLOPE = 0.2
        key = jax.random.key(seed)
        k1, k2, k3, k4, k5, k6 = jax.random.split(key, 6)
        x = jax.random.normal(k1, (N_NODES, IN_FEAT), dtype=jnp.float32)
        edge_index = jax.random.randint(k2, (2, N_EDGES), 0, N_NODES, dtype=jnp.int64)
        scale = 1.0 / np.sqrt(IN_FEAT)
        W = jax.random.normal(k3, (IN_FEAT, HEADS * OUT_FEAT), dtype=jnp.float32) * scale
        att_src = jax.random.normal(k4, (HEADS, OUT_FEAT), dtype=jnp.float32) * scale
        att_dst = jax.random.normal(k5, (HEADS, OUT_FEAT), dtype=jnp.float32) * scale
        bias = jax.random.normal(k6, (HEADS * OUT_FEAT,), dtype=jnp.float32) * 0.01
        return {'x': x, 'edge_index': edge_index, 'W': W, 'att_src': att_src, 'att_dst': att_dst, 'bias': bias}
    _L0_gnn_all = _L0_gnn_setup()
    _L0_gnn_in = {k: v for k, v in _L0_gnn_all.items() if k in ('W', 'att_src', 'att_dst', 'bias')}
    del _L0_gnn_all

    def _L1_gnn_setup():
        import jax, jax.numpy as jnp
        import numpy as np
        N_NODES = 6250
        N_EDGES = 62500
        IN_DIM = 256
        HID = 64
        HEADS = 4
        N_REL = 64
        key = jax.random.key(seed)
        ks = jax.random.split(key, 16)
        s = 0.02
        return {'node_features': jax.random.normal(ks[0], (N_NODES, IN_DIM), jnp.float32), 'edge_index': jax.random.randint(ks[1], (2, N_EDGES), 0, N_NODES, jnp.int32), 'edge_relations': jax.random.randint(ks[2], (N_EDGES,), 0, N_REL, jnp.int32), 'query_emb': jax.random.normal(ks[3], (IN_DIM,), jnp.float32), 'Wq': jax.random.normal(ks[4], (IN_DIM, HID * HEADS), jnp.float32) * s, 'bq': jnp.zeros((HID * HEADS,), jnp.float32), 'Wk': jax.random.normal(ks[5], (IN_DIM, HID * HEADS), jnp.float32) * s, 'bk': jnp.zeros((HID * HEADS,), jnp.float32), 'Wv': jax.random.normal(ks[6], (IN_DIM, HID * HEADS), jnp.float32) * s, 'bv': jnp.zeros((HID * HEADS,), jnp.float32), 'rel_w': jax.random.normal(ks[7], (N_REL, HID), jnp.float32) * s, 'Wo': jax.random.normal(ks[8], (HID * HEADS, IN_DIM), jnp.float32) * s, 'bo': jnp.zeros((IN_DIM,), jnp.float32), 'gamma': jnp.ones((IN_DIM,), jnp.float32), 'beta': jnp.zeros((IN_DIM,), jnp.float32)}
    _L1_gnn_all = _L1_gnn_setup()
    _L1_gnn_in = {k: v for k, v in _L1_gnn_all.items() if k in ('query_emb', 'Wq', 'bq', 'Wk', 'bk', 'Wv', 'bv', 'rel_w', 'Wo', 'bo', 'gamma', 'beta')}
    del _L1_gnn_all

    def _L2_gnn_setup():
        import jax, jax.numpy as jnp
        import numpy as np
        N = 12500
        E = 200000
        IN = 256
        H = 4
        C = 64
        key = jax.random.key(seed)
        k1, k2, k3, k4, k5, k6 = jax.random.split(key, 6)
        x = jax.random.normal(k1, (N, IN), dtype=jnp.float32)
        edge_index = jax.random.randint(k2, (2, E), 0, N, dtype=jnp.int64)
        W = jax.random.normal(k3, (IN, H * C), dtype=jnp.float32) * (1.0 / np.sqrt(IN))
        att_src = jax.random.normal(k4, (H, C), dtype=jnp.float32) * 0.1
        att_dst = jax.random.normal(k5, (H, C), dtype=jnp.float32) * 0.1
        bias = jax.random.normal(k6, (H * C,), dtype=jnp.float32) * 0.01
        return {'x': x, 'edge_index': edge_index, 'W': W, 'att_src': att_src, 'att_dst': att_dst, 'bias': bias}
    _L2_gnn_all = _L2_gnn_setup()
    _L2_gnn_in = {k: v for k, v in _L2_gnn_all.items() if k in ('W', 'att_src', 'att_dst', 'bias')}
    del _L2_gnn_all

    def _L3_gnn_setup():
        import jax, jax.numpy as jnp
        import numpy as np
        N_NODES = 1250
        N_EDGES = 40000
        D = 256
        key = jax.random.key(seed)
        k1, k2, k3, k4, k5 = jax.random.split(key, 5)
        x = jax.random.normal(k1, (N_NODES, D), dtype=jnp.float32)
        src = jax.random.randint(k2, (N_EDGES,), 0, N_NODES, dtype=jnp.int32)
        dst = jax.random.randint(k3, (N_EDGES,), 0, N_NODES, dtype=jnp.int32)
        s = 1.0 / np.sqrt(D)
        theta_w = jax.random.uniform(k4, (D, D), jnp.float32, -s, s)
        theta_b = jnp.zeros((D,), jnp.float32)
        phi_w = jax.random.uniform(k5, (D, D), jnp.float32, -s, s)
        phi_b = jnp.zeros((D,), jnp.float32)
        return {'x': x, 'src': src, 'dst': dst, 'theta_w': theta_w, 'theta_b': theta_b, 'phi_w': phi_w, 'phi_b': phi_b}
    _L3_gnn_all = _L3_gnn_setup()
    _L3_gnn_in = {k: v for k, v in _L3_gnn_all.items() if k in ('theta_w', 'theta_b', 'phi_w', 'phi_b')}
    del _L3_gnn_all
    return {'x': x, 'src': src, 'dst': dst, 'edge_type_64': edge_type_64, 'L0_gnn_W': _L0_gnn_in['W'], 'L0_gnn_att_src': _L0_gnn_in['att_src'], 'L0_gnn_att_dst': _L0_gnn_in['att_dst'], 'L0_gnn_bias': _L0_gnn_in['bias'], 'L1_gnn_query_emb': _L1_gnn_in['query_emb'], 'L1_gnn_Wq': _L1_gnn_in['Wq'], 'L1_gnn_bq': _L1_gnn_in['bq'], 'L1_gnn_Wk': _L1_gnn_in['Wk'], 'L1_gnn_bk': _L1_gnn_in['bk'], 'L1_gnn_Wv': _L1_gnn_in['Wv'], 'L1_gnn_bv': _L1_gnn_in['bv'], 'L1_gnn_rel_w': _L1_gnn_in['rel_w'], 'L1_gnn_Wo': _L1_gnn_in['Wo'], 'L1_gnn_bo': _L1_gnn_in['bo'], 'L1_gnn_gamma': _L1_gnn_in['gamma'], 'L1_gnn_beta': _L1_gnn_in['beta'], 'L2_gnn_W': _L2_gnn_in['W'], 'L2_gnn_att_src': _L2_gnn_in['att_src'], 'L2_gnn_att_dst': _L2_gnn_in['att_dst'], 'L2_gnn_bias': _L2_gnn_in['bias'], 'L3_gnn_theta_w': _L3_gnn_in['theta_w'], 'L3_gnn_theta_b': _L3_gnn_in['theta_b'], 'L3_gnn_phi_w': _L3_gnn_in['phi_w'], 'L3_gnn_phi_b': _L3_gnn_in['phi_b']}

def reference(x, src, dst, edge_type_64, L0_gnn_W, L0_gnn_att_src, L0_gnn_att_dst, L0_gnn_bias, L1_gnn_query_emb, L1_gnn_Wq, L1_gnn_bq, L1_gnn_Wk, L1_gnn_bk, L1_gnn_Wv, L1_gnn_bv, L1_gnn_rel_w, L1_gnn_Wo, L1_gnn_bo, L1_gnn_gamma, L1_gnn_beta, L2_gnn_W, L2_gnn_att_src, L2_gnn_att_dst, L2_gnn_bias, L3_gnn_theta_w, L3_gnn_theta_b, L3_gnn_phi_w, L3_gnn_phi_b):
    import jax
    import jax.numpy as jnp

    def _L0_gnn_ref(x, edge_index, W, att_src, att_dst, bias):
        import jax, jax.numpy as jnp
        import numpy as np
        N_NODES = 6250
        N_EDGES = 100000
        IN_FEAT = 256
        HEADS = 4
        OUT_FEAT = 64
        NEG_SLOPE = 0.2
        N = x.shape[0]
        H, C = att_src.shape
        h = (x @ W).reshape(N, H, C)
        a_src = jnp.sum(h * att_src[None], axis=-1)
        a_dst = jnp.sum(h * att_dst[None], axis=-1)
        loop = jnp.arange(N, dtype=edge_index.dtype)
        src = jnp.concatenate([edge_index[0], loop])
        dst = jnp.concatenate([edge_index[1], loop])
        alpha = jax.nn.leaky_relu(a_src[src] + a_dst[dst], NEG_SLOPE)
        m = jax.ops.segment_max(alpha, dst, num_segments=N)
        alpha = jnp.exp(alpha - jax.lax.stop_gradient(m)[dst])
        denom = jax.ops.segment_sum(alpha, dst, num_segments=N)
        alpha = alpha / (denom[dst] + 1e-16)
        msg = h[src] * alpha[:, :, None]
        out = jax.ops.segment_sum(msg, dst, num_segments=N)
        out = out.reshape(N, H * C) + bias
        return jax.nn.relu(out)

    def _L1_gnn_ref(node_features, edge_index, edge_relations, query_emb, Wq, bq, Wk, bk, Wv, bv, rel_w, Wo, bo, gamma, beta):
        import jax, jax.numpy as jnp
        import numpy as np
        N_NODES = 6250
        N_EDGES = 62500
        IN_DIM = 256
        HID = 64
        HEADS = 4
        N_REL = 64
        N = node_features.shape[0]
        D = rel_w.shape[1]
        H = Wq.shape[1] // D
        enh = node_features + 0.1 * query_emb[None, :]
        Q = (enh @ Wq + bq).reshape(N, H, D)
        K = (enh @ Wk + bk).reshape(N, H, D)
        V = (enh @ Wv + bv).reshape(N, H, D)
        src, dst = (edge_index[0], edge_index[1])
        rel = rel_w[edge_relations]
        mod_k = K[src] + 0.2 * rel[:, None, :]
        scores = jnp.einsum('ehd,ehd->eh', Q[dst], mod_k) / D ** 0.5
        seg_max = jax.ops.segment_max(scores, dst, num_segments=N)
        ex = jnp.exp(scores - seg_max[dst])
        denom = jax.ops.segment_sum(ex, dst, num_segments=N)
        w = ex / denom[dst]
        agg = jax.ops.segment_sum(w[:, :, None] * V[src], dst, num_segments=N)
        deg = jax.ops.segment_sum(jnp.ones((src.shape[0],), jnp.float32), dst, num_segments=N)
        msgs = jnp.where(deg[:, None, None] > 0, agg, V)
        out = msgs.reshape(N, H * D) @ Wo + bo
        x = out + node_features
        mu = jnp.mean(x, axis=-1, keepdims=True)
        var = jnp.var(x, axis=-1, keepdims=True)
        return (x - mu) / jnp.sqrt(var + 1e-05) * gamma + beta

    def _L2_gnn_ref(x, edge_index, W, att_src, att_dst, bias):
        import jax, jax.numpy as jnp
        import numpy as np
        N = 12500
        E = 200000
        IN = 256
        H = 4
        C = 64
        n = x.shape[0]
        loops = jnp.arange(n, dtype=edge_index.dtype)
        src = jnp.concatenate([edge_index[0], loops])
        dst = jnp.concatenate([edge_index[1], loops])
        xp = (x @ W).reshape(n, H, C)
        a_src = jnp.einsum('nhc,hc->nh', xp, att_src)
        a_dst = jnp.einsum('nhc,hc->nh', xp, att_dst)
        alpha = jax.nn.leaky_relu(a_src[src] + a_dst[dst], negative_slope=0.2)
        amax = jax.ops.segment_max(alpha, dst, num_segments=n)
        amax = jnp.where(jnp.isfinite(amax), amax, 0.0)
        ex = jnp.exp(alpha - amax[dst])
        denom = jax.ops.segment_sum(ex, dst, num_segments=n)
        w = ex / denom[dst]
        msg = xp[src] * w[..., None]
        agg = jax.ops.segment_sum(msg, dst, num_segments=n)
        out = agg.reshape(n, H * C) + bias
        return jax.nn.elu(out)

    def _L3_gnn_ref(x, src, dst, theta_w, theta_b, phi_w, phi_b):
        import jax, jax.numpy as jnp
        import numpy as np
        N_NODES = 1250
        N_EDGES = 40000
        D = 256
        x_src = x[src]
        x_dst = x[dst]
        theta_x = (x_dst - x_src) @ theta_w.T + theta_b
        phi_x = x_src @ phi_w.T + phi_b
        e = jax.nn.relu(theta_x + phi_x)
        out = jax.ops.segment_max(e, dst, num_segments=x.shape[0])
        return jnp.where(jnp.isfinite(out), out, 0.0)
    edge_index = jnp.stack([src, dst])
    x = _layernorm(x + _L0_gnn_ref(x, edge_index, L0_gnn_W, L0_gnn_att_src, L0_gnn_att_dst, L0_gnn_bias), axis=-1)
    x = _layernorm(x + _L1_gnn_ref(x, edge_index, edge_type_64, L1_gnn_query_emb, L1_gnn_Wq, L1_gnn_bq, L1_gnn_Wk, L1_gnn_bk, L1_gnn_Wv, L1_gnn_bv, L1_gnn_rel_w, L1_gnn_Wo, L1_gnn_bo, L1_gnn_gamma, L1_gnn_beta), axis=-1)
    x = _layernorm(x + _L2_gnn_ref(x, edge_index, L2_gnn_W, L2_gnn_att_src, L2_gnn_att_dst, L2_gnn_bias), axis=-1)
    x = _layernorm(x + _L3_gnn_ref(x, src, dst, L3_gnn_theta_w, L3_gnn_theta_b, L3_gnn_phi_w, L3_gnn_phi_b), axis=-1)
    return x

_drawn_inputs = setup_inputs


def setup_inputs(seed=0):
    import zlib

    import numpy as np

    out = dict(_drawn_inputs(seed))
    spreads = {'L1_gnn_bq': (0.0, 0.8),
     'L1_gnn_bk': (0.0, 2.0),
     'L1_gnn_bv': (0.0, 0.423),
     'L1_gnn_bo': (0.0, 0.1),
     'L1_gnn_gamma': (1.0, 0.2),
     'L1_gnn_beta': (0.0, 0.1),
     'L3_gnn_theta_b': (0.0, 0.1),
     'L3_gnn_phi_b': (0.0, 0.1)}
    factors = {'L0_gnn_bias': 6.795,
     'L1_gnn_query_emb': 8.0,
     'L1_gnn_Wq': 8.0,
     'L1_gnn_Wk': 8.0,
     'L1_gnn_Wv': 3.504,
     'L1_gnn_rel_w': 64.0,
     'L2_gnn_bias': 6.804}
    for name, (base, spread) in spreads.items():
        noise = np.random.default_rng([zlib.crc32(name.encode()), seed]).standard_normal(out[name].shape)
        drawn = base * np.exp(spread * noise) if base else spread * noise
        out[name] = jnp.asarray(drawn.astype(out[name].dtype))
    for name, factor in factors.items():
        out[name] = (out[name] * factor).astype(out[name].dtype)
    return out
```

```python
from contextlib import ExitStack

import concourse.bass as bass
import concourse.mybir as mybir
from concourse.alu_op_type import AluOpType as ALU

F32, BF16, I32 = mybir.dt.float32, mybir.dt.bfloat16, mybir.dt.int32
ACT = mybir.ActivationFunctionType
AXX = mybir.AxisListType.X

P = 128
N, E, D, H = 6250, 106250, 256, 4
C = D // H
NREL = 64
CHUNK, WIN = 1024, 128
U = CHUNK // P
NCH = -(-E // CHUNK)
MAXPASS = NCH + N // WIN
SL = 3
NIT = -(-(MAXPASS + 1) // SL)
NK = 2 + SL * NIT
TILES = 50
ROWS = TILES * P
PAD_DST = N + 200
BIG = 1.0e30
EPS = 1e-5
GW = D + 2 * H
AW = D + 2 * H
XW = D + 1


class Chain:

    def __init__(self, eng, sem):
        self.eng, self.sem, self.n = eng, sem, 0

    def do(self, ins):
        self.n += 1
        ins.then_inc(self.sem, 1)
        self.eng.wait_ge(self.sem, self.n)


class Stage:

    def __init__(self, nc, tag):
        self.nc, self.tag, self.ctx, self.sems = nc, tag, ExitStack(), []

    def sb(self, name, shape, dt=F32):
        return self.ctx.enter_context(self.nc.sbuf_tensor(f"{self.tag}_{name}", shape, dt))

    def ps(self, name, shape, dt=F32):
        return self.ctx.enter_context(self.nc.psum_tensor(f"{self.tag}_{name}", shape, dt))

    def sem(self, name):
        s = self.nc.alloc_semaphore(f"{self.tag}_{name}")
        self.sems.append(s)
        return s

    def close(self):
        self.ctx.close()
        self.nc.clear_and_free_semaphores(self.sems)
        self.nc.all_engine_barrier()


def prime(sp, buffers, sems, n, r):
    for buf, sem in zip(buffers, sems):
        sp.dma_start(buf[0:1, 0:1], r["x_dram"][0:1, 0:1]).then_inc(sem, n)


def bcast(ap, shape):
    return ap.to_broadcast(shape)


def setup_stage(nc, d, r):
    s = Stage(nc, "setup")
    dst_i = s.sb("dst_i", [NCH, CHUNK + 2], I32)
    src_i = s.sb("src_i", [NCH, CHUNK], I32)
    typ_i = s.sb("typ_i", [NCH, CHUNK], I32)
    dst_f = s.sb("dst_f", [NCH, CHUNK + 2])
    src_f = s.sb("src_f", [NCH, CHUNK])
    typ_f = s.sb("typ_f", [NCH, CHUNK])
    isfirst = s.sb("isfirst", [NCH, CHUNK])
    islast = s.sb("islast", [NCH, CHUNK])
    upper = s.sb("upper", [P, NCH])
    ones = s.sb("ones", [P, P])
    krow = s.sb("krow", [P, NK])
    lo = s.sb("lo", [NCH, 1])
    hi = s.sb("hi", [NCH, 1])
    span_i = s.sb("span_i", [NCH, 1], I32)
    npass = s.sb("npass", [NCH, 1])
    cum = s.sb("cum", [NCH, 1])
    cumend = s.sb("cumend", [NCH, 1])
    base = s.sb("base", [NCH, 1])
    pick = s.sb("pick", [NCH, NK])
    pick2 = s.sb("pick2", [NCH, NK])
    nodes = s.sb("nodes", [NCH, NK])
    n0b = s.sb("n0b", [P, NK])
    anyb = s.sb("anyb", [P, NK])
    count = s.sb("count", [P, 1])
    its = s.sb("its", [P, NIT])
    nits = s.sb("nits", [P, 1])
    blocks = [(0, P), (P, NK - P)]
    n0c = [s.sb(f"n0c{b}", [P, 1]) for b in range(2)]
    rowf = [s.sb(f"rowf{b}", [P, CHUNK], BF16) for b in range(2)]
    rowd = [s.sb(f"rowd{b}", [P, CHUNK], BF16) for b in range(2)]
    rowt = [s.sb(f"rowt{b}", [P, CHUNK], BF16) for b in range(2)]
    zeros = s.sb("zeros", [P, 2 * D])
    attb = s.sb("attb", [P, 4, D])
    wtmp = s.sb("wtmp", [P, 2, D])
    qcol = s.sb("qcol", [P, 2])
    qmat = s.sb("qmat", [P, 2, P])
    bqkv = s.sb("bqkv", [P, 3 * D])
    phi = s.sb("phi", [P, 2, D])
    tb = s.sb("tb", [P, D])
    pst = [s.ps(f"pst{i}", [P, 512]) for i in range(4)]
    psn = s.ps("psn", [P, 512])
    psa = s.ps("psa", [P, 512])
    psc = s.ps("psc", [P, 512])
    psq = s.ps("psq", [P, 512])

    edges_in = s.sem("edges_in")
    weights_in = s.sem("weights_in")
    iota_done = s.sem("iota_done")
    dve_step = s.sem("dve_step")
    npass_ready = s.sem("npass_ready")
    cum_done = s.sem("cum_done")
    pick_ready = s.sem("pick_ready")
    n0_done = s.sem("n0_done")
    n0_used = s.sem("n0_used")
    tab_done = s.sem("tab_done")
    tab_used = s.sem("tab_used")
    qmat_ready = s.sem("qmat_ready")
    qbias_done = s.sem("qbias_done")
    qbias_used = s.sem("qbias_used")
    rows_ready = s.sem("rows_ready")
    zeros_ready = s.sem("zeros_ready")
    stored = s.sem("stored")
    NE, NW = 5, 24

    jobs = [("pass", "src", u) for u in range(U)] + [("pass", "dst", u) for u in range(U)]
    jobs += [("pass", "last", u) for u in range(U)] + [("row", n, b, h) for n in ("dst", "first", "typ")
                                                      for b in range(2) for h in range(2)]
    source = {"src": src_f, "dst": dst_f, "last": islast, "first": isfirst, "typ": typ_f}

    with nc.Block() as block:
        @block.sync
        def _(sp):
            flat = d["dst"]
            view = lambda a: flat[a:a + NCH * CHUNK].rearrange("(c e) -> c e", e=CHUNK)
            sp.dma_start(dst_i[:, 1:CHUNK + 1], view(1)).then_inc(edges_in, 16)
            sp.dma_start(dst_i[:, 0:1], view(0)[:, 0:1], allow_slow_non_contiguous=True).then_inc(edges_in, 16)
            sp.dma_start(dst_i[:, CHUNK + 1:CHUNK + 2], view(2)[:, CHUNK - 1:CHUNK],
                         allow_slow_non_contiguous=True).then_inc(edges_in, 16)
            sp.dma_start(src_i[:, :], d["src"]).then_inc(edges_in, 16)
            sp.dma_start(typ_i[:, :], d["typ"]).then_inc(edges_in, 16)

            def weight(dst, src):
                sp.dma_start(dst, src).then_inc(weights_in, 16)

            def halves(w):
                return w.rearrange("(a p) n -> p a n", p=P)

            weight(r["w0"][:, :, 0:D], halves(d["W0"]))
            weight(r["w2"][:, :, 0:D], halves(d["W2"]))
            for i, name in enumerate(("as0", "ad0", "as2", "ad2")):
                weight(attb[:, i, :], bcast(d[name].rearrange("(a h) c -> a (h c)", a=1), [P, D]))
            for i, name in enumerate(("Wk", "Wv", "Wq")):
                weight(r["wkvq"][:, :, i * D:(i + 1) * D], halves(d[name]))
            for i, name in enumerate(("bk", "bv", "bq")):
                weight(bqkv[:, i * D:(i + 1) * D], bcast(d[name].rearrange("(a n) -> a n", a=1), [P, D]))
            weight(r["wo"][:, :, :], halves(d["Wo"]))
            sp.dma_start(qcol[:, :], d["query"].rearrange("(a p) -> p a", p=P),
                         allow_slow_non_contiguous=True).then_inc(weights_in, 16)
            weight(r["relw"][:, :], d["rel"])
            for name in ("b0", "b2", "bo", "gamma", "beta"):
                weight(r[name][:, :], bcast(d[name].rearrange("(a n) -> a n", a=1), [P, D]))
            weight(r["w3"][:, :, D:2 * D], halves(d["thetaT"]))
            weight(phi[:, :, :], halves(d["phiT"]))
            weight(r["b3"][:, D:2 * D], bcast(d["theta_b"].rearrange("(a n) -> a n", a=1), [P, D]))
            weight(tb[:, :], bcast(d["phi_b"].rearrange("(a n) -> a n", a=1), [P, D]))
            sp.wait_ge(zeros_ready, 1)
            n = 0
            for acc, w in (("agg", AW), ("aggx", XW)):
                for a in range(N, ROWS, P):
                    m = min(P, ROWS - a)
                    sp.dma_start(d[acc][a:a + m, :], zeros[0:m, 0:w]).then_inc(stored, 16)
                    n += 1
            sp.wait_ge(rows_ready, 1)
            for b, (k0, m) in enumerate(blocks):
                for t, dr in ((rowd, "dstrow"), (rowf, "firstrow"), (rowt, "typrow")):
                    sp.dma_start(d[dr][k0:k0 + m, :], t[b][0:m, :]).then_inc(stored, 16)
                    n += 1
            sp.wait_ge(stored, 16 * n)

        @block.gpsimd
        def _(pool):
            nc.gpsimd.iota(r["iota_i"][:, 0:P], [[1, P]], base=0, channel_multiplier=0).then_inc(iota_done, 1)
            nc.gpsimd.iota(r["iota_i"][:, P:P + NK], [[1, NK]], base=-1, channel_multiplier=0).then_inc(iota_done, 1)
            nc.gpsimd.iota(r["iota_i"][:, P + NK:P + NK + 1], [[1, 1]], base=0, channel_multiplier=1).then_inc(iota_done, 1)

        @block.vector
        def _(dve):
            v = nc.vector
            c = Chain(dve, dve_step)
            dve.wait_ge(iota_done, 3)
            c.do(v.tensor_copy(r["iota_row"][:, :], r["iota_i"][:, 0:P]))
            c.do(v.tensor_copy(krow[:, :], r["iota_i"][:, P:P + NK]))
            c.do(v.tensor_copy(r["iota_col"][:, :], r["iota_i"][:, P + NK:P + NK + 1]))
            c.do(v.tensor_scalar(r["ident"][:, :], r["iota_row"][:, :], r["iota_col"][:, 0:1], None, ALU.is_equal))
            c.do(v.tensor_scalar(upper[:, :], r["iota_row"][:, 0:NCH], r["iota_col"][:, 0:1], None, ALU.is_gt))
            c.do(v.memset(ones[:, :], 1.0))
            v.memset(zeros[:, :], 0.0).then_inc(zeros_ready, 1)
            dve.wait_ge(edges_in, 16 * NE)
            c.do(v.tensor_copy(dst_f[:, :], dst_i[:, :]))
            c.do(v.tensor_copy(src_f[:, :], src_i[:, :]))
            c.do(v.tensor_copy(typ_f[:, :], typ_i[:, :]))
            c.do(v.tensor_scalar(lo[:, :], r["iota_col"][0:NCH, 0:1], 0.0, None, ALU.is_gt))
            c.do(v.tensor_tensor(lo[:, :], lo[:, :], dst_f[:, 1:2], ALU.mult))
            c.do(v.tensor_scalar(hi[:, :], dst_f[:, CHUNK + 1:CHUNK + 2], float(N), None, ALU.min))
            c.do(v.tensor_tensor(span_i[:, :], hi[:, :], lo[:, :], ALU.subtract))
            c.do(v.tensor_scalar(span_i[:, :], span_i[:, :], WIN.bit_length() - 1, None, ALU.arith_shift_right))
            c.do(v.tensor_copy(npass[:, :], span_i[:, :]))
            v.tensor_scalar(npass[:, :], npass[:, :], 1.0, None, ALU.add).then_inc(npass_ready, 1)
            c.do(v.tensor_tensor(isfirst[:, :], dst_f[:, 1:CHUNK + 1], dst_f[:, 0:CHUNK], ALU.not_equal))
            c.do(v.tensor_tensor(islast[:, :], dst_f[:, 1:CHUNK + 1], dst_f[:, 2:CHUNK + 2], ALU.not_equal))
            c.do(v.memset(islast[:, CHUNK - 1:CHUNK], 1.0))
            dve.wait_ge(cum_done, 1)
            c.do(v.tensor_copy(cum[:, :], psn[0:NCH, 0:1]))
            dve.wait_ge(npass_ready, 1)
            c.do(v.tensor_tensor(cumend[:, :], cum[:, :], npass[:, :], ALU.add))
            c.do(v.tensor_scalar(pick[:, :], krow[0:NCH, :], cum[:, 0:1], None, ALU.is_ge))
            c.do(v.tensor_scalar(pick2[:, :], krow[0:NCH, :], cumend[:, 0:1], None, ALU.is_lt))
            c.do(v.tensor_tensor(pick[:, :], pick[:, :], pick2[:, :], ALU.mult))
            c.do(v.scalar_tensor_tensor(base[:, :], cum[:, :], float(-WIN), lo[:, :], ALU.mult, ALU.add))
            c.do(v.tensor_scalar(nodes[:, :], krow[0:NCH, :], float(WIN), base[:, 0:1], ALU.mult, ALU.add))
            v.tensor_tensor(nodes[:, :], nodes[:, :], pick[:, :], ALU.mult).then_inc(pick_ready, 1)
            dve.wait_ge(n0_done, 1)
            c.do(v.tensor_copy(anyb[:, :], psa[:, 0:NK]))
            c.do(v.scalar_tensor_tensor(n0b[:, :], anyb[:, :], float(-N), psn[:, 16:16 + NK], ALU.mult, ALU.add))
            c.do(v.tensor_scalar(n0b[:, :], n0b[:, :], float(N), None, ALU.add))
            c.do(v.memset(r["n0_i"][:, 0:2], N))
            c.do(v.tensor_copy(r["n0_i"][:, 2:2 + NK], n0b[0:1, :]))
            c.do(v.memset(r["delta"][:, 0:1], -1.0))
            c.do(v.tensor_tensor(r["delta"][:, 1:NK], n0b[:, 1:NK], n0b[:, 0:NK - 1], ALU.subtract))
            c.do(v.reduce_sum(count[:, :], anyb[:, :], axis=AXX))
            c.do(v.tensor_scalar(its[:, :], r["iota_row"][:, 0:NIT], float(SL), None, ALU.mult))
            c.do(v.tensor_scalar(its[:, :], its[:, :], count[:, 0:1], None, ALU.is_le))
            c.do(v.reduce_sum(nits[:, :], its[:, :], axis=AXX))
            c.do(v.tensor_copy(r["nits_i"][:, :], nits[0:1, :]))
            for b, (k0, m) in enumerate(blocks):
                c.do(v.tensor_scalar(n0c[b][0:m, :], psc[0:m, 2 * b:2 * b + 1], float(-N), None, ALU.mult))
                c.do(v.scalar_tensor_tensor(n0c[b][0:m, :], psc[0:m, 2 * b + 1:2 * b + 2], 1.0, n0c[b][0:m, :],
                                            ALU.mult, ALU.add))
                c.do(v.tensor_scalar(n0c[b][0:m, :], n0c[b][0:m, :], float(N), None, ALU.add))
            for i, job in enumerate(jobs):
                ps = pst[i % 4]
                dve.wait_ge(tab_done, i + 1)
                if job[0] == "pass":
                    _, name, u = job
                    if name == "dst":
                        ins = v.tensor_tensor(r["dstloc"][:, :, u], ps[:, 0:NK], n0b[:, :], ALU.subtract)
                    else:
                        out = r["src_pass"] if name == "src" else r["islast"]
                        ins = v.tensor_copy(out[:, :, u], ps[:, 0:NK])
                else:
                    _, name, b, h = job
                    m, cols = blocks[b][1], slice(h * 512, (h + 1) * 512)
                    if name == "dst":
                        ins = v.tensor_scalar(rowd[b][0:m, cols], ps[0:m, :], n0c[b][0:m, 0:1], None, ALU.subtract)
                    elif name == "first":
                        ins = v.tensor_scalar(rowf[b][0:m, cols], ps[0:m, :], -BIG, None, ALU.mult)
                    else:
                        ins = v.tensor_copy(rowt[b][0:m, cols], ps[0:m, :])
                ins.then_inc(tab_used, 1)
            dve.wait_ge(tab_used, len(jobs))
            c.do(v.tensor_scalar(r["lastloc"][:, :, :], r["dstloc"][:, :, :], 1.0, None, ALU.add))
            c.do(v.tensor_tensor(r["lastloc"][:, :, :], r["lastloc"][:, :, :], r["islast"][:, :, :], ALU.mult))
            c.do(v.tensor_scalar(r["lastloc"][:, :, :], r["lastloc"][:, :, :], -1.0, None, ALU.add))
            v.memset(wtmp[:, :, :], 0.0).then_inc(rows_ready, 1)
            dve.wait_ge(rows_ready, 1)
            dve.wait_ge(weights_in, 16 * NW)
            for w, i0 in (("w0", 0), ("w2", 2)):
                for i in range(2):
                    c.do(v.tensor_tensor(wtmp[:, :, :], r[w][:, :, 0:D],
                                         bcast(attb[:, i0 + i, :].unsqueeze(1), [P, 2, D]), ALU.mult))
                    c.do(v.reduce_sum(r[w][:, :, D + H * i:D + H * (i + 1)],
                                      wtmp[:, :, :].rearrange("p a (h c) -> p a h c", c=C), axis=AXX))
            c.do(v.tensor_scalar(r["wkvq"][:, :, 2 * D:3 * D], r["wkvq"][:, :, 2 * D:3 * D], C ** -0.5, None, ALU.mult))
            c.do(v.tensor_scalar(bqkv[:, 2 * D:3 * D], bqkv[:, 2 * D:3 * D], C ** -0.5, None, ALU.mult))
            c.do(v.tensor_scalar(r["relw"][:, :], r["relw"][:, :], 0.2, None, ALU.mult))
            c.do(v.tensor_tensor(r["w3"][:, :, 0:D], phi[:, :, :], r["w3"][:, :, D:2 * D], ALU.subtract))
            c.do(v.memset(r["b3"][:, 0:D], 0.0))
            c.do(v.tensor_tensor(r["b3"][:, D:2 * D], r["b3"][:, D:2 * D], tb[:, :], ALU.add))
            c.do(v.tensor_scalar(qcol[:, :], qcol[:, :], 0.1, None, ALU.mult))
            v.tensor_copy(qmat[:, :, :], bcast(qcol[:, :].unsqueeze(2), [P, 2, P])).then_inc(qmat_ready, 1)
            for i in range(3):
                dve.wait_ge(qbias_done, i + 1)
                v.tensor_tensor(r["b1"][:, i * D:(i + 1) * D], psq[:, 0:D], bqkv[:, i * D:(i + 1) * D],
                                ALU.add).then_inc(qbias_used, 1)
            c.do(v.memset(r["zero_b"][:, :], 0.0))
            c.do(v.memset(r["mean"][:, :], 0.0))
            c.do(v.memset(r["rstd"][:, :], 1.0))

        @block.tensor
        def _(pe):
            t = nc.tensor
            pe.wait_ge(npass_ready, 1)
            t.matmul(psn[0:NCH, 0:1], upper[0:NCH, :], npass[:, :], start=True, stop=True).then_inc(cum_done, 1)
            pe.wait_ge(pick_ready, 1)
            t.matmul(psa[:, 0:NK], ones[0:NCH, :], pick[:, :], start=True, stop=True)
            for b, (k0, m) in enumerate(blocks):
                t.matmul(psc[0:m, 2 * b:2 * b + 1], pick[:, k0:k0 + m], ones[0:NCH, 0:1], start=True, stop=True)
                t.matmul(psc[0:m, 2 * b + 1:2 * b + 2], nodes[:, k0:k0 + m], ones[0:NCH, 0:1], start=True, stop=True)
            t.matmul(psn[:, 16:16 + NK], ones[0:NCH, :], nodes[:, :], start=True, stop=True).then_inc(n0_done, 1)
            for i, job in enumerate(jobs):
                ps = pst[i % 4]
                if i >= 4:
                    pe.wait_ge(tab_used, i - 3)
                if job[0] == "pass":
                    _, name, u = job
                    x = source[name]
                    o = 1 if name == "dst" else 0
                    ins = t.matmul(ps[:, 0:NK], x[:, o + u * P:o + (u + 1) * P], pick[:, :], start=True, stop=True)
                else:
                    _, name, b, h = job
                    k0, m = blocks[b]
                    o = (1 if name == "dst" else 0) + h * 512
                    ins = t.matmul(ps[0:m, :], pick[:, k0:k0 + m], source[name][:, o:o + 512], start=True, stop=True)
                ins.then_inc(tab_done, 1)
            pe.wait_ge(qmat_ready, 1)
            for i in range(3):
                if i:
                    pe.wait_ge(qbias_used, i)
                w = r["wkvq"][:, :, i * D:(i + 1) * D]
                t.matmul(psq[:, 0:D], qmat[:, 0, :], w[:, 0, :], start=True, stop=False)
                t.matmul(psq[:, 0:D], qmat[:, 1, :], w[:, 1, :], start=False, stop=True).then_inc(qbias_done, 1)
    s.close()


def project_stage(nc, d, r, y, tag, weights, bias, cols, stores):
    s = Stage(nc, tag)
    B = 2
    xn = [s.sb(f"xn{b}", [P, D]) for b in range(B)]
    xT = [s.sb(f"xT{b}", [P, D]) for b in range(B)]
    ob = [s.sb(f"ob{b}", [P, cols]) for b in range(B)]
    psT = [s.ps(f"psT{b}", [P, 512]) for b in range(B)]
    psO = [s.ps(f"psO{b}", [P, -(-cols // 512) * 512]) for b in range(B)]
    pieces = [(a, min(a + 512, cols)) for a in range(0, cols, 512)]
    ready = s.sem("ready")
    norm_done = s.sem("norm_done")
    kept = [s.sem(f"kept{b}") for b in range(B)]
    transposed, xT_ready = s.sem("transposed"), s.sem("xT_ready")
    product_done, row_ready = s.sem("product_done"), s.sem("row_ready")
    stored = [s.sem(f"stored{b}") for b in range(B)]
    CR = B
    at = lambda t: t + 1 + CR

    NST = 16 * len(stores)

    with nc.Block() as block:
        @block.gpsimd
        def _(pool):
            for x in (norm_done, transposed, xT_ready, product_done, row_ready):
                pool.sem_inc(x, CR)
            pool.sem_inc(ready, 1)

        @block.vector
        def _(dve):
            dve.wait_ge(ready, 1)
            with dve.Fori(0, TILES // B) as i:
                for b in range(B):
                    t = i * B + b
                    dve.wait_ge(transposed, at(t - B))
                    dve.wait_ge(kept[b], 16 * (i + 1))
                    nc.vector.tensor_scalar(xn[b][:, :], y[:, bass.ds(t * D, D)], r["mean"][:, bass.ds(t, 1)],
                                            r["rstd"][:, bass.ds(t, 1)], ALU.subtract, ALU.mult).then_inc(norm_done, 1)
                    dve.wait_ge(product_done, at(t))
                    dve.wait_ge(stored[b], NST * (i + 1))
                    nc.vector.tensor_tensor(ob[b][:, :], psO[b][:, 0:cols], bias, ALU.add).then_inc(row_ready, 1)

        @block.tensor
        def _(pe):
            pe.wait_ge(ready, 1)
            with pe.Fori(0, TILES // B) as i:
                for b in range(B):
                    t = i * B + b
                    pe.wait_ge(xT_ready, at(t - B))
                    pe.wait_ge(norm_done, at(t))
                    nc.tensor.transpose(psT[b][:, 0:P], xn[b][:, 0:P], r["ident"][:, :])
                    nc.tensor.transpose(psT[b][:, P:D], xn[b][:, P:D], r["ident"][:, :]).then_inc(transposed, 1)
                    pe.wait_ge(row_ready, at(t - B))
                    pe.wait_ge(xT_ready, at(t))
                    for a, e in pieces:
                        nc.tensor.matmul(psO[b][:, a:e], xT[b][:, 0:P], weights[:, 0, a:e], start=True, stop=False)
                        ins = nc.tensor.matmul(psO[b][:, a:e], xT[b][:, P:D], weights[:, 1, a:e], start=False, stop=True)
                    ins.then_inc(product_done, 1)

        @block.scalar
        def _(act):
            act.wait_ge(ready, 1)
            with act.Fori(0, TILES // B) as i:
                for b in range(B):
                    t = i * B + b
                    act.wait_ge(product_done, at(t - B))
                    act.wait_ge(transposed, at(t))
                    nc.scalar.copy(xT[b][:, :], psT[b][:, 0:D]).then_inc(xT_ready, 1)

        @block.sync
        def _(sp):
            prime(sp, ob, stored, NST, r)
            prime(sp, xn, kept, 16, r)
            sp.wait_ge(ready, 1)
            with sp.Fori(0, TILES // B) as i:
                for b in range(B):
                    t = i * B + b
                    sp.wait_ge(norm_done, at(t))
                    sp.dma_start(d["x"][bass.ds(t * P, P), :], xn[b][:, :]).then_inc(kept[b], 16)
                    sp.wait_ge(row_ready, at(t))
                    for k, (a, e, dram) in enumerate(stores):
                        ins = sp.dma_start(dram[bass.ds(t * P, P), :], ob[b][:, a:e])
                        ins.then_inc(stored[b], 16)
            for b in range(B):
                sp.wait_ge(stored[b], NST * (1 + TILES // B))
                sp.wait_ge(kept[b], 16 * (1 + TILES // B))
    s.close()


def edge_stage(nc, d, r, tag, relational):
    s = Stage(nc, tag)
    V0 = D if relational else 0
    tab, gw = (d["kv"], 2 * D) if relational else (d["h"], GW)
    wcols = (0, D) if relational else (D + H, D + 2 * H)
    wtab = d["q"] if relational else d["h"]
    WC = wcols[1] - wcols[0]
    idx = [s.sb(f"idx{j}", [P, U], I32) for j in range(SL)]
    G = [s.sb(f"G{j}", [P, U, gw]) for j in range(SL)]
    dstrow = [s.sb(f"dstrow{j}", [P, CHUNK], BF16) for j in range(SL)]
    firstrow = [s.sb(f"firstrow{j}", [H, CHUNK], BF16) for j in range(SL)]
    window = [s.sb(f"window{j}", [P, WC]) for j in range(SL)]
    onehot = [s.sb(f"onehot{j}", [P, U, P]) for j in range(SL)]
    onehotT = [s.sb(f"onehotT{j}", [P, CHUNK]) for j in range(SL)]
    ph = [s.sb(f"ph{j}", [P, U, D + H]) for j in range(SL)]
    outw = [s.sb(f"outw{j}", [P, AW]) for j in range(SL)]
    shift = s.sb("shift", [P, P])
    scanned = [s.sb(f"scanned{j}", [H, CHUNK]) for j in range(SL)]
    ssum = s.sb("ssum", [P, U, H])
    score = s.sb("score", [P, U, H])
    lastmax = s.sb("lastmax", [P, U, H])
    expin = s.sb("expin", [P, U, H])
    gin = s.sb("gin", [P, H])
    gex = s.sb("gex", [P, H])
    carried = s.sb("carried", [P, D + H])
    psT = s.ps("psT", [H, CHUNK])
    psO = s.ps("psO", [P, 512])
    psC = s.ps("psC", [P, 512])
    psS = s.ps("psS", [P, 512])
    psA, psF = psS[:, 0:32], psS[:, 32:64]
    psR, psM = psS[:, 64:96], psS[:, 96:100]
    by_u = lambda ap: ap.rearrange("p (u h) -> p u h", h=H)
    if relational:
        typrow = [s.sb(f"typrow{j}", [NREL, CHUNK], BF16) for j in range(SL)]
        typeT = s.sb("typeT", [NREL, CHUNK])
        modk = s.sb("modk", [P, U, D])
        psRel = s.ps("psRel", [P, 512])
        psQ = [s.ps(f"psQ{i}", [P, 512]) for i in range(2)]

    ready = s.sem("ready")
    gathered = [[nc.alloc_semaphore(f"{tag}_gathered{j}_{u}") for u in range(U)] for j in range(SL)]
    dstrow_in = [s.sem(f"dstrow_in{j}") for j in range(SL)]
    firstrow_in = [s.sem(f"firstrow_in{j}") for j in range(SL)]
    window_in = [s.sem(f"window_in{j}") for j in range(SL)]
    out_stored = [s.sem(f"out_stored{j}") for j in range(SL)]
    names = ["idx_ready", "adst_done", "summed", "score_ready", "scoreT_done", "scan_done", "scanback_done",
             "lastmax_ready", "nodemax_done", "nodemax_ready", "refmax_done", "expin_ready", "prob_ready",
             "weighted", "aggregated", "shift_ready", "carry_done", "gdiff_ready", "gin_ready", "rescale_ready",
             "onehot_ready", "onehotT_ready", "carried_ready", "out_ready"]
    if relational:
        names += ["typeT_ready", "rel_done", "modk_ready", "product_ready"]
        typrow_in = [s.sem(f"typrow_in{j}") for j in range(SL)]
        q_done, q_used = s.sem("q_done"), s.sem("q_used")
        NQ = U // 2
    q = {n: s.sem(n) for n in names}
    buffers_zero, all_stored = s.sem("buffers_zero"), s.sem("all_stored")
    store_due = s.sem("store_due")
    NQ = U // 2
    at = lambda k: k + SL
    late = ("weighted", "aggregated", "carry_done", "gdiff_ready", "gin_ready", "rescale_ready", "carried_ready",
            "out_ready")

    def passes(eng, body):
        nit = eng.value_load(r["nits_i"][0:1, 0:1], min_val=1, max_val=NIT)
        with eng.Fori(0, NIT) as i:
            with eng.If(i < nit):
                for j in range(SL):
                    body(i, SL * i + j + 1, (j + 1) % SL, j)
        return nit

    loaded = lambda i, j: 16 * (i + 1 + j // SL)
    rowi = lambda k: bass.ds(k, 1)

    with nc.Block() as block:
        @block.gpsimd
        def _(pool):
            for n, x in q.items():
                if n != "idx_ready":
                    pool.sem_inc(x, SL - 1 if n in late else SL)
            if relational:
                pool.sem_inc(q_used, SL * NQ)
                pool.sem_inc(q_done, SL * NQ)
            pool.sem_inc(ready, 1)

            def body(i, k, sl, j):
                pool.wait_ge(ready, 1)
                pool.wait_ge(q["weighted"], at(k - SL))
                nc.gpsimd.tensor_copy(idx[sl][:, :], r["src_pass"][:, bass.ds(k, 1), :].rearrange(
                    "p a u -> p (a u)")).then_inc(q["idx_ready"], 1)
                pool.wait_ge(ready, 1)
                pool.wait_ge(q["idx_ready"], at(k - SL))
                for u in range(U):
                    nc.gpsimd.indirect_dma_start(
                        G[sl][:, u, :], None, tab,
                        bass.IndirectOffsetOnAxis(ap=idx[sl][:, u:u + 1], axis=0)).then_inc(gathered[sl][u], 16)
            pool.wait_ge(buffers_zero, 1)
            passes(pool, body)

        @block.sync
        def _(sp):
            prime(sp, outw, out_stored, 16, r)

            def load(k, sl, first=False):
                sp.dma_start(dstrow[sl][:, :], bcast(d["dstrow"][rowi(k), :], [P, CHUNK])).then_inc(dstrow_in[sl], 16)
                sp.dma_start(firstrow[sl][:, :], bcast(d["firstrow"][rowi(k), :], [H, CHUNK])).then_inc(
                    firstrow_in[sl], 16)
                n0 = 0 if first else sp.value_load(r["n0_i"][0:1, bass.ds(k + 2, 1)], min_val=0, max_val=N)
                rows = wtab[0:P, :] if first else wtab[bass.ds(n0, P), :]
                sp.dma_start(window[sl][:, :], rows[:, wcols[0]:wcols[1]]).then_inc(window_in[sl], 16)
                if relational:
                    sp.dma_start(typrow[sl][:, :], bcast(d["typrow"][rowi(k), :], [NREL, CHUNK])).then_inc(
                        typrow_in[sl], 16)

            def store(k, sl, before):
                n0 = sp.value_load(r["n0_i"][0:1, bass.ds(k + 2, 1)], min_val=0, max_val=N)
                sp.wait_ge(out_stored[(sl - 1) % SL], before)
                sp.sem_inc(store_due, 1)
                sp.wait_ge(q["out_ready"], at(k))
                sp.sem_inc(store_due, 1)
                sp.dma_start(d["agg"][bass.ds(n0, P), :], outw[sl][:, :]).then_inc(out_stored[sl], 16)

            load(1, 1, first=True)
            sp.wait_ge(ready, 1)
            sp.wait_ge(buffers_zero, 1)

            def body(i, k, sl, j):
                if relational:
                    sp.wait_ge(q_done, NQ * at(k - 2))
                sp.wait_ge(q["onehotT_ready"], at(k - 2))
                sp.wait_ge(q["scan_done"], at(k - 2))
                sp.wait_ge(q["refmax_done"], at(k - 2))
                if not relational:
                    sp.wait_ge(q["adst_done"], at(k - 2))
                else:
                    sp.wait_ge(q["typeT_ready"], at(k - 2))
                load(k + 1, (sl + 1) % SL)
                store(k - 3, sl, 16 * (i + (2 if j else 1)))
            nit = passes(sp, body)
            sp.wait_ge(ready, 1)
            for back in (2, 1):
                k, sl = nit * SL - back, (SL - back) % SL
                store(k, sl, 16 * (nit + (1 if back == 2 else 2)))
            seen, seen2 = sp.snap(16 * (nit + 1)), sp.snap(16 * (nit + 2))
            sp.wait_ge(ready, 1)
            for j in range(SL):
                sp.wait_ge(out_stored[j], seen2 if j else seen)
            for x in [dstrow_in, firstrow_in, window_in] + ([typrow_in] if relational else []):
                sp.wait_ge(x[1], seen)
            sp.sem_inc(all_stored, 1)

        @block.vector
        def _(dve):
            v = nc.vector

            def build_onehot(k, sl):
                loc = r["dstloc"][:, rowi(k), :].rearrange("p a u -> p (a u)").unsqueeze(2)
                v.tensor_tensor(onehot[sl][:, :, :], bcast(loc, [P, U, P]),
                                bcast(r["iota_row"][:, :].unsqueeze(1), [P, U, P]), ALU.is_equal).then_inc(
                                    q["onehot_ready"], 1)

            def build_onehotT(sl):
                v.tensor_scalar(onehotT[sl][:, :], dstrow[sl][:, :], r["iota_col"][:, 0:1], None,
                                ALU.is_equal).then_inc(q["onehotT_ready"], 1)

            for j in range(SL):
                dve.wait_ge(out_stored[j], 16)
                v.memset(outw[j][:, :], 0.0)
            v.memset(G[0][:, :, :], 0.0)
            v.memset(ph[0][:, :, :], 0.0)
            v.memset(onehot[0][:, :, :], 0.0)
            v.memset(scanned[0][:, :], 0.0)
            v.memset(shift[:, :], 0.0).then_inc(buffers_zero, 1)
            dve.wait_ge(ready, 1)
            dve.wait_ge(buffers_zero, 1)
            build_onehot(1, 1)
            dve.wait_ge(dstrow_in[1], 16)
            build_onehotT(1)

            def body(i, k, sl, j):
                pv, nx = (sl - 1) % SL, (sl + 1) % SL
                if relational:
                    dve.wait_ge(q["rel_done"], at(k - 1))
                    dve.wait_ge(typrow_in[sl], loaded(i, j))
                    v.tensor_scalar(typeT[:, :], typrow[sl][:, :], r["iota_col"][0:NREL, 0:1], None,
                                    ALU.is_equal).then_inc(q["typeT_ready"], 1)
                    for u in range(U):
                        dve.wait_ge(gathered[sl][u], 16 * (i + 1))
                    dve.wait_ge(q["score_ready"], at(k - 1))
                    dve.wait_ge(q["rel_done"], at(k))
                    v.tensor_tensor(modk[:, :, :].rearrange("p u (h c) -> p u h c", c=C),
                                    G[sl][:, :, 0:D].rearrange("p u (h c) -> p u h c", c=C),
                                    bcast(psRel[:, :].rearrange("p (u c) -> p u c", c=C).unsqueeze(2), [P, U, H, C]),
                                    ALU.add).then_inc(q["modk_ready"], 1)
                    dve.wait_ge(q["modk_ready"], at(k))
                    for n in range(NQ):
                        dve.wait_ge(q_done, NQ * at(k - 1) + n + 1)
                        m = modk[:, 2 * n:2 * n + 2, :].rearrange("p u n -> p (u n)")
                        v.tensor_tensor(m, m, psQ[n % 2][:, :], ALU.mult).then_inc(q_used, 1)
                    dve.wait_ge(q_used, NQ * at(k))
                    dve.wait_ge(q["expin_ready"], at(k - 1))
                    dve.wait_ge(q["scoreT_done"], at(k - 1))
                    v.reduce_sum(score[:, :, :].rearrange("p u h -> p (u h)"),
                                 modk[:, :, :].rearrange("p u (h c) -> p (u h) c", c=C), axis=AXX).then_inc(
                                     q["score_ready"], 1)
                else:
                    for u in range(U):
                        dve.wait_ge(gathered[sl][u], 16 * (i + 1))
                    dve.wait_ge(q["score_ready"], at(k - 1))
                    dve.wait_ge(q["adst_done"], at(k))
                    v.tensor_tensor(ssum[:, :, :], G[sl][:, :, D:D + H], by_u(psA), ALU.add).then_inc(q["summed"], 1)
                    dve.wait_ge(q["summed"], at(k))
                    dve.wait_ge(q["expin_ready"], at(k - 1))
                    dve.wait_ge(q["scoreT_done"], at(k - 1))
                    v.scalar_tensor_tensor(score[:, :, :], ssum[:, :, :], 0.2, ssum[:, :, :], ALU.mult,
                                           ALU.max).then_inc(q["score_ready"], 1)
                dve.wait_ge(q["aggregated"], at(k - 3))
                dve.wait_ge(q["prob_ready"], at(k - 1))
                v.tensor_tensor(ph[pv][:, :, 0:D].rearrange("p u (h c) -> p u h c", c=C),
                                G[pv][:, :, V0:V0 + D].rearrange("p u (h c) -> p u h c", c=C),
                                bcast(ph[pv][:, :, D:D + H].unsqueeze(3), [P, U, H, C]), ALU.mult).then_inc(
                                    q["weighted"], 1)
                dve.wait_ge(firstrow_in[sl], loaded(i, j))
                dve.wait_ge(q["scan_done"], at(k - 1))
                dve.wait_ge(q["scanback_done"], at(k - 3))
                dve.wait_ge(q["scoreT_done"], at(k))
                v.tensor_tensor_scan(scanned[sl][:, :], firstrow[sl][:, :], psT[:, :],
                                     scanned[pv][:, CHUNK - 1:CHUNK], ALU.add, ALU.max).then_inc(q["scan_done"], 1)
                dve.wait_ge(q["aggregated"], at(k - 2))
                build_onehot(k + 1, nx)
                dve.wait_ge(q["nodemax_done"], at(k - 1))
                dve.wait_ge(q["scanback_done"], at(k))
                v.tensor_tensor(lastmax[:, :, :], by_u(psF),
                                bcast(r["islast"][:, rowi(k), :].rearrange("p a u -> p (a u)").unsqueeze(2), [P, U, H]),
                                ALU.mult).then_inc(q["lastmax_ready"], 1)
                dve.wait_ge(q["refmax_done"], at(k - 2))
                dve.wait_ge(dstrow_in[nx], loaded(i, j + 1))
                build_onehotT(nx)
                dve.wait_ge(out_stored[sl], 16 * (i + 2))
                dve.wait_ge(q["carry_done"], at(k - 2))
                dve.wait_ge(q["nodemax_done"], at(k))
                v.tensor_copy(outw[sl][:, D + H:AW], psM).then_inc(q["nodemax_ready"], 1)
                dve.wait_ge(q["rescale_ready"], at(k - 2))
                dve.wait_ge(q["carry_done"], at(k - 1))
                v.tensor_tensor(gin[:, :], psC[:, D + H:AW], outw[pv][:, D + H:AW], ALU.subtract).then_inc(
                    q["gdiff_ready"], 1)
                dve.wait_ge(q["gdiff_ready"], at(k - 1))
                v.tensor_scalar(gin[:, :], gin[:, :], 0.0, None, ALU.min).then_inc(q["gin_ready"], 1)
                dve.wait_ge(q["shift_ready"], at(k - 1))
                v.tensor_scalar(shift[:, 0:1], r["iota_col"][:, 0:1], r["delta"][:, rowi(k)], None,
                                ALU.is_equal).then_inc(q["shift_ready"], 1)
                dve.wait_ge(q["prob_ready"], at(k - 1))
                dve.wait_ge(q["refmax_done"], at(k))
                v.tensor_tensor(expin[:, :, :], score[:, :, :], by_u(psR), ALU.subtract).then_inc(q["expin_ready"], 1)
                dve.wait_ge(q["rescale_ready"], at(k - 1))
                v.tensor_tensor(carried[:, 0:D].rearrange("p (h c) -> p h c", c=C),
                                psC[:, 0:D].rearrange("p (h c) -> p h c", c=C),
                                bcast(gex[:, :].unsqueeze(2), [P, H, C]), ALU.mult)
                v.tensor_tensor(carried[:, D:D + H], psC[:, D:D + H], gex[:, :], ALU.mult).then_inc(q["carried_ready"], 1)
                dve.wait_ge(q["carried_ready"], at(k - 1))
                dve.wait_ge(q["aggregated"], at(k - 1))
                v.tensor_tensor(outw[pv][:, 0:D + H], carried[:, :], psO[:, 0:D + H], ALU.add).then_inc(q["out_ready"], 1)
            passes(dve, body)

        @block.scalar
        def _(act):
            act.wait_ge(ready, 1)
            act.wait_ge(buffers_zero, 1)

            def body(i, k, sl, j):
                act.wait_ge(q["carried_ready"], at(k - 2))
                act.wait_ge(q["gin_ready"], at(k - 1))
                nc.scalar.activation(gex[:, :], gin[:, :], ACT.Exp).then_inc(q["rescale_ready"], 1)
                act.wait_ge(q["aggregated"], at(k - 3))
                act.wait_ge(q["expin_ready"], at(k))
                nc.scalar.activation(ph[sl][:, :, D:D + H], expin[:, :, :], ACT.Exp).then_inc(q["prob_ready"], 1)
            passes(act, body)

        @block.tensor
        def _(pe):
            t = nc.tensor
            pe.wait_ge(ready, 1)
            pe.wait_ge(buffers_zero, 1)
            cut = lambda u: slice(u * P, (u + 1) * P)

            def body(i, k, sl, j):
                pv, p2 = (sl - 1) % SL, (sl - 2) % SL
                pe.wait_ge(q["shift_ready"], at(k - 1))
                pe.wait_ge(q["out_ready"], at(k - 2))
                t.matmul(psC[:, 0:AW], shift[:, :], outw[p2][:, :], start=True, stop=True).then_inc(q["carry_done"], 1)
                if relational:
                    pe.wait_ge(q["modk_ready"], at(k - 1))
                    pe.wait_ge(q["typeT_ready"], at(k))
                    for u in range(U):
                        ins = t.matmul(psRel[:, u * C:(u + 1) * C], typeT[:, cut(u)], r["relw"][:, :], start=True, stop=True)
                    ins.then_inc(q["rel_done"], 1)
                    pe.wait_ge(q["onehotT_ready"], at(k))
                    pe.wait_ge(window_in[sl], loaded(i, j))
                    for n in range(NQ):
                        pe.wait_ge(q_used, NQ * at(k - 1) + n - 1)
                        for e in range(2):
                            ins = t.matmul(psQ[n % 2][:, e * D:(e + 1) * D], onehotT[sl][:, cut(2 * n + e)],
                                           window[sl][:, :], start=True, stop=True)
                        ins.then_inc(q_done, 1)
                else:
                    pe.wait_ge(q["onehotT_ready"], at(k))
                    pe.wait_ge(window_in[sl], loaded(i, j))
                    pe.wait_ge(q["summed"], at(k - 1))
                    for u in range(U):
                        ins = t.matmul(psA[:, u * H:(u + 1) * H], onehotT[sl][:, cut(u)], window[sl][:, :],
                                       start=True, stop=True)
                    ins.then_inc(q["adst_done"], 1)
                pe.wait_ge(ready, 1)
                pe.wait_ge(q["scan_done"], at(k - 1))
                pe.wait_ge(q["score_ready"], at(k))
                for u in range(U):
                    ins = t.transpose(psT[:, cut(u)], score[:, u, :], r["ident"][:, :])
                ins.then_inc(q["scoreT_done"], 1)
                pe.wait_ge(q["weighted"], at(k - 1))
                for u in range(U):
                    ins = t.matmul(psO[:, 0:D + H], onehot[pv][:, u, :], ph[pv][:, u, :], start=(u == 0), stop=(u == U - 1))
                ins.then_inc(q["aggregated"], 1)
                pe.wait_ge(ready, 1)
                pe.wait_ge(q["lastmax_ready"], at(k - 1))
                pe.wait_ge(q["scan_done"], at(k))
                for u in range(U):
                    ins = t.transpose(psF[:, u * H:(u + 1) * H], scanned[sl][:, cut(u)], r["ident"][0:H, 0:H])
                ins.then_inc(q["scanback_done"], 1)
                pe.wait_ge(q["nodemax_ready"], at(k - 1))
                pe.wait_ge(q["onehot_ready"], at(k))
                pe.wait_ge(q["lastmax_ready"], at(k))
                for u in range(U):
                    ins = t.matmul(psM, onehot[sl][:, u, :], lastmax[:, u, :], start=(u == 0), stop=(u == U - 1))
                ins.then_inc(q["nodemax_done"], 1)
                pe.wait_ge(q["expin_ready"], at(k - 1))
                pe.wait_ge(q["nodemax_ready"], at(k))
                for u in range(U):
                    ins = t.matmul(psR[:, u * H:(u + 1) * H], onehotT[sl][:, cut(u)], outw[sl][:, D + H:AW],
                                   start=True, stop=True)
                ins.then_inc(q["refmax_done"], 1)
            passes(pe, body)
    s.close()


def edgeconv_stage(nc, d, r, tag):
    s = Stage(nc, tag)
    NG, NB = 4, U // 2
    idx = [s.sb(f"idx{j}", [P, U], I32) for j in range(SL)]
    G = [s.sb(f"G{j}", [P, U, D]) for j in range(SL)]
    firstrow = [s.sb(f"firstrow{j}", [P, CHUNK], BF16) for j in range(SL)]
    onehot = [s.sb(f"onehot{j}", [P, U, P]) for j in range(SL)]
    scanned = [[s.sb(f"scanned{j}_{h}", [P, CHUNK]) for h in range(2)] for j in range(SL)]
    back = [s.sb(f"back{j}", [P, U, XW]) for j in range(SL)]
    outw = [s.sb(f"outw{j}", [P, XW]) for j in range(SL)]
    psT = [s.ps(f"psT{i}", [P, 512]) for i in range(4)]
    psB = [s.ps(f"psB{i}", [P, 512]) for i in range(3)]
    psO = s.ps("psO", [P, 512])
    ready = s.sem("ready")
    gathered = [[nc.alloc_semaphore(f"{tag}_gathered{j}_{u}") for u in range(U)] for j in range(SL)]
    firstrow_in = [s.sem(f"firstrow_in{j}") for j in range(SL)]
    out_stored = [s.sem(f"out_stored{j}") for j in range(SL)]
    idx_ready, onehot_ready, selected, out_ready = (s.sem(n) for n in (
        "idx_ready", "onehot_ready", "selected", "out_ready"))
    turned, scan_done, back_done, back_ready = (s.sem(n) for n in ("turned", "scan_done", "back_done", "back_ready"))
    buffers_zero, all_stored = s.sem("buffers_zero"), s.sem("all_stored")
    store_due = s.sem("store_due")
    at = lambda k: k + SL
    at4 = lambda k: NG * (k + SL)
    rowi = lambda k: bass.ds(k, 1)
    loaded = lambda i, j: 16 * (i + 1 + j // SL)

    def passes(eng, body):
        nit = eng.value_load(r["nits_i"][0:1, 0:1], min_val=1, max_val=NIT)
        with eng.Fori(0, NIT) as i:
            with eng.If(i < nit):
                for j in range(SL):
                    body(i, SL * i + j + 1, (j + 1) % SL, j)
        return nit

    with nc.Block() as block:
        @block.gpsimd
        def _(pool):
            for x in (onehot_ready, selected, out_ready):
                pool.sem_inc(x, SL)
            for x in (turned, scan_done, back_done, back_ready):
                pool.sem_inc(x, NG * SL)
            pool.sem_inc(ready, 1)

            def body(i, k, sl, j):
                pool.wait_ge(ready, 1)
                mine = pool.snap(at(k - SL))
                pool.wait_ge(turned, at4(k - SL))
                nc.gpsimd.tensor_copy(idx[sl][:, :], r["src_pass"][:, rowi(k), :].rearrange(
                    "p a u -> p (a u)")).then_inc(idx_ready, 1)
                pool.wait_ge(ready, 1)
                pool.wait_ge(idx_ready, mine)
                for u in range(U):
                    nc.gpsimd.indirect_dma_start(
                        G[sl][:, u, :], None, d["bx"],
                        bass.IndirectOffsetOnAxis(ap=idx[sl][:, u:u + 1], axis=0)).then_inc(gathered[sl][u], 16)
            passes(pool, body)

        @block.sync
        def _(sp):
            prime(sp, outw, out_stored, 16, r)

            def load(k, sl):
                sp.dma_start(firstrow[sl][:, :], bcast(d["firstrow"][rowi(k), :], [P, CHUNK])).then_inc(firstrow_in[sl], 16)

            load(1, 1)
            sp.wait_ge(ready, 1)

            def body(i, k, sl, j):
                sp.wait_ge(scan_done, at4(k - 2))
                load(k + 1, (sl + 1) % SL)
                n0 = sp.value_load(r["n0_i"][0:1, bass.ds(k + 2, 1)], min_val=0, max_val=N)
                before = 16 * (i + (2 if j else 1))
                sp.wait_ge(out_stored[(sl - 1) % SL], before)
                sp.sem_inc(store_due, 1)
                sp.wait_ge(out_ready, at(k))
                sp.sem_inc(store_due, 1)
                sp.dma_start(d["aggx"][bass.ds(n0, P), :], outw[sl][:, :]).then_inc(out_stored[sl], 16)
            nit = passes(sp, body)
            seen = sp.snap(16 * (nit + 1))
            sp.wait_ge(ready, 1)
            for j in range(SL):
                sp.wait_ge(out_stored[j], seen)
            sp.wait_ge(firstrow_in[1], seen)
            sp.sem_inc(all_stored, 1)

        @block.vector
        def _(dve):
            v = nc.vector
            for j in range(SL):
                v.memset(back[j][:, :, D:XW], 1.0)
            for h in range(2):
                v.memset(scanned[0][h][:, :], 0.0).then_inc(buffers_zero, 1)
            dve.wait_ge(ready, 1)
            dve.wait_ge(buffers_zero, 2)

            def body(i, k, sl, j):
                pv = (sl - 1) % SL
                dve.wait_ge(selected, at(k - SL))
                loc = r["lastloc"][:, rowi(k), :].rearrange("p a u -> p (a u)").unsqueeze(2)
                v.tensor_tensor(onehot[sl][:, :, :], bcast(loc, [P, U, P]),
                                bcast(r["iota_row"][:, :].unsqueeze(1), [P, U, P]), ALU.is_equal).then_inc(onehot_ready, 1)
                dve.wait_ge(firstrow_in[sl], loaded(i, j))
                dve.wait_ge(back_done, at4(k - SL))
                for n in range(NG):
                    a, h = n // 2, n % 2
                    cols = slice(a * 512, (a + 1) * 512)
                    start = scanned[sl][h][:, 511:512] if a else scanned[pv][h][:, CHUNK - 1:CHUNK]
                    dve.wait_ge(scan_done, at4(k - 1) + n - 1)
                    dve.wait_ge(turned, at4(k - 1) + n + 1)
                    v.tensor_tensor_scan(scanned[sl][h][:, cols], firstrow[sl][:, cols], psT[n][:, :], start,
                                         ALU.add, ALU.max).then_inc(scan_done, 1)
            passes(dve, body)

        @block.scalar
        def _(act):
            for j in range(SL):
                act.wait_ge(out_stored[j], 16)
            act.wait_ge(ready, 1)

            def body(i, k, sl, j):
                act.wait_ge(selected, at(k - SL))
                for n in range(NB):
                    act.wait_ge(back_done, at4(k - 1) + n + 1)
                    nc.scalar.copy(back[sl][:, 2 * n:2 * n + 2, 0:D],
                                   psB[(NB * j + n) % 3][:, :].rearrange("p (u n) -> p u n", u=2)).then_inc(back_ready, 1)
                act.wait_ge(out_stored[sl], 16 * (i + 1))
                act.wait_ge(selected, at(k))
                nc.scalar.copy(outw[sl][:, :], psO[:, 0:XW]).then_inc(out_ready, 1)
            passes(act, body)

        @block.tensor
        def _(pe):
            t = nc.tensor
            pe.wait_ge(ready, 1)
            pe.wait_ge(buffers_zero, 2)

            def body(i, k, sl, j):
                for u in range(U):
                    pe.wait_ge(gathered[sl][u], 16 * (i + 1))
                for n in range(NG):
                    a, h = n // 2, n % 2
                    pe.wait_ge(ready, 1)
                    pe.wait_ge(scan_done, at4(k - 1) + n + 1 - NG)
                    for u in range(4):
                        ins = t.transpose(psT[n][:, u * P:(u + 1) * P], G[sl][:, 4 * a + u, h * P:(h + 1) * P],
                                          r["ident"][:, :])
                    ins.then_inc(turned, 1)
                for n in range(NB):
                    pe.wait_ge(ready, 1)
                    pe.wait_ge(back_ready, at4(k - 1) + n + 1 - 3)
                    pe.wait_ge(scan_done, at4(k - 1) + 2 * (n // 2) + 2)
                    for u in (2 * n, 2 * n + 1):
                        for h in range(2):
                            ins = t.transpose(psB[(NB * j + n) % 3][:, (u - 2 * n) * D + h * P:(u - 2 * n) * D + (h + 1) * P],
                                              scanned[sl][h][:, u * P:(u + 1) * P], r["ident"][:, :])
                    ins.then_inc(back_done, 1)
                pe.wait_ge(out_ready, at(k - 1))
                pe.wait_ge(onehot_ready, at(k))
                pe.wait_ge(back_ready, at4(k))
                for u in range(U):
                    ins = t.matmul(psO[:, 0:XW], onehot[sl][:, u, :], back[sl][:, u, :], start=(u == 0), stop=(u == U - 1))
                ins.then_inc(selected, 1)
            passes(pe, body)
    s.close()


def coefficient_stage(nc, d, r, tag, kind, ca, cs):
    s = Stage(nc, tag)
    T4 = [P, TILES, H]
    aux = s.sb("aux", [P, TILES, 2 * H])
    own = s.sb("own", [P, TILES, 2 * H])
    tmp = [s.sb(f"tmp{i}", T4) for i in range(4)]
    loaded, dve_step, ex_in, ex_out = s.sem("loaded"), s.sem("dve_step"), s.sem("ex_in"), s.sem("ex_out")
    tiles = lambda dram: dram.rearrange("(t p) w -> p t w", p=P)
    with nc.Block() as block:
        @block.sync
        def _(sp):
            sp.dma_start(aux[:, :, :], tiles(d["agg"])[:, :, D:AW]).then_inc(loaded, 16)
            if kind != "relational":
                sp.dma_start(own[:, :, :], tiles(d["h"])[:, :, D:GW]).then_inc(loaded, 16)

        @block.scalar
        def _(act):
            if kind != "relational":
                act.wait_ge(ex_in, 2)
                nc.scalar.activation(tmp[0][:, :, :], tmp[0][:, :, :], ACT.Exp)
                nc.scalar.activation(tmp[1][:, :, :], tmp[1][:, :, :], ACT.Exp).then_inc(ex_out, 1)

        @block.vector
        def _(dve):
            v, c = nc.vector, Chain(dve, dve_step)
            den, mx = aux[:, :, 0:H], aux[:, :, H:2 * H]
            ea, es, empty, x = (t[:, :, :] for t in tmp)
            dve.wait_ge(loaded, 16 if kind == "relational" else 32)
            c.do(v.tensor_scalar(empty, den, 0.0, None, ALU.is_equal))
            if kind == "relational":
                c.do(v.tensor_tensor(den, den, empty, ALU.add))
                c.do(v.reciprocal(ca[:, :, :], den))
                c.do(v.tensor_copy(cs[:, :, :], empty))
                return
            c.do(v.tensor_tensor(x, own[:, :, 0:H], own[:, :, H:2 * H], ALU.add))
            c.do(v.scalar_tensor_tensor(es, x, 0.2, x, ALU.mult, ALU.max))
            c.do(v.scalar_tensor_tensor(ea, empty, -BIG, mx, ALU.mult, ALU.add))
            c.do(v.tensor_tensor(x, ea, es, ALU.max))
            v.tensor_tensor(ea, ea, x, ALU.subtract).then_inc(ex_in, 1)
            v.tensor_tensor(es, es, x, ALU.subtract).then_inc(ex_in, 1)
            dve.wait_ge(ex_out, 1)
            c.do(v.tensor_tensor(x, den, ea, ALU.mult))
            c.do(v.tensor_tensor(x, x, es, ALU.add))
            if kind == "relu":
                c.do(v.tensor_scalar(x, x, 1e-16, None, ALU.add))
            c.do(v.reciprocal(x, x))
            c.do(v.tensor_tensor(ca[:, :, :], ea, x, ALU.mult))
            c.do(v.tensor_tensor(cs[:, :, :], es, x, ALU.mult))
    s.close()


def stats_stage(nc, r, tag, mv):
    s = Stage(nc, tag)
    dve_step, var_ready, root_ready = s.sem("dve_step"), s.sem("var_ready"), s.sem("root_ready")
    with nc.Block() as block:
        @block.vector
        def _(dve):
            v, c = nc.vector, Chain(dve, dve_step)
            c.do(v.tensor_copy(r["mean"][:, :], mv[:, :, 0]))
            v.tensor_scalar(r["rstd"][:, :], mv[:, :, 1], EPS, None, ALU.add).then_inc(var_ready, 1)
            dve.wait_ge(root_ready, 1)
            c.do(v.reciprocal(r["rstd"][:, :], r["rstd"][:, :]))

        @block.scalar
        def _(act):
            act.wait_ge(var_ready, 1)
            nc.scalar.activation(r["rstd"][:, :], r["rstd"][:, :], ACT.Sqrt).then_inc(root_ready, 1)
    s.close()


def combine_stage(nc, d, r, y, tag, kind, ca, cs, mv, bias):
    s = Stage(nc, tag)
    B = 5
    IT = TILES // B
    att = kind != "conv"
    dram_a, wa = (d["agg"], D) if att else (d["aggx"], XW)
    dram_h = {"relu": d["h"][:, 0:D], "elu": d["h"][:, 0:D], "relational": d["kv"][:, D:2 * D], "conv": d["ax"]}[kind]
    acc = [s.sb(f"acc{b}", [P, wa]) for b in range(B)]
    hv = [s.sb(f"hv{b}", [P, D]) for b in range(B)]
    xt = [s.sb(f"xt{b}", [P, D]) for b in range(B)]
    hs = [s.sb(f"hs{b}", [P, D]) for b in range(B)]
    ta = [s.sb(f"ta{b}", [P, D]) for b in range(B)]
    tb = [s.sb(f"tb{b}", [P, D]) for b in range(B)]
    st = [s.sb(f"st{b}", [P, 6]) for b in range(B)]
    mvt = [s.sb(f"mvt{b}", [P, 2]) for b in range(B)]
    psT = [s.ps(f"psT{b}", [P, 512]) for b in range(2)]
    psW = [s.ps(f"psW{b}", [P, 512]) for b in range(2)]
    loaded = [s.sem(f"loaded{b}") for b in range(B)]
    ready = s.sem("ready")
    names = ["own_ready", "scaled", "summed", "biased", "exp_ready", "turned", "xT_ready", "product_done", "half_done",
             "y_ready", "stats_ready", "scaled_b", "aggr_ready", "tile_done"]
    q = {n: s.sem(n) for n in names}
    at = lambda t: t + 1 + B
    heads = lambda ap: ap.rearrange("p (h c) -> p h c", c=C)
    coef = lambda c, t: bcast(c[:, bass.ds(t, 1), :].rearrange("p a h -> p (a h)").unsqueeze(2), [P, H, C])
    with nc.Block() as block:
        @block.sync
        def _(sp):
            sp.wait_ge(ready, 1)
            with sp.Fori(0, IT) as i:
                for b in range(B):
                    t = i * B + b
                    sp.wait_ge(q["tile_done"], at(t - B))
                    rows = bass.ds(t * P, P)
                    sp.dma_start(acc[b][:, :], dram_a[rows, 0:wa]).then_inc(loaded[b], 16)
                    sp.dma_start(hv[b][:, :], dram_h[rows, :]).then_inc(loaded[b], 16)
                    sp.dma_start(xt[b][:, :], d["x"][rows, :]).then_inc(loaded[b], 16)

        @block.gpsimd
        def _(pool):
            for x in q.values():
                pool.sem_inc(x, B)
            pool.sem_inc(ready, 1)
            with pool.Fori(0, IT) as i:
                for b in range(B):
                    t = i * B + b
                    pool.wait_ge(ready, 1)
                    pool.wait_ge(q["tile_done"], at(t - B))
                    pool.wait_ge(loaded[b], 48 * (i + 1))
                    g = nc.gpsimd
                    if att:
                        ins = g.tensor_tensor(heads(hs[b][:, :]), heads(hv[b][:, :]), coef(cs, t), ALU.mult)
                        if kind == "relational":
                            ins = g.tensor_tensor(xt[b][:, :], xt[b][:, :], bias, ALU.add)
                    else:
                        ins = g.tensor_tensor(hs[b][:, :], hv[b][:, :], acc[b][:, 0:D], ALU.add)
                    ins.then_inc(q["own_ready"], 1)

        @block.vector
        def _(dve):
            v = nc.vector
            dve.wait_ge(ready, 1)

            def first(i, b, t):
                if not att:
                    dve.wait_ge(q["own_ready"], at(t))
                    v.tensor_scalar(ta[b][:, :], hs[b][:, :], 0.0, acc[b][:, D:XW], ALU.max, ALU.mult).then_inc(q["biased"], 1)
                    return
                dve.wait_ge(q["tile_done"], at(t - B))
                dve.wait_ge(loaded[b], 48 * (i + 1))
                v.tensor_tensor(heads(ta[b][:, :]), heads(acc[b][:, :]), coef(ca, t), ALU.mult).then_inc(q["scaled"], 1)
                dve.wait_ge(q["own_ready"], at(t))
                dve.wait_ge(q["scaled"], at(t))
                v.tensor_tensor(ta[b][:, :], ta[b][:, :], hs[b][:, :], ALU.add).then_inc(q["summed"], 1)
                if kind == "relational":
                    return
                dve.wait_ge(q["summed"], at(t))
                v.tensor_tensor(ta[b][:, :], ta[b][:, :], bias, ALU.add).then_inc(q["biased"], 1)
                if kind == "elu":
                    dve.wait_ge(q["biased"], at(t))
                    v.tensor_scalar(tb[b][:, :], ta[b][:, :], 0.0, None, ALU.min).then_inc(q["half_done"], 1)

            def second(i, b, t):
                yt = y[:, bass.ds(t * D, D)]
                if kind == "relu":
                    dve.wait_ge(q["biased"], at(t))
                    v.scalar_tensor_tensor(yt, ta[b][:, :], 0.0, xt[b][:, :], ALU.max, ALU.add).then_inc(q["y_ready"], 1)
                elif kind == "elu":
                    dve.wait_ge(q["exp_ready"], at(t))
                    v.scalar_tensor_tensor(ta[b][:, :], ta[b][:, :], 0.0, tb[b][:, :], ALU.max, ALU.add).then_inc(q["scaled_b"], 1)
                    dve.wait_ge(q["scaled_b"], at(t))
                    v.scalar_tensor_tensor(yt, ta[b][:, :], -1.0, xt[b][:, :], ALU.add, ALU.add).then_inc(q["y_ready"], 1)
                elif kind == "relational":
                    dve.wait_ge(q["product_done"], at(t))
                    v.tensor_tensor(yt, psW[0 if b % 2 == 0 else 1][:, 0:D], xt[b][:, :], ALU.add).then_inc(q["y_ready"], 1)
                else:
                    dve.wait_ge(q["biased"], at(t))
                    v.tensor_tensor(yt, ta[b][:, :], xt[b][:, :], ALU.add).then_inc(q["y_ready"], 1)
                dve.wait_ge(ready, 1)
                dve.wait_ge(q["y_ready"], at(t))
                v.bn_stats(st[b][:, :], yt).then_inc(q["stats_ready"], 1)
                dve.wait_ge(ready, 1)
                dve.wait_ge(q["stats_ready"], at(t))
                v.bn_aggr(mvt[b][:, :], st[b][:, :]).then_inc(q["aggr_ready"], 1)
                dve.wait_ge(q["aggr_ready"], at(t))
                v.tensor_scalar(mv[:, bass.ds(t, 1), :].rearrange("p a w -> p (a w)"), mvt[b][:, :], 1.0, None,
                                ALU.mult).then_inc(q["tile_done"], 1)

            with dve.Fori(0, IT) as i:
                first(i, 0, i * B)
                for b in range(1, B):
                    first(i, b, i * B + b)
                    second(i, b - 1, i * B + b - 1)
                second(i, B - 1, i * B + B - 1)

        @block.scalar
        def _(act):
            act.wait_ge(ready, 1)
            if kind in ("elu", "relational"):
                with act.Fori(0, IT) as i:
                    for b in range(B):
                        t = i * B + b
                        if kind == "elu":
                            act.wait_ge(q["half_done"], at(t))
                            nc.scalar.activation(tb[b][:, :], tb[b][:, :], ACT.Exp).then_inc(q["exp_ready"], 1)
                        else:
                            act.wait_ge(q["turned"], at(t))
                            nc.scalar.copy(hs[b][:, :], psT[b % 2][:, 0:D]).then_inc(q["xT_ready"], 1)

        @block.tensor
        def _(pe):
            pe.wait_ge(ready, 1)
            if kind == "relational":
                w = r["wo"]
                with pe.Fori(0, IT) as i:
                    for b in range(B):
                        t = i * B + b
                        pe.wait_ge(ready, 1)
                        pe.wait_ge(q["xT_ready"], at(t - 1))
                        pe.wait_ge(q["summed"], at(t))
                        nc.tensor.transpose(psT[b % 2][:, 0:P], ta[b][:, 0:P], r["ident"][:, :])
                        nc.tensor.transpose(psT[b % 2][:, P:D], ta[b][:, P:D], r["ident"][:, :]).then_inc(q["turned"], 1)
                        pe.wait_ge(q["y_ready"], at(t - 1))
                        pe.wait_ge(q["xT_ready"], at(t))
                        nc.tensor.matmul(psW[b % 2][:, 0:D], hs[b][:, 0:P], w[:, 0, :], start=True, stop=False)
                        nc.tensor.matmul(psW[b % 2][:, 0:D], hs[b][:, P:D], w[:, 1, :], start=False,
                                         stop=True).then_inc(q["product_done"], 1)
    s.close()


def affine_stage(nc, d, r, y, tag, mv):
    s = Stage(nc, tag)
    B = 5
    IT = TILES // B
    xt = [s.sb(f"xt{b}", [P, D]) for b in range(B)]
    z = [s.sb(f"z{b}", [P, D]) for b in range(B)]
    st = [s.sb(f"st{b}", [P, 6]) for b in range(B)]
    mvt = [s.sb(f"mvt{b}", [P, 2]) for b in range(B)]
    loaded = [s.sem(f"loaded{b}") for b in range(B)]
    ready = s.sem("ready")
    q = {n: s.sem(n) for n in ("xb_ready", "z_ready", "zg_ready", "y_ready", "stats_ready", "aggr_ready", "tile_done")}
    at = lambda t: t + 1 + B
    with nc.Block() as block:
        @block.sync
        def _(sp):
            sp.wait_ge(ready, 1)
            with sp.Fori(0, IT) as i:
                for b in range(B):
                    t = i * B + b
                    sp.wait_ge(q["tile_done"], at(t - B))
                    sp.dma_start(xt[b][:, :], d["x"][bass.ds(t * P, P), :]).then_inc(loaded[b], 16)

        @block.gpsimd
        def _(pool):
            for x in q.values():
                pool.sem_inc(x, B)
            pool.sem_inc(ready, 1)
            with pool.Fori(0, IT) as i:
                for b in range(B):
                    pool.wait_ge(ready, 1)
                    pool.wait_ge(loaded[b], 16 * (i + 1))
                    nc.gpsimd.tensor_tensor(xt[b][:, :], xt[b][:, :], r["beta"][:, :], ALU.add).then_inc(q["xb_ready"], 1)

        @block.vector
        def _(dve):
            v = nc.vector
            dve.wait_ge(ready, 1)
            with dve.Fori(0, IT) as i:
                for b in range(B):
                    t = i * B + b
                    yt = y[:, bass.ds(t * D, D)]
                    v.tensor_scalar(z[b][:, :], yt, r["mean"][:, bass.ds(t, 1)], r["rstd"][:, bass.ds(t, 1)],
                                    ALU.subtract, ALU.mult).then_inc(q["z_ready"], 1)
                    dve.wait_ge(q["z_ready"], at(t))
                    v.tensor_tensor(z[b][:, :], z[b][:, :], r["gamma"][:, :], ALU.mult).then_inc(q["zg_ready"], 1)
                    dve.wait_ge(q["xb_ready"], at(t))
                    dve.wait_ge(q["zg_ready"], at(t))
                    v.tensor_tensor(yt, z[b][:, :], xt[b][:, :], ALU.add).then_inc(q["y_ready"], 1)
                    dve.wait_ge(ready, 1)
                    dve.wait_ge(q["y_ready"], at(t))
                    v.bn_stats(st[b][:, :], yt).then_inc(q["stats_ready"], 1)
                    dve.wait_ge(ready, 1)
                    dve.wait_ge(q["stats_ready"], at(t))
                    v.bn_aggr(mvt[b][:, :], st[b][:, :]).then_inc(q["aggr_ready"], 1)
                    dve.wait_ge(q["aggr_ready"], at(t))
                    v.tensor_scalar(mv[:, bass.ds(t, 1), :].rearrange("p a w -> p (a w)"), mvt[b][:, :], 1.0, None,
                                    ALU.mult).then_inc(q["tile_done"], 1)
    s.close()


def output_stage(nc, d, r, y, out):
    s = Stage(nc, "output")
    B = 5
    xo = [s.sb(f"xo{b}", [P, D]) for b in range(B)]
    stored = [s.sem(f"stored{b}") for b in range(B)]
    norm_done, ready = s.sem("norm_done"), s.sem("ready")
    at = lambda t: t + 1
    with nc.Block() as block:
        @block.sync
        def _(sp):
            prime(sp, xo, stored, 16, r)
            with sp.Fori(0, TILES // B) as i:
                for b in range(B):
                    t = i * B + b
                    sp.wait_ge(norm_done, at(t))
                    sp.dma_start(out[bass.ds(t * P, P), :], xo[b][:, :]).then_inc(stored[b], 16)
            for b in range(B):
                sp.wait_ge(stored[b], 16 * (1 + TILES // B))

        @block.vector
        def _(dve):
            with dve.Fori(0, TILES // B) as i:
                for b in range(B):
                    t = i * B + b
                    dve.wait_ge(stored[b], 16 * (i + 1))
                    nc.vector.tensor_scalar(xo[b][:, :], y[:, bass.ds(t * D, D)], r["mean"][:, bass.ds(t, 1)],
                                            r["rstd"][:, bass.ds(t, 1)], ALU.subtract, ALU.mult).then_inc(norm_done, 1)
    s.close()


def load_x_stage(nc, r, y):
    s = Stage(nc, "loadx")
    loaded = s.sem("loaded")
    with nc.Block() as block:
        @block.sync
        def _(sp):
            sp.dma_start(y[:, :].rearrange("p (t n) -> p t n", n=D),
                         r["x_dram"].rearrange("(t p) n -> p t n", p=P)).then_inc(loaded, 16)
            sp.wait_ge(loaded, 16)
    s.close()


def graph_layers(nc, d, out):
    dram = lambda name, shape, dt=F32: nc.dram_tensor(name, shape, dt, kind="Internal").ap()
    d["x"] = dram("x_kept", (ROWS, D))
    d["h"] = dram("h_table", (ROWS, GW))
    d["kv"] = dram("kv_table", (ROWS, 2 * D))
    d["q"] = dram("q_table", (ROWS, D))
    d["bx"] = dram("source_table", (ROWS, D))
    d["ax"] = dram("destination_table", (ROWS, D))
    d["agg"] = dram("aggregates", (ROWS, AW))
    d["aggx"] = dram("maxima", (ROWS, XW))
    d["dstrow"] = dram("dstrow", (NK, CHUNK), BF16)
    d["firstrow"] = dram("firstrow", (NK, CHUNK), BF16)
    d["typrow"] = dram("typrow", (NK, CHUNK), BF16)
    ctx = ExitStack()
    with ctx:
        def sb(name, shape, dt=F32):
            return ctx.enter_context(nc.sbuf_tensor(name, shape, dt))
        r = {"x_dram": d["x_in"]}
        for name, shape in (("iota_row", [P, P]), ("iota_col", [P, 1]), ("ident", [P, P]), ("dstloc", [P, NK, U]),
                            ("islast", [P, NK, U]), ("lastloc", [P, NK, U]), ("delta", [P, NK]), ("w0", [P, 2, GW]),
                            ("w2", [P, 2, GW]), ("wkvq", [P, 2, 3 * D]), ("wo", [P, 2, D]), ("w3", [P, 2, 2 * D]),
                            ("relw", [NREL, C]), ("b0", [P, D]), ("b1", [P, 3 * D]), ("b2", [P, D]), ("b3", [P, 2 * D]),
                            ("bo", [P, D]), ("gamma", [P, D]), ("beta", [P, D]), ("zero_b", [P, GW]),
                            ("mean", [P, TILES]), ("rstd", [P, TILES])):
            r[name] = sb(name, shape)
        r["iota_i"] = sb("iota_i", [P, P + NK + 1], I32)
        r["src_pass"] = sb("src_pass", [P, NK, U], I32)
        r["n0_i"] = sb("n0_i", [1, NK + 2], I32)
        r["nits_i"] = sb("nits_i", [1, 1], I32)
        setup_stage(nc, d, r)

        def project(y, layer):
            if layer in (0, 2):
                project_stage(nc, d, r, y, f"project{layer}", r[f"w{layer}"], r["zero_b"][:, :], GW, [(0, GW, d["h"])])
            elif layer == 1:
                project_stage(nc, d, r, y, "project1", r["wkvq"], r["b1"][:, :], 3 * D,
                              [(0, 2 * D, d["kv"]), (2 * D, 3 * D, d["q"])])
            else:
                project_stage(nc, d, r, y, "project3", r["w3"], r["b3"][:, :], 2 * D,
                              [(0, D, d["bx"]), (D, 2 * D, d["ax"])])

        with nc.sbuf_tensor("y_in", [P, TILES * D], F32) as y:
            load_x_stage(nc, r, y)
            project(y, 0)
        for layer, kind in enumerate(("relu", "relational", "elu", "conv")):
            if kind == "conv":
                edgeconv_stage(nc, d, r, "edges3")
            else:
                edge_stage(nc, d, r, f"edges{layer}", kind == "relational")
            with ExitStack() as nodes:
                y = nodes.enter_context(nc.sbuf_tensor(f"y{layer}", [P, TILES * D], F32))
                mv = nodes.enter_context(nc.sbuf_tensor(f"mv{layer}", [P, TILES, 2], F32))
                ca = nodes.enter_context(nc.sbuf_tensor(f"ca{layer}", [P, TILES, H], F32))
                cs = nodes.enter_context(nc.sbuf_tensor(f"cs{layer}", [P, TILES, H], F32))
                if kind != "conv":
                    coefficient_stage(nc, d, r, f"coef{layer}", kind, ca, cs)
                bias = {"relu": r["b0"], "relational": r["bo"], "elu": r["b2"], "conv": r["b0"]}[kind][:, :]
                combine_stage(nc, d, r, y, f"combine{layer}", kind, ca, cs, mv, bias)
                stats_stage(nc, r, f"stats{layer}", mv)
                if kind == "relational":
                    affine_stage(nc, d, r, y, "affine", mv)
                    stats_stage(nc, r, "stats_affine", mv)
                if kind == "conv":
                    output_stage(nc, d, r, y, out)
                else:
                    project(y, layer + 1)


def kernel(**inputs):
    import numpy as np
    import concourse.bacc as bacc
    from concourse.bass_utils import run_bass_kernel_spmd

    arr = {k: np.asarray(v) for k, v in inputs.items()}
    x = np.zeros((ROWS, D), np.float32)
    x[:N] = arr["x"]
    dst = np.full(1 + NCH * CHUNK + 1, PAD_DST, np.int32)
    dst[0] = -1
    dst[1:1 + E] = arr["dst"]
    src = np.zeros(NCH * CHUNK, np.int32)
    src[:E] = arr["src"]
    typ = np.zeros(NCH * CHUNK, np.int32)
    typ[:E] = arr["edge_type_64"]
    feeds = {
        "x_in": x, "dst": dst, "src": src.reshape(NCH, CHUNK), "typ": typ.reshape(NCH, CHUNK),
        "W0": arr["L0_gnn_W"], "as0": arr["L0_gnn_att_src"], "ad0": arr["L0_gnn_att_dst"], "b0": arr["L0_gnn_bias"],
        "W2": arr["L2_gnn_W"], "as2": arr["L2_gnn_att_src"], "ad2": arr["L2_gnn_att_dst"], "b2": arr["L2_gnn_bias"],
        "query": arr["L1_gnn_query_emb"], "Wq": arr["L1_gnn_Wq"], "bq": arr["L1_gnn_bq"], "Wk": arr["L1_gnn_Wk"],
        "bk": arr["L1_gnn_bk"], "Wv": arr["L1_gnn_Wv"], "bv": arr["L1_gnn_bv"], "rel": arr["L1_gnn_rel_w"],
        "Wo": arr["L1_gnn_Wo"], "bo": arr["L1_gnn_bo"], "gamma": arr["L1_gnn_gamma"], "beta": arr["L1_gnn_beta"],
        "thetaT": np.ascontiguousarray(arr["L3_gnn_theta_w"].T), "theta_b": arr["L3_gnn_theta_b"],
        "phiT": np.ascontiguousarray(arr["L3_gnn_phi_w"].T), "phi_b": arr["L3_gnn_phi_b"],
    }
    nc = bacc.Bacc("TRN2", target_bir_lowering=False, num_devices=1)
    d, given = {}, {}
    for name, a in feeds.items():
        a = np.ascontiguousarray(a)
        given[f"in_{name}"] = a
        d[name] = nc.dram_tensor(f"in_{name}", a.shape, mybir.dt.from_np(a.dtype), kind="ExternalInput").ap()
    out = nc.dram_tensor("out", (ROWS, D), F32, kind="ExternalOutput").ap()
    graph_layers(nc, d, out)
    result = run_bass_kernel_spmd(nc, [given], core_ids=[0])
    return result.results[0]["out"][:N]
```

```python
from contextlib import ExitStack

import concourse.bass as bass
import concourse.mybir as mybir
from concourse.alu_op_type import AluOpType as ALU

F32, BF16, I32 = mybir.dt.float32, mybir.dt.bfloat16, mybir.dt.int32
ACT = mybir.ActivationFunctionType
AXX = mybir.AxisListType.X

P = 128
N, E, D, H = 6250, 106250, 256, 4
C = D // H
NREL = 64
CHUNK, WIN = 1024, 128
U = CHUNK // P
NCH = -(-E // CHUNK)
MAXPASS = NCH + N // WIN
SL = 3
DRAIN = 2
NIT = -(-(MAXPASS + DRAIN) // SL)
NK = 3 + SL * NIT
TILES = 50
ROWS = TILES * P
PAD_DST = N + 200
BIG = 1.0e30
EPS = 1e-5
GW = D + 2 * H
AW = D + 2 * H
XW = D + 1


class Chain:

    def __init__(self, eng, sem):
        self.eng, self.sem, self.n = eng, sem, 0

    def do(self, ins):
        self.n += 1
        ins.then_inc(self.sem, 1)
        self.eng.wait_ge(self.sem, self.n)


class Stage:

    def __init__(self, nc, tag):
        self.nc, self.tag, self.ctx, self.sems = nc, tag, ExitStack(), []

    def sb(self, name, shape, dt=F32):
        return self.ctx.enter_context(self.nc.sbuf_tensor(f"{self.tag}_{name}", shape, dt))

    def ps(self, name, shape, dt=F32):
        return self.ctx.enter_context(self.nc.psum_tensor(f"{self.tag}_{name}", shape, dt))

    def sem(self, name):
        s = self.nc.alloc_semaphore(f"{self.tag}_{name}")
        self.sems.append(s)
        return s

    def close(self):
        self.ctx.close()
        self.nc.clear_and_free_semaphores(self.sems)
        self.nc.all_engine_barrier()


def prime(sp, buffers, sems, n, r):
    for buf, sem in zip(buffers, sems):
        sp.dma_start(buf[0:1, 0:1], r["x_dram"][0:1, 0:1]).then_inc(sem, n)


def top(ap):
    return ap.bitcast(BF16)[:, 1::2]


def bcast(ap, shape):
    return ap.to_broadcast(shape)


def setup_stage(nc, d, r):
    s = Stage(nc, "setup")
    dst_i = s.sb("dst_i", [NCH, CHUNK + 2], I32)
    src_i = s.sb("src_i", [NCH, CHUNK], I32)
    typ_i = s.sb("typ_i", [NCH, CHUNK], I32)
    dst_f = s.sb("dst_f", [NCH, CHUNK + 2])
    src_f = s.sb("src_f", [NCH, CHUNK])
    typ_f = s.sb("typ_f", [NCH, CHUNK])
    isfirst = s.sb("isfirst", [NCH, CHUNK])
    islast = s.sb("islast", [NCH, CHUNK])
    steplast = s.sb("steplast", [NCH, CHUNK])
    chunklast = s.sb("chunklast", [P, NK, U])
    upper = s.sb("upper", [P, NCH])
    ones = s.sb("ones", [P, P])
    krow = s.sb("krow", [P, NK])
    lo = s.sb("lo", [NCH, 1])
    hi = s.sb("hi", [NCH, 1])
    span_i = s.sb("span_i", [NCH, 1], I32)
    npass = s.sb("npass", [NCH, 1])
    cum = s.sb("cum", [NCH, 1])
    cumend = s.sb("cumend", [NCH, 1])
    base = s.sb("base", [NCH, 1])
    pick = s.sb("pick", [NCH, NK])
    pick2 = s.sb("pick2", [NCH, NK])
    nodes = s.sb("nodes", [NCH, NK])
    n0b = s.sb("n0b", [P, NK])
    anyb = s.sb("anyb", [P, NK])
    count = s.sb("count", [P, 1])
    its = s.sb("its", [P, NIT])
    nits = s.sb("nits", [P, 1])
    blocks = [(0, P), (P, NK - P)]
    n0c = [s.sb(f"n0c{b}", [P, 1]) for b in range(2)]
    rowf = [s.sb(f"rowf{b}", [P, CHUNK], BF16) for b in range(2)]
    rowd = [s.sb(f"rowd{b}", [P, CHUNK], BF16) for b in range(2)]
    rowt = [s.sb(f"rowt{b}", [P, CHUNK], BF16) for b in range(2)]
    zeros = s.sb("zeros", [P, 2 * D])
    attb = s.sb("attb", [P, 4, D])
    wtmp = s.sb("wtmp", [P, 2, D])
    qcol = s.sb("qcol", [P, 2])
    qmat = s.sb("qmat", [P, 2, P])
    bqkv = s.sb("bqkv", [P, 3 * D])
    phi = s.sb("phi", [P, 2, D])
    tb = s.sb("tb", [P, D])
    pst = [s.ps(f"pst{i}", [P, 512]) for i in range(4)]
    psn = s.ps("psn", [P, 512])
    psa = s.ps("psa", [P, 512])
    psc = s.ps("psc", [P, 512])
    psq = s.ps("psq", [P, 512])

    edges_in = s.sem("edges_in")
    weights_in = s.sem("weights_in")
    iota_done = s.sem("iota_done")
    dve_step = s.sem("dve_step")
    npass_ready = s.sem("npass_ready")
    cum_done = s.sem("cum_done")
    pick_ready = s.sem("pick_ready")
    n0_done = s.sem("n0_done")
    n0_used = s.sem("n0_used")
    tab_done = s.sem("tab_done")
    tab_used = s.sem("tab_used")
    qmat_ready = s.sem("qmat_ready")
    qbias_done = s.sem("qbias_done")
    qbias_used = s.sem("qbias_used")
    rows_ready = s.sem("rows_ready")
    zeros_ready = s.sem("zeros_ready")
    stored = s.sem("stored")
    NE, NW = 5, 24

    jobs = [("pass", "src", u) for u in range(U)] + [("pass", "dst", u) for u in range(U)]
    jobs += [("pass", "last", u) for u in range(U)] + [("pass", "steplast", u) for u in range(U)] + [("row", n, b, h) for n in ("dst", "first", "typ")
                                                      for b in range(2) for h in range(2)]
    source = {"src": src_f, "dst": dst_f, "last": islast, "steplast": steplast, "first": isfirst, "typ": typ_f}

    with nc.Block() as block:
        @block.sync
        def _(sp):
            flat = d["dst"]
            view = lambda a: flat[a:a + NCH * CHUNK].rearrange("(c e) -> c e", e=CHUNK)
            sp.dma_start(dst_i[:, 1:CHUNK + 1], view(1)).then_inc(edges_in, 16)
            sp.dma_start(dst_i[:, 0:1], view(0)[:, 0:1], allow_slow_non_contiguous=True).then_inc(edges_in, 16)
            sp.dma_start(dst_i[:, CHUNK + 1:CHUNK + 2], view(2)[:, CHUNK - 1:CHUNK],
                         allow_slow_non_contiguous=True).then_inc(edges_in, 16)
            sp.dma_start(src_i[:, :], d["src"]).then_inc(edges_in, 16)
            sp.dma_start(typ_i[:, :], d["typ"]).then_inc(edges_in, 16)

            def weight(dst, src):
                sp.dma_start(dst, src).then_inc(weights_in, 16)

            def halves(w):
                return w.rearrange("(a p) n -> p a n", p=P)

            weight(r["w0"][:, :, 0:D], halves(d["W0"]))
            weight(r["w2"][:, :, 0:D], halves(d["W2"]))
            for i, name in enumerate(("as0", "ad0", "as2", "ad2")):
                weight(attb[:, i, :], bcast(d[name].rearrange("(a h) c -> a (h c)", a=1), [P, D]))
            for i, name in enumerate(("Wk", "Wv", "Wq")):
                weight(r["wkvq"][:, :, i * D:(i + 1) * D], halves(d[name]))
            for i, name in enumerate(("bk", "bv", "bq")):
                weight(bqkv[:, i * D:(i + 1) * D], bcast(d[name].rearrange("(a n) -> a n", a=1), [P, D]))
            weight(r["wo"][:, :, :], halves(d["Wo"]))
            sp.dma_start(qcol[:, :], d["query"].rearrange("(a p) -> p a", p=P),
                         allow_slow_non_contiguous=True).then_inc(weights_in, 16)
            weight(r["relw"][:, 0, :], d["rel"])
            for name in ("b0", "b2", "bo", "gamma", "beta"):
                weight(r[name][:, :], bcast(d[name].rearrange("(a n) -> a n", a=1), [P, D]))
            weight(r["w3"][:, :, D:2 * D], halves(d["thetaT"]))
            weight(phi[:, :, :], halves(d["phiT"]))
            weight(r["b3"][:, D:2 * D], bcast(d["theta_b"].rearrange("(a n) -> a n", a=1), [P, D]))
            weight(tb[:, :], bcast(d["phi_b"].rearrange("(a n) -> a n", a=1), [P, D]))
            sp.wait_ge(zeros_ready, 1)
            n = 0
            for acc, w in (("agg", AW), ("aggx", XW)):
                for a in range(N, ROWS, P):
                    m = min(P, ROWS - a)
                    sp.dma_start(d[acc][a:a + m, :], zeros[0:m, 0:w]).then_inc(stored, 16)
                    n += 1
            sp.wait_ge(rows_ready, 1)
            for b, (k0, m) in enumerate(blocks):
                for t, dr in ((rowd, "dstrow"), (rowf, "firstrow"), (rowt, "typrow")):
                    sp.dma_start(d[dr][k0:k0 + m, :], t[b][0:m, :]).then_inc(stored, 16)
                    n += 1
                for h in range(H):
                    rows = d["firstrow4"][k0:k0 + m, :].rearrange("k (u h e) -> k u h e", h=H, e=P)
                    sp.dma_start(rows[:, :, h, :], rowf[b][0:m, :].rearrange("k (u e) -> k u e", e=P)).then_inc(stored, 16)
                    n += 1
            sp.wait_ge(stored, 16 * n)

        @block.gpsimd
        def _(pool):
            nc.gpsimd.iota(r["iota_i"][:, 0:P], [[1, P]], base=0, channel_multiplier=0).then_inc(iota_done, 1)
            nc.gpsimd.iota(r["iota_i"][:, P:P + NK], [[1, NK]], base=-1, channel_multiplier=0).then_inc(iota_done, 1)
            nc.gpsimd.iota(r["iota_i"][:, P + NK:P + NK + 1], [[1, 1]], base=0, channel_multiplier=1).then_inc(iota_done, 1)

        @block.vector
        def _(dve):
            v = nc.vector
            c = Chain(dve, dve_step)
            dve.wait_ge(iota_done, 3)
            c.do(v.tensor_copy(r["iota_row"][:, :], r["iota_i"][:, 0:P]))
            c.do(v.tensor_copy(krow[:, :], r["iota_i"][:, P:P + NK]))
            c.do(v.tensor_copy(r["iota_col"][:, :], r["iota_i"][:, P + NK:P + NK + 1]))
            c.do(v.tensor_scalar(r["ident"][:, :], r["iota_row"][:, :], r["iota_col"][:, 0:1], None, ALU.is_equal))
            c.do(v.tensor_scalar(upper[:, :], r["iota_row"][:, 0:NCH], r["iota_col"][:, 0:1], None, ALU.is_gt))
            c.do(v.memset(ones[:, :], 1.0))
            v.memset(zeros[:, :], 0.0).then_inc(zeros_ready, 1)
            dve.wait_ge(edges_in, 16 * NE)
            c.do(v.tensor_copy(dst_f[:, :], dst_i[:, :]))
            c.do(v.tensor_copy(src_f[:, :], src_i[:, :]))
            c.do(v.tensor_copy(typ_f[:, :], typ_i[:, :]))
            c.do(v.tensor_scalar(lo[:, :], r["iota_col"][0:NCH, 0:1], 0.0, None, ALU.is_gt))
            c.do(v.tensor_tensor(lo[:, :], lo[:, :], dst_f[:, 1:2], ALU.mult))
            c.do(v.tensor_scalar(hi[:, :], dst_f[:, CHUNK + 1:CHUNK + 2], float(N), None, ALU.min))
            c.do(v.tensor_tensor(span_i[:, :], hi[:, :], lo[:, :], ALU.subtract))
            c.do(v.tensor_scalar(span_i[:, :], span_i[:, :], WIN.bit_length() - 1, None, ALU.arith_shift_right))
            c.do(v.tensor_copy(npass[:, :], span_i[:, :]))
            v.tensor_scalar(npass[:, :], npass[:, :], 1.0, None, ALU.add).then_inc(npass_ready, 1)
            c.do(v.tensor_tensor(isfirst[:, :], dst_f[:, 1:CHUNK + 1], dst_f[:, 0:CHUNK], ALU.not_equal))
            c.do(v.tensor_tensor(islast[:, :], dst_f[:, 1:CHUNK + 1], dst_f[:, 2:CHUNK + 2], ALU.not_equal))
            c.do(v.memset(islast[:, CHUNK - 1:CHUNK], 1.0))
            c.do(v.tensor_copy(steplast[:, :], islast[:, :]))
            c.do(v.memset(steplast[:, P - 1:CHUNK:P], 1.0))
            dve.wait_ge(cum_done, 1)
            c.do(v.tensor_copy(cum[:, :], psn[0:NCH, 0:1]))
            dve.wait_ge(npass_ready, 1)
            c.do(v.tensor_tensor(cumend[:, :], cum[:, :], npass[:, :], ALU.add))
            c.do(v.tensor_scalar(pick[:, :], krow[0:NCH, :], cum[:, 0:1], None, ALU.is_ge))
            c.do(v.tensor_scalar(pick2[:, :], krow[0:NCH, :], cumend[:, 0:1], None, ALU.is_lt))
            c.do(v.tensor_tensor(pick[:, :], pick[:, :], pick2[:, :], ALU.mult))
            c.do(v.scalar_tensor_tensor(base[:, :], cum[:, :], float(-WIN), lo[:, :], ALU.mult, ALU.add))
            c.do(v.tensor_scalar(nodes[:, :], krow[0:NCH, :], float(WIN), base[:, 0:1], ALU.mult, ALU.add))
            v.tensor_tensor(nodes[:, :], nodes[:, :], pick[:, :], ALU.mult).then_inc(pick_ready, 1)
            dve.wait_ge(n0_done, 1)
            c.do(v.tensor_copy(anyb[:, :], psa[:, 0:NK]))
            c.do(v.scalar_tensor_tensor(n0b[:, :], anyb[:, :], float(-N), psn[:, 16:16 + NK], ALU.mult, ALU.add))
            c.do(v.tensor_scalar(n0b[:, :], n0b[:, :], float(N), None, ALU.add))
            c.do(v.memset(r["n0_i"][:, 0:2], N))
            c.do(v.tensor_copy(r["n0_i"][:, 2:2 + NK], n0b[0:1, :]))
            c.do(v.memset(r["delta"][:, 0:1], -1.0))
            c.do(v.tensor_tensor(r["delta"][:, 1:NK], n0b[:, 1:NK], n0b[:, 0:NK - 1], ALU.subtract))
            c.do(v.tensor_scalar(r["rowneg"][:, :], r["delta"][:, :], 0.0, None, ALU.is_ge))
            c.do(v.scalar_tensor_tensor(r["rowneg"][:, :], r["delta"][:, :], float(WIN), r["rowneg"][:, :],
                                        ALU.is_lt, ALU.mult))
            c.do(v.tensor_scalar(r["rowneg"][:, :], r["rowneg"][:, :], r["ident"][:, 0:1], None, ALU.mult))
            c.do(v.tensor_scalar(r["rowneg"][:, :], r["rowneg"][:, :], -1.0, BIG, ALU.add, ALU.mult))
            c.do(v.reduce_sum(count[:, :], anyb[:, :], axis=AXX))
            c.do(v.tensor_scalar(its[:, :], r["iota_row"][:, 0:NIT], float(SL), None, ALU.mult))
            c.do(v.tensor_scalar(its[:, :], its[:, :], -(DRAIN - 1.0), count[:, 0:1], ALU.add, ALU.is_le))
            c.do(v.reduce_sum(nits[:, :], its[:, :], axis=AXX))
            c.do(v.tensor_copy(r["nits_i"][:, :], nits[0:1, :]))
            for b, (k0, m) in enumerate(blocks):
                c.do(v.tensor_scalar(n0c[b][0:m, :], psc[0:m, 2 * b:2 * b + 1], float(-N), None, ALU.mult))
                c.do(v.scalar_tensor_tensor(n0c[b][0:m, :], psc[0:m, 2 * b + 1:2 * b + 2], 1.0, n0c[b][0:m, :],
                                            ALU.mult, ALU.add))
                c.do(v.tensor_scalar(n0c[b][0:m, :], n0c[b][0:m, :], float(N), None, ALU.add))
            for i, job in enumerate(jobs):
                ps = pst[i % 4]
                dve.wait_ge(tab_done, i + 1)
                if job[0] == "pass":
                    _, name, u = job
                    if name == "dst":
                        ins = v.tensor_tensor(r["dstloc"][:, :, u], ps[:, 0:NK], n0b[:, :], ALU.subtract)
                    else:
                        out = {"src": r["src_pass"], "last": chunklast, "steplast": r["islast"]}[name]
                        ins = v.tensor_copy(out[:, :, u], ps[:, 0:NK])
                else:
                    _, name, b, h = job
                    m, cols = blocks[b][1], slice(h * 512, (h + 1) * 512)
                    if name == "dst":
                        ins = v.tensor_scalar(rowd[b][0:m, cols], ps[0:m, :], n0c[b][0:m, 0:1], None, ALU.subtract)
                    elif name == "first":
                        ins = v.tensor_scalar(rowf[b][0:m, cols], ps[0:m, :], -BIG, None, ALU.mult)
                    else:
                        ins = v.tensor_copy(rowt[b][0:m, cols], ps[0:m, :])
                ins.then_inc(tab_used, 1)
            dve.wait_ge(tab_used, len(jobs))
            c.do(v.tensor_scalar(r["lastloc"][:, :, :], r["dstloc"][:, :, :], 1.0, None, ALU.add))
            c.do(v.tensor_tensor(r["lastloc"][:, :, :], r["lastloc"][:, :, :], chunklast[:, :, :], ALU.mult))
            c.do(v.tensor_scalar(r["lastloc"][:, :, :], r["lastloc"][:, :, :], -1.0, None, ALU.add))
            v.memset(wtmp[:, :, :], 0.0).then_inc(rows_ready, 1)
            dve.wait_ge(rows_ready, 1)
            dve.wait_ge(weights_in, 16 * NW)
            for w, i0 in (("w0", 0), ("w2", 2)):
                for i in range(2):
                    c.do(v.tensor_tensor(wtmp[:, :, :], r[w][:, :, 0:D],
                                         bcast(attb[:, i0 + i, :].unsqueeze(1), [P, 2, D]), ALU.mult))
                    c.do(v.reduce_sum(r[w][:, :, D + H * i:D + H * (i + 1)],
                                      wtmp[:, :, :].rearrange("p a (h c) -> p a h c", c=C), axis=AXX))
            c.do(v.tensor_scalar(r["wkvq"][:, :, 2 * D:3 * D], r["wkvq"][:, :, 2 * D:3 * D], C ** -0.5, None, ALU.mult))
            c.do(v.tensor_scalar(bqkv[:, 2 * D:3 * D], bqkv[:, 2 * D:3 * D], C ** -0.5, None, ALU.mult))
            c.do(v.tensor_scalar(r["relw"][:, 0, :], r["relw"][:, 0, :], 0.2, None, ALU.mult))
            for i in range(2):
                c.do(v.tensor_tensor(r["relw"][:, i + 1, :], r["relw"][:, i, :], top(r["relw"][:, i, :]), ALU.subtract))
            c.do(v.tensor_tensor(r["w3"][:, :, 0:D], phi[:, :, :], r["w3"][:, :, D:2 * D], ALU.subtract))
            c.do(v.memset(r["b3"][:, 0:D], 0.0))
            c.do(v.tensor_tensor(r["b3"][:, D:2 * D], r["b3"][:, D:2 * D], tb[:, :], ALU.add))
            c.do(v.tensor_scalar(qcol[:, :], qcol[:, :], 0.1, None, ALU.mult))
            v.tensor_copy(qmat[:, :, :], bcast(qcol[:, :].unsqueeze(2), [P, 2, P])).then_inc(qmat_ready, 1)
            for i in range(3):
                dve.wait_ge(qbias_done, i + 1)
                v.tensor_tensor(r["b1"][:, i * D:(i + 1) * D], psq[:, 0:D], bqkv[:, i * D:(i + 1) * D],
                                ALU.add).then_inc(qbias_used, 1)
            c.do(v.memset(r["zero_b"][:, :], 0.0))
            c.do(v.memset(r["mean"][:, :], 0.0))
            c.do(v.memset(r["rstd"][:, :], 1.0))

        @block.tensor
        def _(pe):
            t = nc.tensor
            pe.wait_ge(npass_ready, 1)
            t.matmul(psn[0:NCH, 0:1], upper[0:NCH, :], npass[:, :], start=True, stop=True).then_inc(cum_done, 1)
            pe.wait_ge(pick_ready, 1)
            t.matmul(psa[:, 0:NK], ones[0:NCH, :], pick[:, :], start=True, stop=True)
            for b, (k0, m) in enumerate(blocks):
                t.matmul(psc[0:m, 2 * b:2 * b + 1], pick[:, k0:k0 + m], ones[0:NCH, 0:1], start=True, stop=True)
                t.matmul(psc[0:m, 2 * b + 1:2 * b + 2], nodes[:, k0:k0 + m], ones[0:NCH, 0:1], start=True, stop=True)
            t.matmul(psn[:, 16:16 + NK], ones[0:NCH, :], nodes[:, :], start=True, stop=True).then_inc(n0_done, 1)
            for i, job in enumerate(jobs):
                ps = pst[i % 4]
                if i >= 4:
                    pe.wait_ge(tab_used, i - 3)
                if job[0] == "pass":
                    _, name, u = job
                    x = source[name]
                    o = 1 if name == "dst" else 0
                    ins = t.matmul(ps[:, 0:NK], x[:, o + u * P:o + (u + 1) * P], pick[:, :], start=True, stop=True)
                else:
                    _, name, b, h = job
                    k0, m = blocks[b]
                    o = (1 if name == "dst" else 0) + h * 512
                    ins = t.matmul(ps[0:m, :], pick[:, k0:k0 + m], source[name][:, o:o + 512], start=True, stop=True)
                ins.then_inc(tab_done, 1)
            pe.wait_ge(qmat_ready, 1)
            for i in range(3):
                if i:
                    pe.wait_ge(qbias_used, i)
                w = r["wkvq"][:, :, i * D:(i + 1) * D]
                t.matmul(psq[:, 0:D], qmat[:, 0, :], w[:, 0, :], start=True, stop=False)
                t.matmul(psq[:, 0:D], qmat[:, 1, :], w[:, 1, :], start=False, stop=True).then_inc(qbias_done, 1)
    s.close()


def project_stage(nc, d, r, y, tag, weights, bias, cols, stores):
    s = Stage(nc, tag)
    B = 2
    xn = [s.sb(f"xn{b}", [P, D]) for b in range(B)]
    xT = [s.sb(f"xT{b}", [P, D]) for b in range(B)]
    ob = [s.sb(f"ob{b}", [P, cols]) for b in range(B)]
    psT = [s.ps(f"psT{b}", [P, 512]) for b in range(B)]
    psO = [s.ps(f"psO{b}", [P, -(-cols // 512) * 512]) for b in range(B)]
    pieces = [(a, min(a + 512, cols)) for a in range(0, cols, 512)]
    ready = s.sem("ready")
    norm_done = s.sem("norm_done")
    kept = [s.sem(f"kept{b}") for b in range(B)]
    transposed, xT_ready = s.sem("transposed"), s.sem("xT_ready")
    product_done, row_ready = s.sem("product_done"), s.sem("row_ready")
    stored = [s.sem(f"stored{b}") for b in range(B)]
    CR = B
    at = lambda t: t + 1 + CR

    NST = 16 * len(stores)

    with nc.Block() as block:
        @block.gpsimd
        def _(pool):
            for x in (norm_done, transposed, xT_ready, product_done, row_ready):
                pool.sem_inc(x, CR)
            pool.sem_inc(ready, 1)

        @block.vector
        def _(dve):
            dve.wait_ge(ready, 1)
            with dve.Fori(0, TILES // B) as i:
                for b in range(B):
                    t = i * B + b
                    dve.wait_ge(transposed, at(t - B))
                    dve.wait_ge(kept[b], 16 * (i + 1))
                    nc.vector.tensor_scalar(xn[b][:, :], y[:, bass.ds(t * D, D)], r["mean"][:, bass.ds(t, 1)],
                                            r["rstd"][:, bass.ds(t, 1)], ALU.subtract, ALU.mult).then_inc(norm_done, 1)
                    dve.wait_ge(product_done, at(t))
                    dve.wait_ge(stored[b], NST * (i + 1))
                    nc.vector.tensor_tensor(ob[b][:, :], psO[b][:, 0:cols], bias, ALU.add).then_inc(row_ready, 1)

        @block.tensor
        def _(pe):
            pe.wait_ge(ready, 1)
            with pe.Fori(0, TILES // B) as i:
                for b in range(B):
                    t = i * B + b
                    pe.wait_ge(xT_ready, at(t - B))
                    pe.wait_ge(norm_done, at(t))
                    nc.tensor.transpose(psT[b][:, 0:P], xn[b][:, 0:P], r["ident"][:, :])
                    nc.tensor.transpose(psT[b][:, P:D], xn[b][:, P:D], r["ident"][:, :]).then_inc(transposed, 1)
                    pe.wait_ge(row_ready, at(t - B))
                    pe.wait_ge(xT_ready, at(t))
                    for a, e in pieces:
                        nc.tensor.matmul(psO[b][:, a:e], xT[b][:, 0:P], weights[:, 0, a:e], start=True, stop=False)
                        ins = nc.tensor.matmul(psO[b][:, a:e], xT[b][:, P:D], weights[:, 1, a:e], start=False, stop=True)
                    ins.then_inc(product_done, 1)

        @block.scalar
        def _(act):
            act.wait_ge(ready, 1)
            with act.Fori(0, TILES // B) as i:
                for b in range(B):
                    t = i * B + b
                    act.wait_ge(product_done, at(t - B))
                    act.wait_ge(transposed, at(t))
                    nc.scalar.copy(xT[b][:, :], psT[b][:, 0:D]).then_inc(xT_ready, 1)

        @block.sync
        def _(sp):
            prime(sp, ob, stored, NST, r)
            prime(sp, xn, kept, 16, r)
            sp.wait_ge(ready, 1)
            with sp.Fori(0, TILES // B) as i:
                for b in range(B):
                    t = i * B + b
                    sp.wait_ge(norm_done, at(t))
                    sp.dma_start(d["x"][bass.ds(t * P, P), :], xn[b][:, :]).then_inc(kept[b], 16)
                    sp.wait_ge(row_ready, at(t))
                    for k, (a, e, dram) in enumerate(stores):
                        ins = sp.dma_start(dram[bass.ds(t * P, P), :], ob[b][:, a:e])
                        ins.then_inc(stored[b], 16)
            for b in range(B):
                sp.wait_ge(stored[b], NST * (1 + TILES // B))
                sp.wait_ge(kept[b], 16 * (1 + TILES // B))
    s.close()


def edge_stage(nc, d, r, tag, relational):
    s = Stage(nc, tag)
    V0 = D if relational else 0
    AU = 4 if relational else 0
    tab, gw = (d["kv"], 2 * D) if relational else (d["h"], GW)
    wtab = d["q"] if relational else d["h"][:, D + H:GW]
    WC = D if relational else H
    M3 = 3 * H
    idx = [s.sb(f"idx{j}", [P, U], I32) for j in range(SL)]
    G = [s.sb(f"G{j}", [P, U, gw]) for j in range(SL)]
    dstrow = [s.sb(f"dstrow{j}", [P, CHUNK], BF16) for j in range(SL)]
    firstrow = [s.sb(f"firstrow{j}", [U * H, P], BF16) for j in range(SL)]
    window = [s.sb(f"window{j}", [P, WC]) for j in range(SL)]
    onehot = [s.sb(f"onehot{j}", [P, U, P]) for j in range(SL)]
    onehotT = [s.sb(f"onehotT{j}", [P, CHUNK], F32 if relational else BF16) for j in range(SL)]
    ph = [s.sb(f"ph{j}", [P, U, D + H]) for j in range(SL)]
    outw = [s.sb(f"outw{j}", [P, AW]) for j in range(SL)]
    shift = [s.sb(f"shift{j}", [P, P]) for j in range(SL)]
    m3 = [s.sb(f"m3_{j}", [P, M3]) for j in range(SL)]
    gex = [s.sb(f"gex{j}", [P, H]) for j in range(SL)]
    scanned = s.sb("scanned", [U * H, P])
    score = [s.sb(f"score{j}", [P, U, H]) for j in range(SL)]
    last3 = s.sb("last3", [P, U, M3 + 1])
    stepmax = s.sb("stepmax", [P, U, H])
    absent = s.sb("absent", [P, U])
    winmax = s.sb("winmax", [P, H])
    refmax = s.sb("refmax", [P, U, H])
    gin = s.sb("gin", [P, H])
    carried = s.sb("carried", [P, D + H])
    psO = [s.ps(f"psO{j}", [P, 512]) for j in range(SL)]
    psC = s.ps("psC", [P, 512])
    psS = s.ps("psS", [P, 512])
    psM = [psO[j][:, D + H:D + H + U * (M3 + 1)] for j in range(SL)]
    psR = [psO[j][:, 512 - U * M3:512] for j in range(SL)]
    psCm, psF, psT = psC[:, D + H:D + 2 * H], psS[:, 0:U * H], psS[0:U * H, P:2 * P]
    parts = lambda ap, w: ap.rearrange("p (u w) -> p u w", w=w)[:, :, 0:M3].rearrange("p u (a h) -> p u h a", h=H)
    flat = lambda ap: ap.rearrange("p u h -> p (u h)")
    by_head = lambda ap: ap.rearrange("p u (h c) -> p u h c", c=C)
    if relational:
        typrow = [s.sb(f"typrow{j}", [NREL, CHUNK], BF16) for j in range(SL)]
        typeT = s.sb("typeT", [NREL, CHUNK], BF16)
        modk = s.sb("modk", [P, U, D])
        psRel = s.ps("psRel", [P, 512])
        psQ = [s.ps(f"psQ{i}", [P, 512]) for i in range(2)]
    else:
        psA = s.ps("psA", [P, U * M3])
        w3 = s.sb("w3", [P, M3])
        ssum = s.sb("ssum", [P, U, H])

    ready = s.sem("ready")
    gathered = [[nc.alloc_semaphore(f"{tag}_gathered{j}_{u}") for u in range(U)] for j in range(SL)]
    dstrow_in = [s.sem(f"dstrow_in{j}") for j in range(SL)]
    firstrow_in = [s.sem(f"firstrow_in{j}") for j in range(SL)]
    window_in = [s.sem(f"window_in{j}") for j in range(SL)]
    out_stored = [s.sem(f"out_stored{j}") for j in range(SL)]
    first_pass = {n: 1 for n in (
        "score_ready", "scoreT_done", "scan_done", "scanback_done", "last_top", "last_mid", "last3_ready",
        "presence_ready", "nodemax_done", "stepsum", "absent_ready", "stepmax_ready", "winmax_ready", "carrym_done",
        "m_ready", "m_mid", "m3_ready", "refmax_done", "refsum", "expin_ready", "prob_ready", "gdiff", "gin_ready",
        "rescale_ready", "kept_max", "onehot_ready", "onehotT_ready", "shift_ready")}
    first_pass.update({n: 0 for n in ("weighted", "aggregated")})
    if AU:
        first_pass["weighted_act"] = 0
    first_pass.update({n: -1 for n in ("carry_done", "carried_ready", "out_ready")})
    if relational:
        first_pass.update({n: 1 for n in ("typeT_ready", "rel_done", "modk_ready")})
        typrow_in = [s.sem(f"typrow_in{j}") for j in range(SL)]
        q_done, q_used = s.sem("q_done"), s.sem("q_used")
    else:
        first_pass.update({n: 1 for n in ("w_mid", "w3_ready", "adst_done", "summed", "added")})
    q = {n: s.sem(n) for n in first_pass}
    idx_ready = s.sem("idx_ready")
    buffers_zero, all_stored = s.sem("buffers_zero"), s.sem("all_stored")
    store_due = s.sem("store_due")
    NQ = U // 2
    at = lambda k: k + SL

    def passes(eng, body):
        nit = eng.value_load(r["nits_i"][0:1, 0:1], min_val=1, max_val=NIT)
        with eng.Fori(0, NIT) as i:
            with eng.If(i < nit):
                for j in range(SL):
                    body(i, SL * i + j + 1, (j + 1) % SL, j)
        return nit

    loaded = lambda i, j: 16 * (i + 1 + j // SL)
    rowi = lambda k: bass.ds(k, 1)

    with nc.Block() as block:
        @block.gpsimd
        def _(pool):
            for n, x in q.items():
                pool.sem_inc(x, SL + first_pass[n] - 1)
            if relational:
                pool.sem_inc(q_used, SL * NQ)
                pool.sem_inc(q_done, SL * NQ)
            pool.sem_inc(ready, 1)

            def gather(k, sl):
                if AU:
                    pool.wait_ge(ready, 1)
                    pool.wait_ge(q["weighted_act"], at(k - SL))
                pool.wait_ge(ready, 1)
                pool.wait_ge(q["weighted"], at(k - SL))
                nc.gpsimd.tensor_copy(idx[sl][:, :], r["src_pass"][:, rowi(k), :].rearrange(
                    "p a u -> p (a u)")).then_inc(idx_ready, 1)
                pool.wait_ge(ready, 1)
                pool.wait_ge(idx_ready, at(k - SL))
                for u in range(U):
                    nc.gpsimd.indirect_dma_start(
                        G[sl][:, u, :], None, tab,
                        bass.IndirectOffsetOnAxis(ap=idx[sl][:, u:u + 1], axis=0)).then_inc(gathered[sl][u], 16)

            pool.wait_ge(buffers_zero, 1)
            gather(1, 1)
            passes(pool, lambda i, k, sl, j: gather(k + 1, (sl + 1) % SL))

        @block.sync
        def _(sp):
            prime(sp, outw, out_stored, 16, r)

            def load(k, sl):
                sp.dma_start(dstrow[sl][:, :], bcast(d["dstrow"][rowi(k), :], [P, CHUNK])).then_inc(dstrow_in[sl], 16)
                sp.dma_start(firstrow[sl][:, :], d["firstrow4"][rowi(k), :].rearrange(
                    "k (r e) -> (k r) e", e=P)).then_inc(firstrow_in[sl], 16)
                n0 = sp.value_load(r["n0_i"][0:1, bass.ds(k + 2, 1)], min_val=0, max_val=N)
                sp.dma_start(window[sl][:, :], wtab[bass.ds(n0, P), :]).then_inc(window_in[sl], 16)
                if relational:
                    sp.dma_start(typrow[sl][:, :], bcast(d["typrow"][rowi(k), :], [NREL, CHUNK])).then_inc(
                        typrow_in[sl], 16)

            def store(k, sl, before):
                n0 = sp.value_load(r["n0_i"][0:1, bass.ds(k + 2, 1)], min_val=0, max_val=N)
                sp.wait_ge(out_stored[(sl - 1) % SL], before)
                sp.sem_inc(store_due, 1)
                sp.wait_ge(q["kept_max"], at(k))
                sp.wait_ge(q["out_ready"], at(k))
                sp.sem_inc(store_due, 1)
                sp.dma_start(d["agg"][bass.ds(n0, P), :], outw[sl][:, :]).then_inc(out_stored[sl], 16)

            load(1, 1)
            load(2, 2)
            sp.wait_ge(ready, 1)
            sp.wait_ge(buffers_zero, 1)

            def body(i, k, sl, j):
                if relational:
                    sp.wait_ge(q_done, NQ * at(k - 1))
                sp.wait_ge(q["onehotT_ready"], at(k - 1))
                sp.wait_ge(q["scan_done"], at(k - 1))
                sp.wait_ge(q["typeT_ready" if relational else "w3_ready"], at(k - 1))
                load(k + 2, (sl + 2) % SL)
                store(k - 3, sl, 16 * (i + (2 if j else 1)))
            nit = passes(sp, body)
            sp.wait_ge(ready, 1)
            store(nit * SL - 2, (SL - 2) % SL, 16 * (nit + 1))
            seen, seen2 = sp.snap(16 * (nit + 1)), sp.snap(16 * (nit + 2))
            sp.wait_ge(ready, 1)
            for j in range(SL):
                sp.wait_ge(out_stored[j], seen2 if j == 1 else seen)
            for x in [dstrow_in, firstrow_in, window_in] + ([typrow_in] if relational else []):
                sp.wait_ge(x[1], seen)
                sp.wait_ge(x[2], seen)
            sp.sem_inc(all_stored, 1)

        @block.vector
        def _(dve):
            v = nc.vector

            def build_onehot(k, sl):
                loc = r["dstloc"][:, rowi(k), :].rearrange("p a u -> p (a u)").unsqueeze(2)
                v.tensor_tensor(onehot[sl][:, :, :], bcast(loc, [P, U, P]),
                                bcast(r["iota_row"][:, :].unsqueeze(1), [P, U, P]), ALU.is_equal).then_inc(
                                    q["onehot_ready"], 1)

            def ahead(k, sl, at_k, in_now):
                dve.wait_ge(q["refmax_done"], at_k - SL)
                if relational:
                    dve.wait_ge(q_done, NQ * (at_k - SL))
                dve.wait_ge(dstrow_in[sl], in_now)
                v.tensor_scalar(onehotT[sl][:, :], dstrow[sl][:, :], r["iota_col"][:, 0:1], None,
                                ALU.is_equal).then_inc(q["onehotT_ready"], 1)
                if relational:
                    dve.wait_ge(q["rel_done"], at_k - 1)
                    dve.wait_ge(typrow_in[sl], in_now)
                    v.tensor_scalar(typeT[:, :], typrow[sl][:, :], r["iota_col"][0:NREL, 0:1], None,
                                    ALU.is_equal).then_inc(q["typeT_ready"], 1)

            def adst_top(sl, at_k, in_now):
                dve.wait_ge(q["adst_done"], at_k - 1)
                dve.wait_ge(window_in[sl], in_now)
                v.tensor_scalar(w3[:, 0:H], window[sl][:, :], 1.0, None, ALU.mult).then_inc(q["w_mid"], 1)

            def adst_mid(sl, at_k):
                dve.wait_ge(q["w_mid"], 2 * at_k - SL - 1)
                v.tensor_tensor(w3[:, H:2 * H], w3[:, 0:H], top(w3[:, 0:H]), ALU.subtract).then_inc(q["w_mid"], 1)

            def adst_low(sl, at_k):
                dve.wait_ge(q["w_mid"], 2 * at_k - SL)
                v.tensor_tensor(w3[:, 2 * H:M3], w3[:, H:2 * H], top(w3[:, H:2 * H]), ALU.subtract).then_inc(
                    q["w3_ready"], 1)

            def build_shift(k, sl, at_k):
                dve.wait_ge(q["carry_done"], at_k - SL)
                dve.wait_ge(q["carrym_done"], at_k - SL)
                v.tensor_scalar(shift[sl][:, 0:1], r["iota_col"][:, 0:1], r["delta"][:, rowi(k)], None,
                                ALU.is_equal).then_inc(q["shift_ready"], 1)

            def add_relation(k, sl, in_now):
                for u in range(U):
                    dve.wait_ge(gathered[sl][u], in_now)
                dve.wait_ge(q["score_ready"], at(k - 1))
                dve.wait_ge(q["rel_done"], at(k))
                v.tensor_tensor(by_head(modk[:, :, :]), by_head(G[sl][:, :, 0:D]),
                                bcast(psRel[:, :].rearrange("p (u c) -> p u c", c=C).unsqueeze(2), [P, U, H, C]),
                                ALU.add).then_inc(q["modk_ready"], 1)

            def times_queries(k, ns):
                dve.wait_ge(q["modk_ready"], at(k))
                for n in ns:
                    dve.wait_ge(q_done, NQ * at(k - 1) + n + 1)
                    m = modk[:, 2 * n:2 * n + 2, :].rearrange("p u n -> p (u n)")
                    v.tensor_tensor(m, m, psQ[n % 2][:, :], ALU.mult).then_inc(q_used, 1)

            def sum_products(k, sl):
                dve.wait_ge(q_used, NQ * at(k))
                dve.wait_ge(q["expin_ready"], at(k - SL))
                dve.wait_ge(q["scoreT_done"], at(k - SL))
                v.reduce_sum(flat(score[sl][:, :, :]), modk[:, :, :].rearrange("p u (h c) -> p (u h) c", c=C),
                             axis=AXX).then_inc(q["score_ready"], 1)

            def sum_parts(k):
                dve.wait_ge(q["score_ready"], at(k - 1))
                dve.wait_ge(q["adst_done"], at(k))
                v.reduce_sum(ssum[:, :, :], parts(psA[:, :], M3), axis=AXX).then_inc(q["summed"], 1)

            def add_source(k, sl, in_now):
                for u in range(U):
                    dve.wait_ge(gathered[sl][u], in_now)
                dve.wait_ge(q["summed"], at(k))
                v.tensor_tensor(ssum[:, :, :], G[sl][:, :, D:D + H], ssum[:, :, :], ALU.add).then_inc(q["added"], 1)

            def leaky(k, sl):
                dve.wait_ge(q["added"], at(k))
                dve.wait_ge(q["expin_ready"], at(k - SL))
                dve.wait_ge(q["scoreT_done"], at(k - SL))
                v.scalar_tensor_tensor(score[sl][:, :, :], ssum[:, :, :], 0.2, ssum[:, :, :], ALU.mult,
                                       ALU.max).then_inc(q["score_ready"], 1)

            for j in range(SL):
                dve.wait_ge(out_stored[j], 16)
                v.memset(outw[j][:, :], 0.0)
                v.memset(gex[j][:, :], 1.0)
                v.memset(shift[j][:, :], 0.0)
            v.memset(psO[SL - 1][:, :], 0.0)
            v.memset(m3[0][:, :], 0.0)
            v.memset(G[0][:, :, :], 0.0)
            v.memset(ph[0][:, :, :], 0.0)
            v.memset(onehot[0][:, :, :], 0.0).then_inc(buffers_zero, 1)
            dve.wait_ge(buffers_zero, 1)
            dve.wait_ge(ready, 1)
            build_onehot(1, 1)
            build_shift(1, 1, at(1))
            for k in (1, 2):
                ahead(k, k, at(k), 16)
                if not relational:
                    adst_top(k, at(k), 16)
                    adst_mid(k, at(k))
                    adst_low(k, at(k))
            if relational:
                add_relation(1, 1, 16)
                times_queries(1, range(NQ))
                sum_products(1, 1)
            else:
                sum_parts(1)
                add_source(1, 1, 16)
                leaky(1, 1)

            def body(i, k, sl, j):
                pv, nx, p2 = (sl - 1) % SL, (sl + 1) % SL, (sl - 2) % SL
                far, now_far, now_next = at(k + 2), loaded(i, j + 2), loaded(i, j + 1)
                dve.wait_ge(firstrow_in[sl], loaded(i, j))
                dve.wait_ge(q["scanback_done"], at(k - 1))
                dve.wait_ge(q["scoreT_done"], at(k))
                v.tensor_tensor_scan(scanned[:, :], firstrow[sl][:, :], psT, -BIG, ALU.add, ALU.max).then_inc(
                    q["scan_done"], 1)
                dve.wait_ge(q["prob_ready"], at(k - 1))
                v.tensor_tensor(by_head(ph[pv][:, 0:U - AU, 0:D]), by_head(G[pv][:, 0:U - AU, V0:V0 + D]),
                                bcast(ph[pv][:, 0:U - AU, D:D + H].unsqueeze(3), [P, U - AU, H, C]), ALU.mult).then_inc(
                                    q["weighted"], 1)
                dve.wait_ge(q["nodemax_done"], at(k - 1))
                dve.wait_ge(q["scanback_done"], at(k))
                v.tensor_tensor(last3[:, :, 0:H], psF.rearrange("p (u h) -> p u h", h=H),
                                bcast(r["islast"][:, rowi(k), :].rearrange("p a u -> p (a u)").unsqueeze(2), [P, U, H]),
                                ALU.mult).then_inc(q["last_top"], 1)
                dve.wait_ge(q["rescale_ready"], at(k - 2))
                dve.wait_ge(q["carrym_done"], at(k))
                dve.wait_ge(q["carry_done"], at(k - 2))
                v.tensor_tensor(carried[:, 0:D].rearrange("p (h c) -> p h c", c=C),
                                psC[:, 0:D].rearrange("p (h c) -> p h c", c=C),
                                bcast(gex[p2][:, :].unsqueeze(2), [P, H, C]), ALU.mult)
                v.tensor_tensor(carried[:, D:D + H], psC[:, D:D + H], gex[p2][:, :], ALU.mult).then_inc(
                    q["carried_ready"], 1)
                dve.wait_ge(q["last_top"], at(k))
                top3 = last3[:, :, :].bitcast(BF16)
                v.tensor_tensor(last3[:, :, H:2 * H], last3[:, :, 0:H], top3[:, :, 1:2 * H:2], ALU.subtract).then_inc(
                    q["last_mid"], 1)
                dve.wait_ge(q["carried_ready"], at(k - 2))
                dve.wait_ge(q["aggregated"], at(k - 2))
                v.tensor_tensor(outw[p2][:, 0:D + H], carried[:, :], psO[p2][:, 0:D + H], ALU.add).then_inc(
                    q["out_ready"], 1)
                dve.wait_ge(q["last_mid"], at(k))
                v.tensor_tensor(last3[:, :, 2 * H:M3], last3[:, :, H:2 * H], top3[:, :, 2 * H + 1:4 * H:2],
                                ALU.subtract).then_inc(q["last3_ready"], 1)
                if relational:
                    add_relation(k + 1, nx, now_next)
                dve.wait_ge(q["nodemax_done"], at(k))
                v.reduce_sum(stepmax[:, :, :], parts(psM[sl], M3 + 1), axis=AXX).then_inc(q["stepsum"], 1)
                v.tensor_scalar(absent[:, :], psM[sl].rearrange("p (u w) -> p u w", w=M3 + 1)[:, :, M3], -1.0, BIG,
                                ALU.add, ALU.mult).then_inc(q["absent_ready"], 1)
                if relational:
                    times_queries(k + 1, [0])
                else:
                    adst_top(pv, far, now_far)
                dve.wait_ge(q["stepsum"], at(k))
                dve.wait_ge(q["absent_ready"], at(k))
                v.tensor_tensor(stepmax[:, :, :], stepmax[:, :, :], bcast(absent[:, :].unsqueeze(2), [P, U, H]),
                                ALU.add).then_inc(q["stepmax_ready"], 1)
                if relational:
                    times_queries(k + 1, [1])
                else:
                    adst_mid(pv, far)
                dve.wait_ge(q["stepmax_ready"], at(k))
                v.reduce_max(winmax[:, :], stepmax[:, :, :].rearrange("p u h -> p h u"), axis=AXX).then_inc(
                    q["winmax_ready"], 1)
                if not relational:
                    adst_low(pv, far)
                dve.wait_ge(q["kept_max"], at(k - 1))
                dve.wait_ge(q["carrym_done"], at(k))
                dve.wait_ge(q["winmax_ready"], at(k))
                v.scalar_tensor_tensor(m3[sl][:, 0:H], psCm, r["rowneg"][:, rowi(k)], winmax[:, :], ALU.add,
                                       ALU.max).then_inc(q["m_ready"], 1)
                if not relational:
                    sum_parts(k + 1)
                dve.wait_ge(q["m_ready"], at(k))
                v.tensor_tensor(m3[sl][:, H:2 * H], m3[sl][:, 0:H], top(m3[sl][:, 0:H]), ALU.subtract).then_inc(
                    q["m_mid"], 1)
                if not relational:
                    add_source(k + 1, nx, now_next)
                dve.wait_ge(q["m_mid"], at(k))
                v.tensor_tensor(m3[sl][:, 2 * H:M3], m3[sl][:, H:2 * H], top(m3[sl][:, H:2 * H]),
                                ALU.subtract).then_inc(q["m3_ready"], 1)
                dve.wait_ge(q["rescale_ready"], at(k - 1))
                v.tensor_tensor(gin[:, :], psCm, m3[sl][:, 0:H], ALU.subtract).then_inc(q["gdiff"], 1)
                build_shift(k + 1, nx, at(k + 1))
                dve.wait_ge(q["gdiff"], at(k))
                v.tensor_scalar(gin[:, :], gin[:, :], 0.0, None, ALU.min).then_inc(q["gin_ready"], 1)
                if relational:
                    times_queries(k + 1, range(2, NQ))
                if not relational:
                    leaky(k + 1, nx)
                dve.wait_ge(q["prob_ready"], at(k - 1))
                dve.wait_ge(q["refmax_done"], at(k))
                v.reduce_sum(refmax[:, :, :], parts(psR[sl], M3), axis=AXX).then_inc(q["refsum"], 1)
                dve.wait_ge(q["refsum"], at(k))
                v.tensor_tensor(refmax[:, :, :], score[sl][:, :, :], refmax[:, :, :], ALU.subtract).then_inc(
                    q["expin_ready"], 1)
                dve.wait_ge(q["aggregated"], at(k - 2))
                build_onehot(k + 1, nx)
                ahead(k + 2, pv, far, now_far)
                if relational:
                    sum_products(k + 1, nx)
            passes(dve, body)

        @block.scalar
        def _(act):
            act.wait_ge(buffers_zero, 1)
            act.wait_ge(ready, 1)
            a = nc.scalar

            def body(i, k, sl, j):
                pv = (sl - 1) % SL
                act.wait_ge(ready, 1)
                act.wait_ge(q["nodemax_done"], at(k - 1))
                a.copy(last3[:, :, M3], r["islast"][:, rowi(k), :].rearrange("p a u -> p (a u)")).then_inc(
                    q["presence_ready"], 1)
                if AU:
                    act.wait_ge(q["prob_ready"], at(k - 1))
                    for u in range(U - AU, U):
                        for h in range(H):
                            ins = a.activation(ph[pv][:, u, h * C:(h + 1) * C], G[pv][:, u, V0 + h * C:V0 + (h + 1) * C],
                                               ACT.Copy, scale=ph[pv][:, u, D + h:D + h + 1])
                    ins.then_inc(q["weighted_act"], 1)
                act.wait_ge(out_stored[sl], 16 * (i + 2))
                act.wait_ge(q["m_ready"], at(k))
                a.copy(outw[sl][:, D + H:AW], m3[sl][:, 0:H]).then_inc(q["kept_max"], 1)
                act.wait_ge(q["carried_ready"], at(k - 3))
                act.wait_ge(q["gin_ready"], at(k))
                a.activation(gex[sl][:, :], gin[:, :], ACT.Exp).then_inc(q["rescale_ready"], 1)
                act.wait_ge(q["aggregated"], at(k - 3))
                act.wait_ge(q["expin_ready"], at(k))
                a.activation(ph[sl][:, :, D:D + H], refmax[:, :, :], ACT.Exp).then_inc(q["prob_ready"], 1)
            passes(act, body)

        @block.tensor
        def _(pe):
            t = nc.tensor
            pe.wait_ge(buffers_zero, 1)
            pe.wait_ge(ready, 1)
            cut = lambda u: slice(u * P, (u + 1) * P)
            top_of = lambda ap: ap if ap.dtype == BF16 else top(ap)

            def queries(n, k, sl, in_now=None):
                if in_now is not None:
                    pe.wait_ge(window_in[sl], in_now)
                pe.wait_ge(q_used, NQ * at(k - 1) + n - 1)
                for e in range(2):
                    ins = t.matmul(psQ[n % 2][:, e * D:(e + 1) * D], onehotT[sl][:, cut(2 * n + e)],
                                   window[sl][:, :], start=True, stop=True)
                ins.then_inc(q_done, 1)

            def ahead(k, sl):
                pe.wait_ge(q["onehotT_ready"], at(k))
                if relational:
                    pe.wait_ge(q["modk_ready"], at(k - 1))
                    pe.wait_ge(q["typeT_ready"], at(k))
                    for u in range(U):
                        for n in range(3):
                            ins = t.matmul(psRel[:, u * C:(u + 1) * C], typeT[:, cut(u)], top(r["relw"][:, n, :]),
                                           start=(n == 0), stop=(n == 2))
                    ins.then_inc(q["rel_done"], 1)
                else:
                    pe.wait_ge(q["summed"], at(k - 1))
                    pe.wait_ge(q["w3_ready"], at(k))
                    for u in range(U):
                        ins = t.matmul(psA[:, u * M3:(u + 1) * M3], onehotT[sl][:, cut(u)], top(w3[:, :]),
                                       start=True, stop=True)
                    ins.then_inc(q["adst_done"], 1)

            def turn(k, sl):
                pe.wait_ge(ready, 1)
                pe.wait_ge(q["scan_done"], at(k - 1))
                pe.wait_ge(q["score_ready"], at(k))
                t.transpose(psT, flat(score[sl][:, :, :]), r["ident"][:, :]).then_inc(q["scoreT_done"], 1)

            ahead(1, 1)
            if relational:
                for n in range(NQ):
                    queries(n, 1, 1, None if n else 16)
            ahead(2, 2)
            if not relational:
                turn(1, 1)

            def body(i, k, sl, j):
                pv, p2, nx = (sl - 1) % SL, (sl - 2) % SL, (sl + 1) % SL
                def carry():
                    pe.wait_ge(q["out_ready"], at(k - 3))
                    pe.wait_ge(q["gdiff"], at(k - 1))
                    t.matmul(psC[:, 0:D + H], shift[p2][:, :], outw[sl][:, 0:D + H], start=True, stop=True).then_inc(
                        q["carry_done"], 1)
                    pe.wait_ge(q["shift_ready"], at(k))
                    t.matmul(psCm, shift[sl][:, :], m3[pv][:, 0:H], start=True, stop=True).then_inc(q["carrym_done"], 1)

                def turn_back():
                    pe.wait_ge(ready, 1)
                    pe.wait_ge(q["last_top"], at(k - 1))
                    pe.wait_ge(q["scan_done"], at(k))
                    t.transpose(psF, scanned[:, :], r["ident"][0:U * H, 0:U * H]).then_inc(q["scanback_done"], 1)

                def sums(us):
                    for u in us:
                        ins = t.matmul(psO[pv][:, 0:D + H], onehot[pv][:, u, :], ph[pv][:, u, :], start=(u == 0),
                                       stop=(u == U - 1))
                    return ins

                if relational:
                    turn(k, sl)
                if relational:
                    turn_back()
                carry()
                if not relational:
                    turn_back()
                if relational:
                    queries(0, k + 1, nx, loaded(i, j + 1))
                    queries(1, k + 1, nx)
                pe.wait_ge(q["presence_ready"], at(k))
                pe.wait_ge(q["stepsum"], at(k - 1))
                pe.wait_ge(q["absent_ready"], at(k - 1))
                pe.wait_ge(q["onehot_ready"], at(k))
                pe.wait_ge(q["last3_ready"], at(k))
                for u in range(U):
                    ins = t.matmul(psM[sl][:, u * (M3 + 1):(u + 1) * (M3 + 1)], top(onehot[sl][:, u, :]), top(last3[:, u, :]),
                                   start=True, stop=True)
                ins.then_inc(q["nodemax_done"], 1)
                pe.wait_ge(q["out_ready"], at(k - 3))
                pe.wait_ge(q["weighted"], at(k - 1))
                sums(range(0, 1))
                sums(range(1, 3))
                if relational:
                    queries(2, k + 1, nx)
                    queries(3, k + 1, nx)
                pe.wait_ge(q["refsum"], at(k - 1))
                pe.wait_ge(q["m3_ready"], at(k))
                for u in range(U):
                    ins = t.matmul(psR[sl][:, u * M3:(u + 1) * M3], top_of(onehotT[sl][:, cut(u)]), top(m3[sl][:, :]),
                                   start=True, stop=True)
                ins.then_inc(q["refmax_done"], 1)
                if not relational:
                    turn(k + 1, nx)
                sums(range(3, 4))
                if AU:
                    pe.wait_ge(q["weighted_act"], at(k - 1))
                sums(range(4, U)).then_inc(q["aggregated"], 1)
                ahead(k + 2, pv)
            passes(pe, body)
    s.close()


def edgeconv_stage(nc, d, r, tag):
    s = Stage(nc, tag)
    NG, NB = 4, U // 2
    idx = [s.sb(f"idx{j}", [P, U], I32) for j in range(SL)]
    G = [s.sb(f"G{j}", [P, U, D]) for j in range(SL)]
    firstrow = [s.sb(f"firstrow{j}", [P, CHUNK], BF16) for j in range(SL)]
    onehot = [s.sb(f"onehot{j}", [P, U, P]) for j in range(SL)]
    scanned = [[s.sb(f"scanned{j}_{h}", [P, CHUNK]) for h in range(2)] for j in range(SL)]
    back = [s.sb(f"back{j}", [P, U, XW]) for j in range(SL)]
    outw = [s.sb(f"outw{j}", [P, XW]) for j in range(SL)]
    psT = [s.ps(f"psT{i}", [P, 512]) for i in range(4)]
    psB = [s.ps(f"psB{i}", [P, 512]) for i in range(3)]
    psO = s.ps("psO", [P, 512])
    ready = s.sem("ready")
    gathered = [[nc.alloc_semaphore(f"{tag}_gathered{j}_{u}") for u in range(U)] for j in range(SL)]
    firstrow_in = [s.sem(f"firstrow_in{j}") for j in range(SL)]
    out_stored = [s.sem(f"out_stored{j}") for j in range(SL)]
    idx_ready, onehot_ready, selected, out_ready = (s.sem(n) for n in (
        "idx_ready", "onehot_ready", "selected", "out_ready"))
    turned, scan_done, back_done, back_ready = (s.sem(n) for n in ("turned", "scan_done", "back_done", "back_ready"))
    buffers_zero, all_stored = s.sem("buffers_zero"), s.sem("all_stored")
    store_due = s.sem("store_due")
    at = lambda k: k + SL
    at4 = lambda k: NG * (k + SL)
    rowi = lambda k: bass.ds(k, 1)
    loaded = lambda i, j: 16 * (i + 1 + j // SL)

    def passes(eng, body):
        nit = eng.value_load(r["nits_i"][0:1, 0:1], min_val=1, max_val=NIT)
        with eng.Fori(0, NIT) as i:
            with eng.If(i < nit):
                for j in range(SL):
                    body(i, SL * i + j + 1, (j + 1) % SL, j)
        return nit

    with nc.Block() as block:
        @block.gpsimd
        def _(pool):
            for x in (onehot_ready, selected, out_ready):
                pool.sem_inc(x, SL)
            for x in (turned, scan_done, back_done, back_ready):
                pool.sem_inc(x, NG * SL)
            pool.sem_inc(ready, 1)

            def body(i, k, sl, j):
                pool.wait_ge(ready, 1)
                mine = pool.snap(at(k - SL))
                pool.wait_ge(turned, at4(k - SL))
                nc.gpsimd.tensor_copy(idx[sl][:, :], r["src_pass"][:, rowi(k), :].rearrange(
                    "p a u -> p (a u)")).then_inc(idx_ready, 1)
                pool.wait_ge(ready, 1)
                pool.wait_ge(idx_ready, mine)
                for u in range(U):
                    nc.gpsimd.indirect_dma_start(
                        G[sl][:, u, :], None, d["bx"],
                        bass.IndirectOffsetOnAxis(ap=idx[sl][:, u:u + 1], axis=0)).then_inc(gathered[sl][u], 16)
            passes(pool, body)

        @block.sync
        def _(sp):
            prime(sp, outw, out_stored, 16, r)

            def load(k, sl):
                sp.dma_start(firstrow[sl][:, :], bcast(d["firstrow"][rowi(k), :], [P, CHUNK])).then_inc(firstrow_in[sl], 16)

            load(1, 1)
            sp.wait_ge(ready, 1)

            def body(i, k, sl, j):
                sp.wait_ge(scan_done, at4(k - 2))
                load(k + 1, (sl + 1) % SL)
                n0 = sp.value_load(r["n0_i"][0:1, bass.ds(k + 2, 1)], min_val=0, max_val=N)
                before = 16 * (i + (2 if j else 1))
                sp.wait_ge(out_stored[(sl - 1) % SL], before)
                sp.sem_inc(store_due, 1)
                sp.wait_ge(out_ready, at(k))
                sp.sem_inc(store_due, 1)
                sp.dma_start(d["aggx"][bass.ds(n0, P), :], outw[sl][:, :]).then_inc(out_stored[sl], 16)
            nit = passes(sp, body)
            seen = sp.snap(16 * (nit + 1))
            sp.wait_ge(ready, 1)
            for j in range(SL):
                sp.wait_ge(out_stored[j], seen)
            sp.wait_ge(firstrow_in[1], seen)
            sp.sem_inc(all_stored, 1)

        @block.vector
        def _(dve):
            v = nc.vector
            for j in range(SL):
                v.memset(back[j][:, :, D:XW], 1.0)
            for h in range(2):
                v.memset(scanned[0][h][:, :], 0.0).then_inc(buffers_zero, 1)
            dve.wait_ge(ready, 1)
            dve.wait_ge(buffers_zero, 2)

            def body(i, k, sl, j):
                pv = (sl - 1) % SL
                dve.wait_ge(selected, at(k - SL))
                loc = r["lastloc"][:, rowi(k), :].rearrange("p a u -> p (a u)").unsqueeze(2)
                v.tensor_tensor(onehot[sl][:, :, :], bcast(loc, [P, U, P]),
                                bcast(r["iota_row"][:, :].unsqueeze(1), [P, U, P]), ALU.is_equal).then_inc(onehot_ready, 1)
                dve.wait_ge(firstrow_in[sl], loaded(i, j))
                dve.wait_ge(back_done, at4(k - SL))
                for n in range(NG):
                    a, h = n // 2, n % 2
                    cols = slice(a * 512, (a + 1) * 512)
                    start = scanned[sl][h][:, 511:512] if a else scanned[pv][h][:, CHUNK - 1:CHUNK]
                    dve.wait_ge(scan_done, at4(k - 1) + n - 1)
                    dve.wait_ge(turned, at4(k - 1) + n + 1)
                    v.tensor_tensor_scan(scanned[sl][h][:, cols], firstrow[sl][:, cols], psT[n][:, :], start,
                                         ALU.add, ALU.max).then_inc(scan_done, 1)
            passes(dve, body)

        @block.scalar
        def _(act):
            for j in range(SL):
                act.wait_ge(out_stored[j], 16)
            act.wait_ge(ready, 1)

            def body(i, k, sl, j):
                act.wait_ge(selected, at(k - SL))
                for n in range(NB):
                    act.wait_ge(back_done, at4(k - 1) + n + 1)
                    nc.scalar.copy(back[sl][:, 2 * n:2 * n + 2, 0:D],
                                   psB[(NB * j + n) % 3][:, :].rearrange("p (u n) -> p u n", u=2)).then_inc(back_ready, 1)
                act.wait_ge(out_stored[sl], 16 * (i + 1))
                act.wait_ge(selected, at(k))
                nc.scalar.copy(outw[sl][:, :], psO[:, 0:XW]).then_inc(out_ready, 1)
            passes(act, body)

        @block.tensor
        def _(pe):
            t = nc.tensor
            pe.wait_ge(ready, 1)
            pe.wait_ge(buffers_zero, 2)

            def body(i, k, sl, j):
                for u in range(U):
                    pe.wait_ge(gathered[sl][u], 16 * (i + 1))
                for n in range(NG):
                    a, h = n // 2, n % 2
                    pe.wait_ge(ready, 1)
                    pe.wait_ge(scan_done, at4(k - 1) + n + 1 - NG)
                    for u in range(4):
                        ins = t.transpose(psT[n][:, u * P:(u + 1) * P], G[sl][:, 4 * a + u, h * P:(h + 1) * P],
                                          r["ident"][:, :])
                    ins.then_inc(turned, 1)
                for n in range(NB):
                    pe.wait_ge(ready, 1)
                    pe.wait_ge(back_ready, at4(k - 1) + n + 1 - 3)
                    pe.wait_ge(scan_done, at4(k - 1) + 2 * (n // 2) + 2)
                    for u in (2 * n, 2 * n + 1):
                        for h in range(2):
                            ins = t.transpose(psB[(NB * j + n) % 3][:, (u - 2 * n) * D + h * P:(u - 2 * n) * D + (h + 1) * P],
                                              scanned[sl][h][:, u * P:(u + 1) * P], r["ident"][:, :])
                    ins.then_inc(back_done, 1)
                pe.wait_ge(out_ready, at(k - 1))
                pe.wait_ge(onehot_ready, at(k))
                pe.wait_ge(back_ready, at4(k))
                for u in range(U):
                    ins = t.matmul(psO[:, 0:XW], onehot[sl][:, u, :], back[sl][:, u, :], start=(u == 0), stop=(u == U - 1))
                ins.then_inc(selected, 1)
            passes(pe, body)
    s.close()


def coefficient_stage(nc, d, r, tag, kind, ca, cs):
    s = Stage(nc, tag)
    T4 = [P, TILES, H]
    aux = s.sb("aux", [P, TILES, 2 * H])
    own = s.sb("own", [P, TILES, 2 * H])
    tmp = [s.sb(f"tmp{i}", T4) for i in range(4)]
    loaded, dve_step, ex_in, ex_out = s.sem("loaded"), s.sem("dve_step"), s.sem("ex_in"), s.sem("ex_out")
    tiles = lambda dram: dram.rearrange("(t p) w -> p t w", p=P)
    with nc.Block() as block:
        @block.sync
        def _(sp):
            sp.dma_start(aux[:, :, :], tiles(d["agg"])[:, :, D:AW]).then_inc(loaded, 16)
            if kind != "relational":
                sp.dma_start(own[:, :, :], tiles(d["h"])[:, :, D:GW]).then_inc(loaded, 16)

        @block.scalar
        def _(act):
            if kind != "relational":
                act.wait_ge(ex_in, 2)
                nc.scalar.activation(tmp[0][:, :, :], tmp[0][:, :, :], ACT.Exp)
                nc.scalar.activation(tmp[1][:, :, :], tmp[1][:, :, :], ACT.Exp).then_inc(ex_out, 1)

        @block.vector
        def _(dve):
            v, c = nc.vector, Chain(dve, dve_step)
            den, mx = aux[:, :, 0:H], aux[:, :, H:2 * H]
            ea, es, empty, x = (t[:, :, :] for t in tmp)
            dve.wait_ge(loaded, 16 if kind == "relational" else 32)
            c.do(v.tensor_scalar(empty, den, 0.0, None, ALU.is_equal))
            if kind == "relational":
                c.do(v.tensor_tensor(den, den, empty, ALU.add))
                c.do(v.reciprocal(ca[:, :, :], den))
                c.do(v.tensor_copy(cs[:, :, :], empty))
                return
            c.do(v.tensor_tensor(x, own[:, :, 0:H], own[:, :, H:2 * H], ALU.add))
            c.do(v.scalar_tensor_tensor(es, x, 0.2, x, ALU.mult, ALU.max))
            c.do(v.tensor_tensor(x, mx, es, ALU.max))
            v.tensor_tensor(ea, mx, x, ALU.subtract).then_inc(ex_in, 1)
            v.tensor_tensor(es, es, x, ALU.subtract).then_inc(ex_in, 1)
            dve.wait_ge(ex_out, 1)
            c.do(v.tensor_tensor(x, den, ea, ALU.mult))
            c.do(v.tensor_tensor(x, x, es, ALU.add))
            if kind == "relu":
                c.do(v.tensor_scalar(x, x, 1e-16, None, ALU.add))
            c.do(v.reciprocal(x, x))
            c.do(v.tensor_tensor(ca[:, :, :], ea, x, ALU.mult))
            c.do(v.tensor_tensor(cs[:, :, :], es, x, ALU.mult))
    s.close()


def stats_stage(nc, r, tag, mv):
    s = Stage(nc, tag)
    dve_step, var_ready, root_ready = s.sem("dve_step"), s.sem("var_ready"), s.sem("root_ready")
    with nc.Block() as block:
        @block.vector
        def _(dve):
            v, c = nc.vector, Chain(dve, dve_step)
            c.do(v.tensor_copy(r["mean"][:, :], mv[:, :, 0]))
            v.tensor_scalar(r["rstd"][:, :], mv[:, :, 1], EPS, None, ALU.add).then_inc(var_ready, 1)
            dve.wait_ge(root_ready, 1)
            c.do(v.reciprocal(r["rstd"][:, :], r["rstd"][:, :]))

        @block.scalar
        def _(act):
            act.wait_ge(var_ready, 1)
            nc.scalar.activation(r["rstd"][:, :], r["rstd"][:, :], ACT.Sqrt).then_inc(root_ready, 1)
    s.close()


def combine_stage(nc, d, r, y, tag, kind, ca, cs, mv, bias):
    s = Stage(nc, tag)
    B = 5
    IT = TILES // B
    att = kind != "conv"
    dram_a, wa = (d["agg"], D) if att else (d["aggx"], XW)
    dram_h = {"relu": d["h"][:, 0:D], "elu": d["h"][:, 0:D], "relational": d["kv"][:, D:2 * D], "conv": d["ax"]}[kind]
    acc = [s.sb(f"acc{b}", [P, wa]) for b in range(B)]
    hv = [s.sb(f"hv{b}", [P, D]) for b in range(B)]
    xt = [s.sb(f"xt{b}", [P, D]) for b in range(B)]
    hs = [s.sb(f"hs{b}", [P, D]) for b in range(B)]
    ta = [s.sb(f"ta{b}", [P, D]) for b in range(B)]
    tb = [s.sb(f"tb{b}", [P, D]) for b in range(B)]
    st = [s.sb(f"st{b}", [P, 6]) for b in range(B)]
    mvt = [s.sb(f"mvt{b}", [P, 2]) for b in range(B)]
    psT = [s.ps(f"psT{b}", [P, 512]) for b in range(2)]
    psW = [s.ps(f"psW{b}", [P, 512]) for b in range(2)]
    loaded = [s.sem(f"loaded{b}") for b in range(B)]
    ready = s.sem("ready")
    names = ["own_ready", "scaled", "summed", "biased", "exp_ready", "turned", "xT_ready", "product_done", "half_done",
             "y_ready", "stats_ready", "scaled_b", "aggr_ready", "tile_done"]
    q = {n: s.sem(n) for n in names}
    at = lambda t: t + 1 + B
    heads = lambda ap: ap.rearrange("p (h c) -> p h c", c=C)
    coef = lambda c, t: bcast(c[:, bass.ds(t, 1), :].rearrange("p a h -> p (a h)").unsqueeze(2), [P, H, C])
    with nc.Block() as block:
        @block.sync
        def _(sp):
            sp.wait_ge(ready, 1)
            with sp.Fori(0, IT) as i:
                for b in range(B):
                    t = i * B + b
                    sp.wait_ge(q["tile_done"], at(t - B))
                    rows = bass.ds(t * P, P)
                    sp.dma_start(acc[b][:, :], dram_a[rows, 0:wa]).then_inc(loaded[b], 16)
                    sp.dma_start(hv[b][:, :], dram_h[rows, :]).then_inc(loaded[b], 16)
                    sp.dma_start(xt[b][:, :], d["x"][rows, :]).then_inc(loaded[b], 16)

        @block.gpsimd
        def _(pool):
            for x in q.values():
                pool.sem_inc(x, B)
            pool.sem_inc(ready, 1)
            with pool.Fori(0, IT) as i:
                for b in range(B):
                    t = i * B + b
                    pool.wait_ge(ready, 1)
                    pool.wait_ge(q["tile_done"], at(t - B))
                    pool.wait_ge(loaded[b], 48 * (i + 1))
                    g = nc.gpsimd
                    if att:
                        ins = g.tensor_tensor(heads(hs[b][:, :]), heads(hv[b][:, :]), coef(cs, t), ALU.mult)
                        if kind == "relational":
                            ins = g.tensor_tensor(xt[b][:, :], xt[b][:, :], bias, ALU.add)
                    else:
                        ins = g.tensor_tensor(hs[b][:, :], hv[b][:, :], acc[b][:, 0:D], ALU.add)
                    ins.then_inc(q["own_ready"], 1)

        @block.vector
        def _(dve):
            v = nc.vector
            dve.wait_ge(ready, 1)

            def first(i, b, t):
                if not att:
                    dve.wait_ge(q["own_ready"], at(t))
                    v.tensor_scalar(ta[b][:, :], hs[b][:, :], 0.0, acc[b][:, D:XW], ALU.max, ALU.mult).then_inc(q["biased"], 1)
                    return
                dve.wait_ge(q["tile_done"], at(t - B))
                dve.wait_ge(loaded[b], 48 * (i + 1))
                v.tensor_tensor(heads(ta[b][:, :]), heads(acc[b][:, :]), coef(ca, t), ALU.mult).then_inc(q["scaled"], 1)
                dve.wait_ge(q["own_ready"], at(t))
                dve.wait_ge(q["scaled"], at(t))
                v.tensor_tensor(ta[b][:, :], ta[b][:, :], hs[b][:, :], ALU.add).then_inc(q["summed"], 1)
                if kind == "relational":
                    return
                dve.wait_ge(q["summed"], at(t))
                v.tensor_tensor(ta[b][:, :], ta[b][:, :], bias, ALU.add).then_inc(q["biased"], 1)
                if kind == "elu":
                    dve.wait_ge(q["biased"], at(t))
                    v.tensor_scalar(tb[b][:, :], ta[b][:, :], 0.0, None, ALU.min).then_inc(q["half_done"], 1)

            def second(i, b, t):
                yt = y[:, bass.ds(t * D, D)]
                if kind == "relu":
                    dve.wait_ge(q["biased"], at(t))
                    v.scalar_tensor_tensor(yt, ta[b][:, :], 0.0, xt[b][:, :], ALU.max, ALU.add).then_inc(q["y_ready"], 1)
                elif kind == "elu":
                    dve.wait_ge(q["exp_ready"], at(t))
                    v.scalar_tensor_tensor(ta[b][:, :], ta[b][:, :], 0.0, tb[b][:, :], ALU.max, ALU.add).then_inc(q["scaled_b"], 1)
                    dve.wait_ge(q["scaled_b"], at(t))
                    v.scalar_tensor_tensor(yt, ta[b][:, :], -1.0, xt[b][:, :], ALU.add, ALU.add).then_inc(q["y_ready"], 1)
                elif kind == "relational":
                    dve.wait_ge(q["product_done"], at(t))
                    v.tensor_tensor(yt, psW[0 if b % 2 == 0 else 1][:, 0:D], xt[b][:, :], ALU.add).then_inc(q["y_ready"], 1)
                else:
                    dve.wait_ge(q["biased"], at(t))
                    v.tensor_tensor(yt, ta[b][:, :], xt[b][:, :], ALU.add).then_inc(q["y_ready"], 1)
                dve.wait_ge(ready, 1)
                dve.wait_ge(q["y_ready"], at(t))
                v.bn_stats(st[b][:, :], yt).then_inc(q["stats_ready"], 1)
                dve.wait_ge(ready, 1)
                dve.wait_ge(q["stats_ready"], at(t))
                v.bn_aggr(mvt[b][:, :], st[b][:, :]).then_inc(q["aggr_ready"], 1)
                dve.wait_ge(q["aggr_ready"], at(t))
                v.tensor_scalar(mv[:, bass.ds(t, 1), :].rearrange("p a w -> p (a w)"), mvt[b][:, :], 1.0, None,
                                ALU.mult).then_inc(q["tile_done"], 1)

            with dve.Fori(0, IT) as i:
                first(i, 0, i * B)
                for b in range(1, B):
                    first(i, b, i * B + b)
                    second(i, b - 1, i * B + b - 1)
                second(i, B - 1, i * B + B - 1)

        @block.scalar
        def _(act):
            act.wait_ge(ready, 1)
            if kind in ("elu", "relational"):
                with act.Fori(0, IT) as i:
                    for b in range(B):
                        t = i * B + b
                        if kind == "elu":
                            act.wait_ge(q["half_done"], at(t))
                            nc.scalar.activation(tb[b][:, :], tb[b][:, :], ACT.Exp).then_inc(q["exp_ready"], 1)
                        else:
                            act.wait_ge(q["turned"], at(t))
                            nc.scalar.copy(hs[b][:, :], psT[b % 2][:, 0:D]).then_inc(q["xT_ready"], 1)

        @block.tensor
        def _(pe):
            pe.wait_ge(ready, 1)
            if kind == "relational":
                w = r["wo"]
                with pe.Fori(0, IT) as i:
                    for b in range(B):
                        t = i * B + b
                        pe.wait_ge(ready, 1)
                        pe.wait_ge(q["xT_ready"], at(t - 1))
                        pe.wait_ge(q["summed"], at(t))
                        nc.tensor.transpose(psT[b % 2][:, 0:P], ta[b][:, 0:P], r["ident"][:, :])
                        nc.tensor.transpose(psT[b % 2][:, P:D], ta[b][:, P:D], r["ident"][:, :]).then_inc(q["turned"], 1)
                        pe.wait_ge(q["y_ready"], at(t - 1))
                        pe.wait_ge(q["xT_ready"], at(t))
                        nc.tensor.matmul(psW[b % 2][:, 0:D], hs[b][:, 0:P], w[:, 0, :], start=True, stop=False)
                        nc.tensor.matmul(psW[b % 2][:, 0:D], hs[b][:, P:D], w[:, 1, :], start=False,
                                         stop=True).then_inc(q["product_done"], 1)
    s.close()


def affine_stage(nc, d, r, y, tag, mv):
    s = Stage(nc, tag)
    B = 5
    IT = TILES // B
    xt = [s.sb(f"xt{b}", [P, D]) for b in range(B)]
    z = [s.sb(f"z{b}", [P, D]) for b in range(B)]
    st = [s.sb(f"st{b}", [P, 6]) for b in range(B)]
    mvt = [s.sb(f"mvt{b}", [P, 2]) for b in range(B)]
    loaded = [s.sem(f"loaded{b}") for b in range(B)]
    ready = s.sem("ready")
    q = {n: s.sem(n) for n in ("xb_ready", "z_ready", "zg_ready", "y_ready", "stats_ready", "aggr_ready", "tile_done")}
    at = lambda t: t + 1 + B
    with nc.Block() as block:
        @block.sync
        def _(sp):
            sp.wait_ge(ready, 1)
            with sp.Fori(0, IT) as i:
                for b in range(B):
                    t = i * B + b
                    sp.wait_ge(q["tile_done"], at(t - B))
                    sp.dma_start(xt[b][:, :], d["x"][bass.ds(t * P, P), :]).then_inc(loaded[b], 16)

        @block.gpsimd
        def _(pool):
            for x in q.values():
                pool.sem_inc(x, B)
            pool.sem_inc(ready, 1)
            with pool.Fori(0, IT) as i:
                for b in range(B):
                    pool.wait_ge(ready, 1)
                    pool.wait_ge(loaded[b], 16 * (i + 1))
                    nc.gpsimd.tensor_tensor(xt[b][:, :], xt[b][:, :], r["beta"][:, :], ALU.add).then_inc(q["xb_ready"], 1)

        @block.vector
        def _(dve):
            v = nc.vector
            dve.wait_ge(ready, 1)
            with dve.Fori(0, IT) as i:
                for b in range(B):
                    t = i * B + b
                    yt = y[:, bass.ds(t * D, D)]
                    v.tensor_scalar(z[b][:, :], yt, r["mean"][:, bass.ds(t, 1)], r["rstd"][:, bass.ds(t, 1)],
                                    ALU.subtract, ALU.mult).then_inc(q["z_ready"], 1)
                    dve.wait_ge(q["z_ready"], at(t))
                    v.tensor_tensor(z[b][:, :], z[b][:, :], r["gamma"][:, :], ALU.mult).then_inc(q["zg_ready"], 1)
                    dve.wait_ge(q["xb_ready"], at(t))
                    dve.wait_ge(q["zg_ready"], at(t))
                    v.tensor_tensor(yt, z[b][:, :], xt[b][:, :], ALU.add).then_inc(q["y_ready"], 1)
                    dve.wait_ge(ready, 1)
                    dve.wait_ge(q["y_ready"], at(t))
                    v.bn_stats(st[b][:, :], yt).then_inc(q["stats_ready"], 1)
                    dve.wait_ge(ready, 1)
                    dve.wait_ge(q["stats_ready"], at(t))
                    v.bn_aggr(mvt[b][:, :], st[b][:, :]).then_inc(q["aggr_ready"], 1)
                    dve.wait_ge(q["aggr_ready"], at(t))
                    v.tensor_scalar(mv[:, bass.ds(t, 1), :].rearrange("p a w -> p (a w)"), mvt[b][:, :], 1.0, None,
                                    ALU.mult).then_inc(q["tile_done"], 1)
    s.close()


def output_stage(nc, d, r, y, out):
    s = Stage(nc, "output")
    B = 5
    xo = [s.sb(f"xo{b}", [P, D]) for b in range(B)]
    stored = [s.sem(f"stored{b}") for b in range(B)]
    norm_done, ready = s.sem("norm_done"), s.sem("ready")
    at = lambda t: t + 1
    with nc.Block() as block:
        @block.sync
        def _(sp):
            prime(sp, xo, stored, 16, r)
            with sp.Fori(0, TILES // B) as i:
                for b in range(B):
                    t = i * B + b
                    sp.wait_ge(norm_done, at(t))
                    sp.dma_start(out[bass.ds(t * P, P), :], xo[b][:, :]).then_inc(stored[b], 16)
            for b in range(B):
                sp.wait_ge(stored[b], 16 * (1 + TILES // B))

        @block.vector
        def _(dve):
            with dve.Fori(0, TILES // B) as i:
                for b in range(B):
                    t = i * B + b
                    dve.wait_ge(stored[b], 16 * (i + 1))
                    nc.vector.tensor_scalar(xo[b][:, :], y[:, bass.ds(t * D, D)], r["mean"][:, bass.ds(t, 1)],
                                            r["rstd"][:, bass.ds(t, 1)], ALU.subtract, ALU.mult).then_inc(norm_done, 1)
    s.close()


def load_x_stage(nc, r, y):
    s = Stage(nc, "loadx")
    loaded = s.sem("loaded")
    with nc.Block() as block:
        @block.sync
        def _(sp):
            sp.dma_start(y[:, :].rearrange("p (t n) -> p t n", n=D),
                         r["x_dram"].rearrange("(t p) n -> p t n", p=P)).then_inc(loaded, 16)
            sp.wait_ge(loaded, 16)
    s.close()


def graph_layers(nc, d, out):
    dram = lambda name, shape, dt=F32: nc.dram_tensor(name, shape, dt, kind="Internal").ap()
    d["x"] = dram("x_kept", (ROWS, D))
    d["h"] = dram("h_table", (ROWS, GW))
    d["kv"] = dram("kv_table", (ROWS, 2 * D))
    d["q"] = dram("q_table", (ROWS, D))
    d["bx"] = dram("source_table", (ROWS, D))
    d["ax"] = dram("destination_table", (ROWS, D))
    d["agg"] = dram("aggregates", (ROWS, AW))
    d["aggx"] = dram("maxima", (ROWS, XW))
    d["dstrow"] = dram("dstrow", (NK, CHUNK), BF16)
    d["firstrow"] = dram("firstrow", (NK, CHUNK), BF16)
    d["firstrow4"] = dram("firstrow4", (NK, H * CHUNK), BF16)
    d["typrow"] = dram("typrow", (NK, CHUNK), BF16)
    ctx = ExitStack()
    with ctx:
        def sb(name, shape, dt=F32):
            return ctx.enter_context(nc.sbuf_tensor(name, shape, dt))
        r = {"x_dram": d["x_in"]}
        for name, shape in (("iota_row", [P, P]), ("iota_col", [P, 1]), ("ident", [P, P]), ("dstloc", [P, NK, U]),
                            ("islast", [P, NK, U]), ("lastloc", [P, NK, U]), ("delta", [P, NK]), ("rowneg", [P, NK]), ("w0", [P, 2, GW]),
                            ("w2", [P, 2, GW]), ("wkvq", [P, 2, 3 * D]), ("wo", [P, 2, D]), ("w3", [P, 2, 2 * D]),
                            ("relw", [NREL, 3, C]), ("b0", [P, D]), ("b1", [P, 3 * D]), ("b2", [P, D]), ("b3", [P, 2 * D]),
                            ("bo", [P, D]), ("gamma", [P, D]), ("beta", [P, D]), ("zero_b", [P, GW]),
                            ("mean", [P, TILES]), ("rstd", [P, TILES])):
            r[name] = sb(name, shape)
        r["iota_i"] = sb("iota_i", [P, P + NK + 1], I32)
        r["src_pass"] = sb("src_pass", [P, NK, U], I32)
        r["n0_i"] = sb("n0_i", [1, NK + 2], I32)
        r["nits_i"] = sb("nits_i", [1, 1], I32)
        setup_stage(nc, d, r)

        def project(y, layer):
            if layer in (0, 2):
                project_stage(nc, d, r, y, f"project{layer}", r[f"w{layer}"], r["zero_b"][:, :], GW, [(0, GW, d["h"])])
            elif layer == 1:
                project_stage(nc, d, r, y, "project1", r["wkvq"], r["b1"][:, :], 3 * D,
                              [(0, 2 * D, d["kv"]), (2 * D, 3 * D, d["q"])])
            else:
                project_stage(nc, d, r, y, "project3", r["w3"], r["b3"][:, :], 2 * D,
                              [(0, D, d["bx"]), (D, 2 * D, d["ax"])])

        with nc.sbuf_tensor("y_in", [P, TILES * D], F32) as y:
            load_x_stage(nc, r, y)
            project(y, 0)
        for layer, kind in enumerate(("relu", "relational", "elu", "conv")):
            if kind == "conv":
                edgeconv_stage(nc, d, r, "edges3")
            else:
                edge_stage(nc, d, r, f"edges{layer}", kind == "relational")
            with ExitStack() as nodes:
                y = nodes.enter_context(nc.sbuf_tensor(f"y{layer}", [P, TILES * D], F32))
                mv = nodes.enter_context(nc.sbuf_tensor(f"mv{layer}", [P, TILES, 2], F32))
                ca = nodes.enter_context(nc.sbuf_tensor(f"ca{layer}", [P, TILES, H], F32))
                cs = nodes.enter_context(nc.sbuf_tensor(f"cs{layer}", [P, TILES, H], F32))
                if kind != "conv":
                    coefficient_stage(nc, d, r, f"coef{layer}", kind, ca, cs)
                bias = {"relu": r["b0"], "relational": r["bo"], "elu": r["b2"], "conv": r["b0"]}[kind][:, :]
                combine_stage(nc, d, r, y, f"combine{layer}", kind, ca, cs, mv, bias)
                stats_stage(nc, r, f"stats{layer}", mv)
                if kind == "relational":
                    affine_stage(nc, d, r, y, "affine", mv)
                    stats_stage(nc, r, "stats_affine", mv)
                if kind == "conv":
                    output_stage(nc, d, r, y, out)
                else:
                    project(y, layer + 1)


def kernel(**inputs):
    import numpy as np
    import concourse.bacc as bacc
    from concourse.bass_utils import run_bass_kernel_spmd

    arr = {k: np.asarray(v) for k, v in inputs.items()}
    x = np.zeros((ROWS, D), np.float32)
    x[:N] = arr["x"]
    dst = np.full(1 + NCH * CHUNK + 1, PAD_DST, np.int32)
    dst[0] = -1
    dst[1:1 + E] = arr["dst"]
    src = np.zeros(NCH * CHUNK, np.int32)
    src[:E] = arr["src"]
    typ = np.zeros(NCH * CHUNK, np.int32)
    typ[:E] = arr["edge_type_64"]
    feeds = {
        "x_in": x, "dst": dst, "src": src.reshape(NCH, CHUNK), "typ": typ.reshape(NCH, CHUNK),
        "W0": arr["L0_gnn_W"], "as0": arr["L0_gnn_att_src"], "ad0": arr["L0_gnn_att_dst"], "b0": arr["L0_gnn_bias"],
        "W2": arr["L2_gnn_W"], "as2": arr["L2_gnn_att_src"], "ad2": arr["L2_gnn_att_dst"], "b2": arr["L2_gnn_bias"],
        "query": arr["L1_gnn_query_emb"], "Wq": arr["L1_gnn_Wq"], "bq": arr["L1_gnn_bq"], "Wk": arr["L1_gnn_Wk"],
        "bk": arr["L1_gnn_bk"], "Wv": arr["L1_gnn_Wv"], "bv": arr["L1_gnn_bv"], "rel": arr["L1_gnn_rel_w"],
        "Wo": arr["L1_gnn_Wo"], "bo": arr["L1_gnn_bo"], "gamma": arr["L1_gnn_gamma"], "beta": arr["L1_gnn_beta"],
        "thetaT": np.ascontiguousarray(arr["L3_gnn_theta_w"].T), "theta_b": arr["L3_gnn_theta_b"],
        "phiT": np.ascontiguousarray(arr["L3_gnn_phi_w"].T), "phi_b": arr["L3_gnn_phi_b"],
    }
    nc = bacc.Bacc("TRN2", target_bir_lowering=False, num_devices=1)
    d, given = {}, {}
    for name, a in feeds.items():
        a = np.ascontiguousarray(a)
        given[f"in_{name}"] = a
        d[name] = nc.dram_tensor(f"in_{name}", a.shape, mybir.dt.from_np(a.dtype), kind="ExternalInput").ap()
    out = nc.dram_tensor("out", (ROWS, D), F32, kind="ExternalOutput").ap()
    graph_layers(nc, d, out)
    result = run_bass_kernel_spmd(nc, [given], core_ids=[0])
    return result.results[0]["out"][:N]
```

```python
from contextlib import ExitStack

import concourse.bass as bass
import concourse.mybir as mybir
from concourse.alu_op_type import AluOpType as ALU

F32, BF16, I32 = mybir.dt.float32, mybir.dt.bfloat16, mybir.dt.int32
ACT = mybir.ActivationFunctionType
AXX = mybir.AxisListType.X

P = 128
N, E, D, H = 6250, 106250, 256, 4
C = D // H
NREL = 64
CHUNK, WIN = 1024, 128
U = CHUNK // P
NCH = -(-E // CHUNK)
MAXPASS = NCH + N // WIN
SL = 3
DRAIN = 2
NIT = -(-(MAXPASS + DRAIN) // SL)
NK = 3 + SL * NIT
TILES = 50
ROWS = TILES * P
NB = 10
PAD_DST = N + 200
BIG = 1.0e30
EPS = 1e-5
GW = D + 2 * H
AW = D + 2 * H
XW = D + 1


class Chain:

    def __init__(self, eng, sem):
        self.eng, self.sem, self.n = eng, sem, 0

    def do(self, ins):
        self.n += 1
        ins.then_inc(self.sem, 1)
        self.eng.wait_ge(self.sem, self.n)


class Stage:

    def __init__(self, nc, tag):
        self.nc, self.tag, self.ctx, self.sems = nc, tag, ExitStack(), []

    def sb(self, name, shape, dt=F32):
        return self.ctx.enter_context(self.nc.sbuf_tensor(f"{self.tag}_{name}", shape, dt))

    def ps(self, name, shape, dt=F32):
        return self.ctx.enter_context(self.nc.psum_tensor(f"{self.tag}_{name}", shape, dt))

    def sem(self, name):
        s = self.nc.alloc_semaphore(f"{self.tag}_{name}")
        self.sems.append(s)
        return s

    def close(self):
        self.ctx.close()
        self.nc.clear_and_free_semaphores(self.sems)
        self.nc.all_engine_barrier()


def prime(sp, buffers, sems, n, r):
    for buf, sem in zip(buffers, sems):
        sp.dma_start(buf[0:1, 0:1], r["x_dram"][0:1, 0:1]).then_inc(sem, n)


def top(ap):
    return ap.bitcast(BF16)[:, 1::2]


def bcast(ap, shape):
    return ap.to_broadcast(shape)


def setup_stage(nc, d, r):
    s = Stage(nc, "setup")
    dst_i = s.sb("dst_i", [NCH, CHUNK + 2], I32)
    src_i = s.sb("src_i", [NCH, CHUNK], I32)
    typ_i = s.sb("typ_i", [NCH, CHUNK], I32)
    dst_f = s.sb("dst_f", [NCH, CHUNK + 2])
    src_f = s.sb("src_f", [NCH, CHUNK])
    typ_f = s.sb("typ_f", [NCH, CHUNK])
    isfirst = s.sb("isfirst", [NCH, CHUNK])
    islast = s.sb("islast", [NCH, CHUNK])
    steplast = s.sb("steplast", [NCH, CHUNK])
    chunklast = s.sb("chunklast", [P, NK, U])
    upper = s.sb("upper", [P, NCH])
    ones = s.sb("ones", [P, P])
    krow = s.sb("krow", [P, NK])
    lo = s.sb("lo", [NCH, 1])
    hi = s.sb("hi", [NCH, 1])
    span_i = s.sb("span_i", [NCH, 1], I32)
    npass = s.sb("npass", [NCH, 1])
    cum = s.sb("cum", [NCH, 1])
    cumend = s.sb("cumend", [NCH, 1])
    base = s.sb("base", [NCH, 1])
    pick = s.sb("pick", [NCH, NK])
    pick2 = s.sb("pick2", [NCH, NK])
    nodes = s.sb("nodes", [NCH, NK])
    n0b = s.sb("n0b", [P, NK])
    anyb = s.sb("anyb", [P, NK])
    count = s.sb("count", [P, 1])
    its = s.sb("its", [P, NIT])
    nits = s.sb("nits", [P, 1])
    blocks = [(0, P), (P, NK - P)]
    n0c = [s.sb(f"n0c{b}", [P, 1]) for b in range(2)]
    rowf = [s.sb(f"rowf{b}", [P, CHUNK], BF16) for b in range(2)]
    rowd = [s.sb(f"rowd{b}", [P, CHUNK], BF16) for b in range(2)]
    rowt = [s.sb(f"rowt{b}", [P, CHUNK], BF16) for b in range(2)]
    zeros = s.sb("zeros", [P, 2 * D])
    attb = s.sb("attb", [P, 4, D])
    wtmp = s.sb("wtmp", [P, 2, D])
    qcol = s.sb("qcol", [P, 2])
    qmat = s.sb("qmat", [P, 2, P])
    bqkv = s.sb("bqkv", [P, 3 * D])
    phi = s.sb("phi", [P, 2, D])
    tb = s.sb("tb", [P, D])
    pst = [s.ps(f"pst{i}", [P, 512]) for i in range(4)]
    psn = s.ps("psn", [P, 512])
    psa = s.ps("psa", [P, 512])
    psc = s.ps("psc", [P, 512])
    psq = s.ps("psq", [P, 512])

    edges_in = s.sem("edges_in")
    weights_in = s.sem("weights_in")
    iota_done = s.sem("iota_done")
    dve_step = s.sem("dve_step")
    npass_ready = s.sem("npass_ready")
    cum_done = s.sem("cum_done")
    pick_ready = s.sem("pick_ready")
    n0_done = s.sem("n0_done")
    n0_used = s.sem("n0_used")
    tab_done = s.sem("tab_done")
    tab_used = s.sem("tab_used")
    qmat_ready = s.sem("qmat_ready")
    qbias_done = s.sem("qbias_done")
    qbias_used = s.sem("qbias_used")
    rows_ready = s.sem("rows_ready")
    zeros_ready = s.sem("zeros_ready")
    stored = s.sem("stored")
    NE, NW = 5, 24

    jobs = [("pass", "src", u) for u in range(U)] + [("pass", "dst", u) for u in range(U)]
    jobs += [("pass", "last", u) for u in range(U)] + [("pass", "steplast", u) for u in range(U)] + [("row", n, b, h) for n in ("dst", "first", "typ")
                                                      for b in range(2) for h in range(2)]
    source = {"src": src_f, "dst": dst_f, "last": islast, "steplast": steplast, "first": isfirst, "typ": typ_f}

    with nc.Block() as block:
        @block.sync
        def _(sp):
            flat = d["dst"]
            view = lambda a: flat[a:a + NCH * CHUNK].rearrange("(c e) -> c e", e=CHUNK)
            sp.dma_start(dst_i[:, 1:CHUNK + 1], view(1)).then_inc(edges_in, 16)
            sp.dma_start(dst_i[:, 0:1], view(0)[:, 0:1], allow_slow_non_contiguous=True).then_inc(edges_in, 16)
            sp.dma_start(dst_i[:, CHUNK + 1:CHUNK + 2], view(2)[:, CHUNK - 1:CHUNK],
                         allow_slow_non_contiguous=True).then_inc(edges_in, 16)
            sp.dma_start(src_i[:, :], d["src"]).then_inc(edges_in, 16)
            sp.dma_start(typ_i[:, :], d["typ"]).then_inc(edges_in, 16)

            def weight(dst, src):
                sp.dma_start(dst, src).then_inc(weights_in, 16)

            def halves(w):
                return w.rearrange("(a p) n -> p a n", p=P)

            weight(r["w0"][:, :, 0:D], halves(d["W0"]))
            weight(r["w2"][:, :, 0:D], halves(d["W2"]))
            for i, name in enumerate(("as0", "ad0", "as2", "ad2")):
                weight(attb[:, i, :], bcast(d[name].rearrange("(a h) c -> a (h c)", a=1), [P, D]))
            for i, name in enumerate(("Wk", "Wv", "Wq")):
                weight(r["wkvq"][:, :, i * D:(i + 1) * D], halves(d[name]))
            for i, name in enumerate(("bk", "bv", "bq")):
                weight(bqkv[:, i * D:(i + 1) * D], bcast(d[name].rearrange("(a n) -> a n", a=1), [P, D]))
            weight(r["wo"][:, :, :], halves(d["Wo"]))
            sp.dma_start(qcol[:, :], d["query"].rearrange("(a p) -> p a", p=P),
                         allow_slow_non_contiguous=True).then_inc(weights_in, 16)
            weight(r["relw"][:, 0, :], d["rel"])
            for name in ("b0", "b2", "bo", "gamma", "beta"):
                weight(r[name][:, :], bcast(d[name].rearrange("(a n) -> a n", a=1), [P, D]))
            weight(r["w3"][:, :, D:2 * D], halves(d["thetaT"]))
            weight(phi[:, :, :], halves(d["phiT"]))
            weight(r["b3"][:, D:2 * D], bcast(d["theta_b"].rearrange("(a n) -> a n", a=1), [P, D]))
            weight(tb[:, :], bcast(d["phi_b"].rearrange("(a n) -> a n", a=1), [P, D]))
            sp.wait_ge(zeros_ready, 1)
            n = 0
            for acc, w in (("agg", AW), ("aggx", XW)):
                for a in range(N, ROWS, P):
                    m = min(P, ROWS - a)
                    sp.dma_start(d[acc][a:a + m, :], zeros[0:m, 0:w]).then_inc(stored, 16)
                    n += 1
            sp.wait_ge(rows_ready, 1)
            for b, (k0, m) in enumerate(blocks):
                for t, dr in ((rowd, "dstrow"), (rowf, "firstrow"), (rowt, "typrow")):
                    sp.dma_start(d[dr][k0:k0 + m, :], t[b][0:m, :]).then_inc(stored, 16)
                    n += 1
                for h in range(H):
                    rows = d["firstrow4"][k0:k0 + m, :].rearrange("k (u h e) -> k u h e", h=H, e=P)
                    sp.dma_start(rows[:, :, h, :], rowf[b][0:m, :].rearrange("k (u e) -> k u e", e=P)).then_inc(stored, 16)
                    n += 1
            sp.wait_ge(stored, 16 * n)

        @block.gpsimd
        def _(pool):
            nc.gpsimd.iota(r["iota_i"][:, 0:P], [[1, P]], base=0, channel_multiplier=0).then_inc(iota_done, 1)
            nc.gpsimd.iota(r["iota_i"][:, P:P + NK], [[1, NK]], base=-1, channel_multiplier=0).then_inc(iota_done, 1)
            nc.gpsimd.iota(r["iota_i"][:, P + NK:P + NK + 1], [[1, 1]], base=0, channel_multiplier=1).then_inc(iota_done, 1)

        @block.vector
        def _(dve):
            v = nc.vector
            c = Chain(dve, dve_step)
            dve.wait_ge(iota_done, 3)
            c.do(v.tensor_copy(r["iota_row"][:, :], r["iota_i"][:, 0:P]))
            c.do(v.tensor_copy(krow[:, :], r["iota_i"][:, P:P + NK]))
            c.do(v.tensor_copy(r["iota_col"][:, :], r["iota_i"][:, P + NK:P + NK + 1]))
            c.do(v.tensor_scalar(r["ident"][:, :], r["iota_row"][:, :], r["iota_col"][:, 0:1], None, ALU.is_equal))
            c.do(v.tensor_scalar(upper[:, :], r["iota_row"][:, 0:NCH], r["iota_col"][:, 0:1], None, ALU.is_gt))
            c.do(v.memset(ones[:, :], 1.0))
            v.memset(zeros[:, :], 0.0).then_inc(zeros_ready, 1)
            dve.wait_ge(edges_in, 16 * NE)
            c.do(v.tensor_copy(dst_f[:, :], dst_i[:, :]))
            c.do(v.tensor_copy(src_f[:, :], src_i[:, :]))
            c.do(v.tensor_copy(typ_f[:, :], typ_i[:, :]))
            c.do(v.tensor_scalar(lo[:, :], r["iota_col"][0:NCH, 0:1], 0.0, None, ALU.is_gt))
            c.do(v.tensor_tensor(lo[:, :], lo[:, :], dst_f[:, 1:2], ALU.mult))
            c.do(v.tensor_scalar(hi[:, :], dst_f[:, CHUNK + 1:CHUNK + 2], float(N), None, ALU.min))
            c.do(v.tensor_tensor(span_i[:, :], hi[:, :], lo[:, :], ALU.subtract))
            c.do(v.tensor_scalar(span_i[:, :], span_i[:, :], WIN.bit_length() - 1, None, ALU.arith_shift_right))
            c.do(v.tensor_copy(npass[:, :], span_i[:, :]))
            v.tensor_scalar(npass[:, :], npass[:, :], 1.0, None, ALU.add).then_inc(npass_ready, 1)
            c.do(v.tensor_tensor(isfirst[:, :], dst_f[:, 1:CHUNK + 1], dst_f[:, 0:CHUNK], ALU.not_equal))
            c.do(v.tensor_tensor(islast[:, :], dst_f[:, 1:CHUNK + 1], dst_f[:, 2:CHUNK + 2], ALU.not_equal))
            c.do(v.memset(islast[:, CHUNK - 1:CHUNK], 1.0))
            c.do(v.tensor_copy(steplast[:, :], islast[:, :]))
            c.do(v.memset(steplast[:, P - 1:CHUNK:P], 1.0))
            dve.wait_ge(cum_done, 1)
            c.do(v.tensor_copy(cum[:, :], psn[0:NCH, 0:1]))
            dve.wait_ge(npass_ready, 1)
            c.do(v.tensor_tensor(cumend[:, :], cum[:, :], npass[:, :], ALU.add))
            c.do(v.tensor_scalar(pick[:, :], krow[0:NCH, :], cum[:, 0:1], None, ALU.is_ge))
            c.do(v.tensor_scalar(pick2[:, :], krow[0:NCH, :], cumend[:, 0:1], None, ALU.is_lt))
            c.do(v.tensor_tensor(pick[:, :], pick[:, :], pick2[:, :], ALU.mult))
            c.do(v.scalar_tensor_tensor(base[:, :], cum[:, :], float(-WIN), lo[:, :], ALU.mult, ALU.add))
            c.do(v.tensor_scalar(nodes[:, :], krow[0:NCH, :], float(WIN), base[:, 0:1], ALU.mult, ALU.add))
            v.tensor_tensor(nodes[:, :], nodes[:, :], pick[:, :], ALU.mult).then_inc(pick_ready, 1)
            dve.wait_ge(n0_done, 1)
            c.do(v.tensor_copy(anyb[:, :], psa[:, 0:NK]))
            c.do(v.scalar_tensor_tensor(n0b[:, :], anyb[:, :], float(-N), psn[:, 16:16 + NK], ALU.mult, ALU.add))
            c.do(v.tensor_scalar(n0b[:, :], n0b[:, :], float(N), None, ALU.add))
            c.do(v.memset(r["n0_i"][:, 0:2], N))
            c.do(v.tensor_copy(r["n0_i"][:, 2:2 + NK], n0b[0:1, :]))
            c.do(v.memset(r["delta"][:, 0:1], -1.0))
            c.do(v.tensor_tensor(r["delta"][:, 1:NK], n0b[:, 1:NK], n0b[:, 0:NK - 1], ALU.subtract))
            c.do(v.tensor_scalar(r["rowneg"][:, :], r["delta"][:, :], 0.0, None, ALU.is_ge))
            c.do(v.scalar_tensor_tensor(r["rowneg"][:, :], r["delta"][:, :], float(WIN), r["rowneg"][:, :],
                                        ALU.is_lt, ALU.mult))
            c.do(v.tensor_scalar(r["rowneg"][:, :], r["rowneg"][:, :], r["ident"][:, 0:1], None, ALU.mult))
            c.do(v.tensor_scalar(r["rowneg"][:, :], r["rowneg"][:, :], -1.0, BIG, ALU.add, ALU.mult))
            c.do(v.reduce_sum(count[:, :], anyb[:, :], axis=AXX))
            c.do(v.tensor_scalar(its[:, :], r["iota_row"][:, 0:NIT], float(SL), None, ALU.mult))
            c.do(v.tensor_scalar(its[:, :], its[:, :], -(DRAIN - 1.0), count[:, 0:1], ALU.add, ALU.is_le))
            c.do(v.reduce_sum(nits[:, :], its[:, :], axis=AXX))
            c.do(v.tensor_copy(r["nits_i"][:, :], nits[0:1, :]))
            for b, (k0, m) in enumerate(blocks):
                c.do(v.tensor_scalar(n0c[b][0:m, :], psc[0:m, 2 * b:2 * b + 1], float(-N), None, ALU.mult))
                c.do(v.scalar_tensor_tensor(n0c[b][0:m, :], psc[0:m, 2 * b + 1:2 * b + 2], 1.0, n0c[b][0:m, :],
                                            ALU.mult, ALU.add))
                c.do(v.tensor_scalar(n0c[b][0:m, :], n0c[b][0:m, :], float(N), None, ALU.add))
            for i, job in enumerate(jobs):
                ps = pst[i % 4]
                dve.wait_ge(tab_done, i + 1)
                if job[0] == "pass":
                    _, name, u = job
                    if name == "dst":
                        ins = v.tensor_tensor(r["dstloc"][:, :, u], ps[:, 0:NK], n0b[:, :], ALU.subtract)
                    else:
                        out = {"src": r["src_pass"], "last": chunklast, "steplast": r["islast"]}[name]
                        ins = v.tensor_copy(out[:, :, u], ps[:, 0:NK])
                else:
                    _, name, b, h = job
                    m, cols = blocks[b][1], slice(h * 512, (h + 1) * 512)
                    if name == "dst":
                        ins = v.tensor_scalar(rowd[b][0:m, cols], ps[0:m, :], n0c[b][0:m, 0:1], None, ALU.subtract)
                    elif name == "first":
                        ins = v.tensor_scalar(rowf[b][0:m, cols], ps[0:m, :], -BIG, None, ALU.mult)
                    else:
                        ins = v.tensor_copy(rowt[b][0:m, cols], ps[0:m, :])
                ins.then_inc(tab_used, 1)
            dve.wait_ge(tab_used, len(jobs))
            c.do(v.tensor_scalar(r["lastloc"][:, :, :], r["dstloc"][:, :, :], 1.0, None, ALU.add))
            c.do(v.tensor_tensor(r["lastloc"][:, :, :], r["lastloc"][:, :, :], chunklast[:, :, :], ALU.mult))
            c.do(v.tensor_scalar(r["lastloc"][:, :, :], r["lastloc"][:, :, :], -1.0, None, ALU.add))
            v.memset(wtmp[:, :, :], 0.0).then_inc(rows_ready, 1)
            dve.wait_ge(rows_ready, 1)
            dve.wait_ge(weights_in, 16 * NW)
            for w, i0 in (("w0", 0), ("w2", 2)):
                for i in range(2):
                    c.do(v.tensor_tensor(wtmp[:, :, :], r[w][:, :, 0:D],
                                         bcast(attb[:, i0 + i, :].unsqueeze(1), [P, 2, D]), ALU.mult))
                    c.do(v.reduce_sum(r[w][:, :, D + H * i:D + H * (i + 1)],
                                      wtmp[:, :, :].rearrange("p a (h c) -> p a h c", c=C), axis=AXX))
            c.do(v.tensor_scalar(r["wkvq"][:, :, 2 * D:3 * D], r["wkvq"][:, :, 2 * D:3 * D], C ** -0.5, None, ALU.mult))
            c.do(v.tensor_scalar(bqkv[:, 2 * D:3 * D], bqkv[:, 2 * D:3 * D], C ** -0.5, None, ALU.mult))
            c.do(v.tensor_scalar(r["relw"][:, 0, :], r["relw"][:, 0, :], 0.2, None, ALU.mult))
            for i in range(2):
                c.do(v.tensor_tensor(r["relw"][:, i + 1, :], r["relw"][:, i, :], top(r["relw"][:, i, :]), ALU.subtract))
            c.do(v.tensor_tensor(r["w3"][:, :, 0:D], phi[:, :, :], r["w3"][:, :, D:2 * D], ALU.subtract))
            c.do(v.memset(r["b3"][:, 0:D], 0.0))
            c.do(v.tensor_tensor(r["b3"][:, D:2 * D], r["b3"][:, D:2 * D], tb[:, :], ALU.add))
            c.do(v.tensor_scalar(qcol[:, :], qcol[:, :], 0.1, None, ALU.mult))
            v.tensor_copy(qmat[:, :, :], bcast(qcol[:, :].unsqueeze(2), [P, 2, P])).then_inc(qmat_ready, 1)
            for i in range(3):
                dve.wait_ge(qbias_done, i + 1)
                v.tensor_tensor(r["b1"][:, i * D:(i + 1) * D], psq[:, 0:D], bqkv[:, i * D:(i + 1) * D],
                                ALU.add).then_inc(qbias_used, 1)
            c.do(v.memset(r["mean"][:, :], 0.0))
            c.do(v.memset(r["rstd"][:, :], 1.0))

        @block.tensor
        def _(pe):
            t = nc.tensor
            pe.wait_ge(npass_ready, 1)
            t.matmul(psn[0:NCH, 0:1], upper[0:NCH, :], npass[:, :], start=True, stop=True).then_inc(cum_done, 1)
            pe.wait_ge(pick_ready, 1)
            t.matmul(psa[:, 0:NK], ones[0:NCH, :], pick[:, :], start=True, stop=True)
            for b, (k0, m) in enumerate(blocks):
                t.matmul(psc[0:m, 2 * b:2 * b + 1], pick[:, k0:k0 + m], ones[0:NCH, 0:1], start=True, stop=True)
                t.matmul(psc[0:m, 2 * b + 1:2 * b + 2], nodes[:, k0:k0 + m], ones[0:NCH, 0:1], start=True, stop=True)
            t.matmul(psn[:, 16:16 + NK], ones[0:NCH, :], nodes[:, :], start=True, stop=True).then_inc(n0_done, 1)
            for i, job in enumerate(jobs):
                ps = pst[i % 4]
                if i >= 4:
                    pe.wait_ge(tab_used, i - 3)
                if job[0] == "pass":
                    _, name, u = job
                    x = source[name]
                    o = 1 if name == "dst" else 0
                    ins = t.matmul(ps[:, 0:NK], x[:, o + u * P:o + (u + 1) * P], pick[:, :], start=True, stop=True)
                else:
                    _, name, b, h = job
                    k0, m = blocks[b]
                    o = (1 if name == "dst" else 0) + h * 512
                    ins = t.matmul(ps[0:m, :], pick[:, k0:k0 + m], source[name][:, o:o + 512], start=True, stop=True)
                ins.then_inc(tab_done, 1)
            pe.wait_ge(qmat_ready, 1)
            for i in range(3):
                if i:
                    pe.wait_ge(qbias_used, i)
                w = r["wkvq"][:, :, i * D:(i + 1) * D]
                t.matmul(psq[:, 0:D], qmat[:, 0, :], w[:, 0, :], start=True, stop=False)
                t.matmul(psq[:, 0:D], qmat[:, 1, :], w[:, 1, :], start=False, stop=True).then_inc(qbias_done, 1)
    s.close()


def project_stage(nc, d, r, y, tag, weights, bias, cols, stores):
    s = Stage(nc, tag)
    B = 10
    USES = B // NB
    xn = [s.sb(f"xn{b}", [P, D]) for b in range(NB)]
    xT = [s.sb(f"xT{b}", [P, D]) for b in range(NB)]
    ob = [s.sb(f"ob{b}", [P, cols]) for b in range(NB)]
    psT = [s.ps(f"psT{b}", [P, 512]) for b in range(2)]
    psO = [s.ps(f"psO{b}", [P, -(-cols // 512) * 512]) for b in range(2)]
    pieces = [(a, min(a + 512, cols)) for a in range(0, cols, 512)]
    ready = s.sem("ready")
    norm_done = s.sem("norm_done")
    kept = [s.sem(f"kept{b}") for b in range(NB)]
    transposed, xT_ready = s.sem("transposed"), s.sem("xT_ready")
    product_done, row_ready = s.sem("product_done"), s.sem("row_ready")
    stored = [s.sem(f"stored{b}") for b in range(NB)]
    at = lambda t: t + 1 + NB
    stored_before = lambda i, b: i * USES + b // NB + 1
    NST = 16 * len(stores)

    with nc.Block() as block:
        @block.gpsimd
        def _(pool):
            for x in (norm_done, transposed, xT_ready, product_done, row_ready):
                pool.sem_inc(x, NB)
            pool.sem_inc(ready, 1)

        @block.vector
        def _(dve):
            v = nc.vector
            dve.wait_ge(ready, 1)

            def normalize(i, b):
                t = i * B + b
                dve.wait_ge(transposed, at(t - NB))
                dve.wait_ge(kept[b % NB], 16 * stored_before(i, b))
                v.tensor_scalar(xn[b % NB][:, :], y[:, bass.ds(t * D, D)], r["mean"][:, bass.ds(t, 1)],
                                r["rstd"][:, bass.ds(t, 1)], ALU.subtract, ALU.mult).then_inc(norm_done, 1)

            def finish(i, b):
                dve.wait_ge(product_done, at(i * B + b))
                dve.wait_ge(stored[b % NB], NST * stored_before(i, b))
                if bias is None:
                    ins = v.tensor_copy(ob[b % NB][:, :], psO[b % 2][:, 0:cols])
                else:
                    ins = v.tensor_tensor(ob[b % NB][:, :], psO[b % 2][:, 0:cols], bias, ALU.add)
                ins.then_inc(row_ready, 1)

            with dve.Fori(0, TILES // B) as i:
                for b in range(3):
                    normalize(i, b)
                for b in range(B):
                    if b + 3 < B:
                        normalize(i, b + 3)
                    finish(i, b)

        @block.tensor
        def _(pe):
            pe.wait_ge(ready, 1)

            def turn(t, b):
                x = xn[b % NB]
                pe.wait_ge(xT_ready, at(t - 2))
                pe.wait_ge(norm_done, at(t))
                nc.tensor.transpose(psT[b % 2][:, 0:P], x[:, 0:P], r["ident"][:, :])
                nc.tensor.transpose(psT[b % 2][:, P:D], x[:, P:D], r["ident"][:, :]).then_inc(transposed, 1)

            def multiply(t, b):
                x, o = xT[b % NB], psO[b % 2]
                pe.wait_ge(row_ready, at(t - 2))
                pe.wait_ge(xT_ready, at(t))
                for a, e in pieces:
                    nc.tensor.matmul(o[:, a:e], x[:, 0:P], weights[:, 0, a:e], start=True, stop=False)
                    ins = nc.tensor.matmul(o[:, a:e], x[:, P:D], weights[:, 1, a:e], start=False, stop=True)
                ins.then_inc(product_done, 1)

            with pe.Fori(0, TILES // B) as i:
                turn(i * B, 0)
                for b in range(B):
                    if b + 1 < B:
                        turn(i * B + b + 1, b + 1)
                    multiply(i * B + b, b)

        @block.scalar
        def _(act):
            act.wait_ge(ready, 1)
            with act.Fori(0, TILES // B) as i:
                for b in range(B):
                    t = i * B + b
                    act.wait_ge(product_done, at(t - NB))
                    act.wait_ge(transposed, at(t))
                    nc.scalar.copy(xT[b % NB][:, :], psT[b % 2][:, 0:D]).then_inc(xT_ready, 1)

        @block.sync
        def _(sp):
            prime(sp, ob, stored, NST, r)
            prime(sp, xn, kept, 16, r)
            sp.wait_ge(ready, 1)

            def keep(t, b):
                sp.wait_ge(norm_done, at(t))
                sp.dma_start(d["x"][bass.ds(t * P, P), :], xn[b % NB][:, :]).then_inc(kept[b % NB], 16)

            with sp.Fori(0, TILES // B) as i:
                for b in range(2):
                    keep(i * B + b, b)
                for b in range(B):
                    t = i * B + b
                    if b + 2 < B:
                        keep(t + 2, b + 2)
                    sp.wait_ge(row_ready, at(t))
                    for a, e, dram in stores:
                        sp.dma_start(dram[bass.ds(t * P, P), :], ob[b % NB][:, a:e]).then_inc(stored[b % NB], 16)
            for b in range(NB):
                sp.wait_ge(stored[b], NST * (1 + TILES // NB))
                sp.wait_ge(kept[b], 16 * (1 + TILES // NB))
    s.close()


def edge_stage(nc, d, r, tag, relational):
    s = Stage(nc, tag)
    V0 = D if relational else 0
    AU = 6 if relational else 0
    tab, gw = (d["kv"], 2 * D) if relational else (d["h"], GW)
    wtab = d["q"] if relational else d["h"][:, D + H:GW]
    WC = D if relational else H
    M3 = 3 * H
    idx = [s.sb(f"idx{j}", [P, U], I32) for j in range(SL)]
    G = [s.sb(f"G{j}", [P, U, gw]) for j in range(SL)]
    dstrow = [s.sb(f"dstrow{j}", [P, CHUNK], BF16) for j in range(SL)]
    firstrow = [s.sb(f"firstrow{j}", [U * H, P], BF16) for j in range(SL)]
    window = [s.sb(f"window{j}", [P, WC]) for j in range(SL)]
    onehot = [s.sb(f"onehot{j}", [P, U, P]) for j in range(SL)]
    onehotT = [s.sb(f"onehotT{j}", [P, CHUNK], F32 if relational else BF16) for j in range(SL)]
    ph = [s.sb(f"ph{j}", [P, U, D + H]) for j in range(SL)]
    outw = [s.sb(f"outw{j}", [P, AW]) for j in range(SL)]
    shift = [s.sb(f"shift{j}", [P, P]) for j in range(SL)]
    m3 = [s.sb(f"m3_{j}", [P, M3]) for j in range(SL)]
    gex = [s.sb(f"gex{j}", [P, H]) for j in range(SL)]
    scanned = s.sb("scanned", [U * H, P])
    score = [s.sb(f"score{j}", [P, U, H]) for j in range(SL)]
    last3 = s.sb("last3", [P, U, M3 + 1])
    stepmax = s.sb("stepmax", [P, U, H])
    absent = s.sb("absent", [P, U])
    winmax = s.sb("winmax", [P, H])
    refmax = s.sb("refmax", [P, U, H])
    gin = s.sb("gin", [P, H])
    carried = s.sb("carried", [P, D + H])
    psO = [s.ps(f"psO{j}", [P, 512]) for j in range(SL)]
    psC = s.ps("psC", [P, 512])
    psS = s.ps("psS", [P, 512])
    psM = [psO[j][:, D + H:D + H + U * (M3 + 1)] for j in range(SL)]
    psR = [psO[j][:, 512 - U * M3:512] for j in range(SL)]
    psCm, psF, psT = psC[:, D + H:D + 2 * H], psS[:, 0:U * H], psS[0:U * H, P:2 * P]
    parts = lambda ap, w: ap.rearrange("p (u w) -> p u w", w=w)[:, :, 0:M3].rearrange("p u (a h) -> p u h a", h=H)
    flat = lambda ap: ap.rearrange("p u h -> p (u h)")
    by_head = lambda ap: ap.rearrange("p u (h c) -> p u h c", c=C)
    if relational:
        typrow = [s.sb(f"typrow{j}", [NREL, CHUNK], BF16) for j in range(SL)]
        typeT = s.sb("typeT", [NREL, CHUNK], BF16)
        modk = s.sb("modk", [P, U, D])
        psRel = s.ps("psRel", [P, 512])
        psQ = [s.ps(f"psQ{i}", [P, 512]) for i in range(2)]
    else:
        psA = s.ps("psA", [P, U * M3])
        w3 = s.sb("w3", [P, M3])
        ssum = s.sb("ssum", [P, U, H])

    ready = s.sem("ready")
    gathered = [[nc.alloc_semaphore(f"{tag}_gathered{j}_{u}") for u in range(U)] for j in range(SL)]
    dstrow_in = [s.sem(f"dstrow_in{j}") for j in range(SL)]
    firstrow_in = [s.sem(f"firstrow_in{j}") for j in range(SL)]
    window_in = [s.sem(f"window_in{j}") for j in range(SL)]
    out_stored = [s.sem(f"out_stored{j}") for j in range(SL)]
    first_pass = {n: 1 for n in (
        "score_ready", "scoreT_done", "scan_done", "scanback_done", "last_top", "last_mid", "last3_ready",
        "presence_ready", "nodemax_done", "stepsum", "absent_ready", "stepmax_ready", "winmax_ready", "carrym_done",
        "m_ready", "m_mid", "m3_ready", "refmax_done", "refsum", "expin_ready", "prob_ready", "gdiff", "gin_ready",
        "rescale_ready", "kept_max", "onehot_ready", "onehotT_ready", "shift_ready")}
    first_pass.update({n: 0 for n in ("weighted", "aggregated")})
    if AU:
        first_pass["weighted_act"] = 0
    first_pass.update({n: -1 for n in ("carry_done", "carried_ready", "out_ready")})
    if relational:
        first_pass.update({n: 1 for n in ("typeT_ready", "rel_done", "modk_ready")})
        typrow_in = [s.sem(f"typrow_in{j}") for j in range(SL)]
        q_done, q_used = s.sem("q_done"), s.sem("q_used")
    else:
        first_pass.update({n: 1 for n in ("w_mid", "w3_ready", "adst_done", "summed", "added")})
    q = {n: s.sem(n) for n in first_pass}
    idx_ready = s.sem("idx_ready")
    buffers_zero, all_stored = s.sem("buffers_zero"), s.sem("all_stored")
    store_due = s.sem("store_due")
    NQ = U // 2
    at = lambda k: k + SL

    def build_onehot(k, sl):
        loc = r["dstloc"][:, rowi(k), :].rearrange("p a u -> p (a u)").unsqueeze(2)
        nc.vector.tensor_tensor(onehot[sl][:, :, :], bcast(loc, [P, U, P]),
                        bcast(r["iota_row"][:, :].unsqueeze(1), [P, U, P]), ALU.is_equal).then_inc(
                            q["onehot_ready"], 1)

    def passes(eng, body):
        nit = eng.value_load(r["nits_i"][0:1, 0:1], min_val=1, max_val=NIT)
        with eng.Fori(0, NIT) as i:
            with eng.If(i < nit):
                for j in range(SL):
                    body(i, SL * i + j + 1, (j + 1) % SL, j)
        return nit

    loaded = lambda i, j: 16 * (i + 1 + j // SL)
    rowi = lambda k: bass.ds(k, 1)

    with nc.Block() as block:
        @block.gpsimd
        def _(pool):
            for n, x in q.items():
                pool.sem_inc(x, SL + first_pass[n] - 1)
            if relational:
                pool.sem_inc(q_used, SL * NQ)
                pool.sem_inc(q_done, SL * NQ)
            pool.sem_inc(ready, 1)

            def gather(k, sl):
                if AU:
                    pool.wait_ge(ready, 1)
                    pool.wait_ge(q["weighted_act"], at(k - SL))
                pool.wait_ge(ready, 1)
                pool.wait_ge(q["weighted"], at(k - SL))
                nc.gpsimd.tensor_copy(idx[sl][:, :], r["src_pass"][:, rowi(k), :].rearrange(
                    "p a u -> p (a u)")).then_inc(idx_ready, 1)
                pool.wait_ge(ready, 1)
                pool.wait_ge(idx_ready, at(k - SL))
                for u in range(U):
                    nc.gpsimd.indirect_dma_start(
                        G[sl][:, u, :], None, tab,
                        bass.IndirectOffsetOnAxis(ap=idx[sl][:, u:u + 1], axis=0)).then_inc(gathered[sl][u], 16)

            pool.wait_ge(buffers_zero, 1)
            gather(1, 1)
            passes(pool, lambda i, k, sl, j: gather(k + 1, (sl + 1) % SL))

        @block.sync
        def _(sp):
            prime(sp, outw, out_stored, 16, r)

            def load(k, sl):
                sp.dma_start(dstrow[sl][:, :], bcast(d["dstrow"][rowi(k), :], [P, CHUNK])).then_inc(dstrow_in[sl], 16)
                sp.dma_start(firstrow[sl][:, :], d["firstrow4"][rowi(k), :].rearrange(
                    "k (r e) -> (k r) e", e=P)).then_inc(firstrow_in[sl], 16)
                n0 = sp.value_load(r["n0_i"][0:1, bass.ds(k + 2, 1)], min_val=0, max_val=N)
                sp.dma_start(window[sl][:, :], wtab[bass.ds(n0, P), :]).then_inc(window_in[sl], 16)
                if relational:
                    sp.dma_start(typrow[sl][:, :], bcast(d["typrow"][rowi(k), :], [NREL, CHUNK])).then_inc(
                        typrow_in[sl], 16)

            def store(k, sl, before):
                n0 = sp.value_load(r["n0_i"][0:1, bass.ds(k + 2, 1)], min_val=0, max_val=N)
                sp.wait_ge(out_stored[(sl - 1) % SL], before)
                sp.sem_inc(store_due, 1)
                sp.wait_ge(q["kept_max"], at(k))
                sp.wait_ge(q["out_ready"], at(k))
                sp.sem_inc(store_due, 1)
                sp.dma_start(d["agg"][bass.ds(n0, P), :], outw[sl][:, :]).then_inc(out_stored[sl], 16)

            load(1, 1)
            load(2, 2)
            sp.wait_ge(ready, 1)
            sp.wait_ge(buffers_zero, 1)

            def body(i, k, sl, j):
                if relational:
                    sp.wait_ge(q_done, NQ * at(k - 1))
                sp.wait_ge(q["onehotT_ready"], at(k - 1))
                sp.wait_ge(q["scan_done"], at(k - 1))
                sp.wait_ge(q["typeT_ready" if relational else "w3_ready"], at(k - 1))
                load(k + 2, (sl + 2) % SL)
                store(k - 3, sl, 16 * (i + (2 if j else 1)))
            nit = passes(sp, body)
            sp.wait_ge(ready, 1)
            store(nit * SL - 2, (SL - 2) % SL, 16 * (nit + 1))
            seen, seen2 = sp.snap(16 * (nit + 1)), sp.snap(16 * (nit + 2))
            sp.wait_ge(ready, 1)
            for j in range(SL):
                sp.wait_ge(out_stored[j], seen2 if j == 1 else seen)
            for x in [dstrow_in, firstrow_in, window_in] + ([typrow_in] if relational else []):
                sp.wait_ge(x[1], seen)
                sp.wait_ge(x[2], seen)
            sp.sem_inc(all_stored, 1)

        @block.vector
        def _(dve):
            v = nc.vector

            def ahead(k, sl, at_k, in_now):
                dve.wait_ge(q["refmax_done"], at_k - SL)
                if relational:
                    dve.wait_ge(q_done, NQ * (at_k - SL))
                dve.wait_ge(dstrow_in[sl], in_now)
                v.tensor_scalar(onehotT[sl][:, :], dstrow[sl][:, :], r["iota_col"][:, 0:1], None,
                                ALU.is_equal).then_inc(q["onehotT_ready"], 1)
                if relational:
                    dve.wait_ge(q["rel_done"], at_k - 1)
                    dve.wait_ge(typrow_in[sl], in_now)
                    v.tensor_scalar(typeT[:, :], typrow[sl][:, :], r["iota_col"][0:NREL, 0:1], None,
                                    ALU.is_equal).then_inc(q["typeT_ready"], 1)

            def adst_top(sl, at_k, in_now):
                dve.wait_ge(q["adst_done"], at_k - 1)
                dve.wait_ge(window_in[sl], in_now)
                v.tensor_scalar(w3[:, 0:H], window[sl][:, :], 1.0, None, ALU.mult).then_inc(q["w_mid"], 1)

            def adst_mid(sl, at_k):
                dve.wait_ge(q["w_mid"], 2 * at_k - SL - 1)
                v.tensor_tensor(w3[:, H:2 * H], w3[:, 0:H], top(w3[:, 0:H]), ALU.subtract).then_inc(q["w_mid"], 1)

            def adst_low(sl, at_k):
                dve.wait_ge(q["w_mid"], 2 * at_k - SL)
                v.tensor_tensor(w3[:, 2 * H:M3], w3[:, H:2 * H], top(w3[:, H:2 * H]), ALU.subtract).then_inc(
                    q["w3_ready"], 1)

            def build_shift(k, sl, at_k):
                dve.wait_ge(q["carry_done"], at_k - SL)
                dve.wait_ge(q["carrym_done"], at_k - SL)
                v.tensor_scalar(shift[sl][:, 0:1], r["iota_col"][:, 0:1], r["delta"][:, rowi(k)], None,
                                ALU.is_equal).then_inc(q["shift_ready"], 1)

            def add_relation(k, sl, in_now):
                for u in range(U):
                    dve.wait_ge(gathered[sl][u], in_now)
                dve.wait_ge(q["score_ready"], at(k - 1))
                dve.wait_ge(q["rel_done"], at(k))
                v.tensor_tensor(by_head(modk[:, :, :]), by_head(G[sl][:, :, 0:D]),
                                bcast(psRel[:, :].rearrange("p (u c) -> p u c", c=C).unsqueeze(2), [P, U, H, C]),
                                ALU.add).then_inc(q["modk_ready"], 1)

            def times_queries(k, ns):
                dve.wait_ge(q["modk_ready"], at(k))
                for n in ns:
                    dve.wait_ge(q_done, NQ * at(k - 1) + n + 1)
                    m = modk[:, 2 * n:2 * n + 2, :].rearrange("p u n -> p (u n)")
                    v.tensor_tensor(m, m, psQ[n % 2][:, :], ALU.mult).then_inc(q_used, 1)

            def sum_products(k, sl):
                dve.wait_ge(q_used, NQ * at(k))
                dve.wait_ge(q["expin_ready"], at(k - SL))
                dve.wait_ge(q["scoreT_done"], at(k - SL))
                v.reduce_sum(flat(score[sl][:, :, :]), modk[:, :, :].rearrange("p u (h c) -> p (u h) c", c=C),
                             axis=AXX).then_inc(q["score_ready"], 1)

            def sum_parts(k):
                dve.wait_ge(q["score_ready"], at(k - 1))
                dve.wait_ge(q["adst_done"], at(k))
                v.reduce_sum(ssum[:, :, :], parts(psA[:, :], M3), axis=AXX).then_inc(q["summed"], 1)

            def add_source(k, sl, in_now):
                for u in range(U):
                    dve.wait_ge(gathered[sl][u], in_now)
                dve.wait_ge(q["summed"], at(k))
                v.tensor_tensor(ssum[:, :, :], G[sl][:, :, D:D + H], ssum[:, :, :], ALU.add).then_inc(q["added"], 1)

            def leaky(k, sl):
                dve.wait_ge(q["added"], at(k))
                dve.wait_ge(q["expin_ready"], at(k - SL))
                dve.wait_ge(q["scoreT_done"], at(k - SL))
                v.scalar_tensor_tensor(score[sl][:, :, :], ssum[:, :, :], 0.2, ssum[:, :, :], ALU.mult,
                                       ALU.max).then_inc(q["score_ready"], 1)

            for j in range(SL):
                dve.wait_ge(out_stored[j], 16)
                v.memset(outw[j][:, :], 0.0)
                v.memset(gex[j][:, :], 1.0)
                v.memset(shift[j][:, :], 0.0)
            v.memset(psO[SL - 1][:, :], 0.0)
            v.memset(m3[0][:, :], 0.0)
            v.memset(G[0][:, :, :], 0.0)
            v.memset(ph[0][:, :, :], 0.0)
            v.memset(onehot[0][:, :, :], 0.0).then_inc(buffers_zero, 1)
            dve.wait_ge(buffers_zero, 1)
            dve.wait_ge(ready, 1)
            build_onehot(1, 1)
            build_shift(1, 1, at(1))
            for k in (1, 2):
                ahead(k, k, at(k), 16)
                if not relational:
                    adst_top(k, at(k), 16)
                    adst_mid(k, at(k))
                    adst_low(k, at(k))
            if relational:
                add_relation(1, 1, 16)
                times_queries(1, range(NQ))
                sum_products(1, 1)
            else:
                sum_parts(1)
                add_source(1, 1, 16)
                leaky(1, 1)

            def body(i, k, sl, j):
                pv, nx, p2 = (sl - 1) % SL, (sl + 1) % SL, (sl - 2) % SL
                far, now_far, now_next = at(k + 2), loaded(i, j + 2), loaded(i, j + 1)
                def scan():
                    dve.wait_ge(firstrow_in[sl], loaded(i, j))
                    dve.wait_ge(q["scanback_done"], at(k - 1))
                    dve.wait_ge(q["scoreT_done"], at(k))
                    v.tensor_tensor_scan(scanned[:, :], firstrow[sl][:, :], psT, -BIG, ALU.add, ALU.max).then_inc(
                        q["scan_done"], 1)

                def weigh():
                    dve.wait_ge(q["prob_ready"], at(k - 1))
                    v.tensor_tensor(by_head(ph[pv][:, 0:U - AU, 0:D]), by_head(G[pv][:, 0:U - AU, V0:V0 + D]),
                                    bcast(ph[pv][:, 0:U - AU, D:D + H].unsqueeze(3), [P, U - AU, H, C]), ALU.mult).then_inc(
                                        q["weighted"], 1)

                if relational:
                    weigh()
                    scan()
                else:
                    scan()
                    weigh()
                dve.wait_ge(q["nodemax_done"], at(k - 1))
                dve.wait_ge(q["scanback_done"], at(k))
                v.tensor_tensor(last3[:, :, 0:H], psF.rearrange("p (u h) -> p u h", h=H),
                                bcast(r["islast"][:, rowi(k), :].rearrange("p a u -> p (a u)").unsqueeze(2), [P, U, H]),
                                ALU.mult).then_inc(q["last_top"], 1)
                dve.wait_ge(q["rescale_ready"], at(k - 2))
                dve.wait_ge(q["carrym_done"], at(k))
                dve.wait_ge(q["carry_done"], at(k - 2))
                v.tensor_tensor(carried[:, 0:D].rearrange("p (h c) -> p h c", c=C),
                                psC[:, 0:D].rearrange("p (h c) -> p h c", c=C),
                                bcast(gex[p2][:, :].unsqueeze(2), [P, H, C]), ALU.mult)
                v.tensor_tensor(carried[:, D:D + H], psC[:, D:D + H], gex[p2][:, :], ALU.mult).then_inc(
                    q["carried_ready"], 1)
                dve.wait_ge(q["last_top"], at(k))
                top3 = last3[:, :, :].bitcast(BF16)
                v.tensor_tensor(last3[:, :, H:2 * H], last3[:, :, 0:H], top3[:, :, 1:2 * H:2], ALU.subtract).then_inc(
                    q["last_mid"], 1)
                dve.wait_ge(q["carried_ready"], at(k - 2))
                dve.wait_ge(q["aggregated"], at(k - 2))
                v.tensor_tensor(outw[p2][:, 0:D + H], carried[:, :], psO[p2][:, 0:D + H], ALU.add).then_inc(
                    q["out_ready"], 1)
                dve.wait_ge(q["last_mid"], at(k))
                v.tensor_tensor(last3[:, :, 2 * H:M3], last3[:, :, H:2 * H], top3[:, :, 2 * H + 1:4 * H:2],
                                ALU.subtract).then_inc(q["last3_ready"], 1)
                if relational:
                    add_relation(k + 1, nx, now_next)
                dve.wait_ge(q["nodemax_done"], at(k))
                v.reduce_sum(stepmax[:, :, :], parts(psM[sl], M3 + 1), axis=AXX).then_inc(q["stepsum"], 1)
                v.tensor_scalar(absent[:, :], psM[sl].rearrange("p (u w) -> p u w", w=M3 + 1)[:, :, M3], -1.0, BIG,
                                ALU.add, ALU.mult).then_inc(q["absent_ready"], 1)
                if relational:
                    times_queries(k + 1, [0])
                else:
                    adst_top(pv, far, now_far)
                dve.wait_ge(q["stepsum"], at(k))
                dve.wait_ge(q["absent_ready"], at(k))
                v.tensor_tensor(stepmax[:, :, :], stepmax[:, :, :], bcast(absent[:, :].unsqueeze(2), [P, U, H]),
                                ALU.add).then_inc(q["stepmax_ready"], 1)
                if relational:
                    times_queries(k + 1, [1])
                else:
                    adst_mid(pv, far)
                dve.wait_ge(q["stepmax_ready"], at(k))
                v.reduce_max(winmax[:, :], stepmax[:, :, :].rearrange("p u h -> p h u"), axis=AXX).then_inc(
                    q["winmax_ready"], 1)
                if not relational:
                    adst_low(pv, far)
                dve.wait_ge(q["kept_max"], at(k - 1))
                dve.wait_ge(q["carrym_done"], at(k))
                dve.wait_ge(q["winmax_ready"], at(k))
                v.scalar_tensor_tensor(m3[sl][:, 0:H], psCm, r["rowneg"][:, rowi(k)], winmax[:, :], ALU.add,
                                       ALU.max).then_inc(q["m_ready"], 1)
                if not relational:
                    sum_parts(k + 1)
                dve.wait_ge(q["m_ready"], at(k))
                v.tensor_tensor(m3[sl][:, H:2 * H], m3[sl][:, 0:H], top(m3[sl][:, 0:H]), ALU.subtract).then_inc(
                    q["m_mid"], 1)
                if not relational:
                    add_source(k + 1, nx, now_next)
                dve.wait_ge(q["m_mid"], at(k))
                v.tensor_tensor(m3[sl][:, 2 * H:M3], m3[sl][:, H:2 * H], top(m3[sl][:, H:2 * H]),
                                ALU.subtract).then_inc(q["m3_ready"], 1)
                dve.wait_ge(q["rescale_ready"], at(k - 1))
                v.tensor_tensor(gin[:, :], psCm, m3[sl][:, 0:H], ALU.subtract).then_inc(q["gdiff"], 1)
                build_shift(k + 1, nx, at(k + 1))
                dve.wait_ge(q["gdiff"], at(k))
                v.tensor_scalar(gin[:, :], gin[:, :], 0.0, None, ALU.min).then_inc(q["gin_ready"], 1)
                if relational:
                    times_queries(k + 1, range(2, NQ))
                if not relational:
                    leaky(k + 1, nx)
                dve.wait_ge(q["prob_ready"], at(k - 1))
                dve.wait_ge(q["refmax_done"], at(k))
                v.reduce_sum(refmax[:, :, :], parts(psR[sl], M3), axis=AXX).then_inc(q["refsum"], 1)
                dve.wait_ge(q["refsum"], at(k))
                v.tensor_tensor(refmax[:, :, :], score[sl][:, :, :], refmax[:, :, :], ALU.subtract).then_inc(
                    q["expin_ready"], 1)
                dve.wait_ge(q["aggregated"], at(k - 2))
                build_onehot(k + 1, nx)
                ahead(k + 2, pv, far, now_far)
                if relational:
                    sum_products(k + 1, nx)
            passes(dve, body)

        @block.scalar
        def _(act):
            act.wait_ge(buffers_zero, 1)
            act.wait_ge(ready, 1)
            a = nc.scalar

            def body(i, k, sl, j):
                pv = (sl - 1) % SL
                act.wait_ge(ready, 1)
                act.wait_ge(q["nodemax_done"], at(k - 1))
                a.copy(last3[:, :, M3], r["islast"][:, rowi(k), :].rearrange("p a u -> p (a u)")).then_inc(
                    q["presence_ready"], 1)
                if AU:
                    act.wait_ge(q["prob_ready"], at(k - 1))
                    for u in range(U - AU, U):
                        for h in range(H):
                            ins = a.activation(ph[pv][:, u, h * C:(h + 1) * C], G[pv][:, u, V0 + h * C:V0 + (h + 1) * C],
                                               ACT.Copy, scale=ph[pv][:, u, D + h:D + h + 1])
                    ins.then_inc(q["weighted_act"], 1)
                act.wait_ge(out_stored[sl], 16 * (i + 2))
                act.wait_ge(q["m_ready"], at(k))
                a.copy(outw[sl][:, D + H:AW], m3[sl][:, 0:H]).then_inc(q["kept_max"], 1)
                act.wait_ge(q["carried_ready"], at(k - 3))
                act.wait_ge(q["gin_ready"], at(k))
                a.activation(gex[sl][:, :], gin[:, :], ACT.Exp).then_inc(q["rescale_ready"], 1)
                act.wait_ge(q["aggregated"], at(k - 3))
                act.wait_ge(q["expin_ready"], at(k))
                a.activation(ph[sl][:, :, D:D + H], refmax[:, :, :], ACT.Exp).then_inc(q["prob_ready"], 1)
            passes(act, body)

        @block.tensor
        def _(pe):
            t = nc.tensor
            pe.wait_ge(buffers_zero, 1)
            pe.wait_ge(ready, 1)
            cut = lambda u: slice(u * P, (u + 1) * P)
            early = min(3, U - AU)
            top_of = lambda ap: ap if ap.dtype == BF16 else top(ap)

            def queries(n, k, sl, in_now=None):
                if in_now is not None:
                    pe.wait_ge(window_in[sl], in_now)
                pe.wait_ge(q_used, NQ * at(k - 1) + n - 1)
                for e in range(2):
                    ins = t.matmul(psQ[n % 2][:, e * D:(e + 1) * D], onehotT[sl][:, cut(2 * n + e)],
                                   window[sl][:, :], start=True, stop=True)
                ins.then_inc(q_done, 1)

            def ahead(k, sl):
                pe.wait_ge(q["onehotT_ready"], at(k))
                if relational:
                    pe.wait_ge(q["modk_ready"], at(k - 1))
                    pe.wait_ge(q["typeT_ready"], at(k))
                    for u in range(U):
                        for n in range(3):
                            ins = t.matmul(psRel[:, u * C:(u + 1) * C], typeT[:, cut(u)], top(r["relw"][:, n, :]),
                                           start=(n == 0), stop=(n == 2))
                    ins.then_inc(q["rel_done"], 1)
                else:
                    pe.wait_ge(q["summed"], at(k - 1))
                    pe.wait_ge(q["w3_ready"], at(k))
                    for u in range(U):
                        ins = t.matmul(psA[:, u * M3:(u + 1) * M3], onehotT[sl][:, cut(u)], top(w3[:, :]),
                                       start=True, stop=True)
                    ins.then_inc(q["adst_done"], 1)

            def turn(k, sl):
                pe.wait_ge(ready, 1)
                pe.wait_ge(q["scan_done"], at(k - 1))
                pe.wait_ge(q["score_ready"], at(k))
                t.transpose(psT, flat(score[sl][:, :, :]), r["ident"][:, :]).then_inc(q["scoreT_done"], 1)

            ahead(1, 1)
            if relational:
                for n in range(NQ):
                    queries(n, 1, 1, None if n else 16)
            ahead(2, 2)
            if not relational:
                turn(1, 1)

            def body(i, k, sl, j):
                pv, p2, nx = (sl - 1) % SL, (sl - 2) % SL, (sl + 1) % SL

                def carry():
                    pe.wait_ge(q["out_ready"], at(k - 3))
                    pe.wait_ge(q["gdiff"], at(k - 1))
                    t.matmul(psC[:, 0:D + H], shift[p2][:, :], outw[sl][:, 0:D + H], start=True, stop=True).then_inc(
                        q["carry_done"], 1)
                    pe.wait_ge(q["shift_ready"], at(k))
                    t.matmul(psCm, shift[sl][:, :], m3[pv][:, 0:H], start=True, stop=True).then_inc(q["carrym_done"], 1)

                def turn_back():
                    pe.wait_ge(ready, 1)
                    pe.wait_ge(q["last_top"], at(k - 1))
                    pe.wait_ge(q["scan_done"], at(k))
                    t.transpose(psF, scanned[:, :], r["ident"][0:U * H, 0:U * H]).then_inc(q["scanback_done"], 1)

                def sums(us):
                    for u in us:
                        ins = t.matmul(psO[pv][:, 0:D + H], onehot[pv][:, u, :], ph[pv][:, u, :], start=(u == 0),
                                       stop=(u == U - 1))
                    return ins

                carry()
                if relational:
                    turn(k, sl)
                turn_back()
                if relational:
                    queries(0, k + 1, nx, loaded(i, j + 1))
                    queries(1, k + 1, nx)
                pe.wait_ge(q["presence_ready"], at(k))
                pe.wait_ge(q["stepsum"], at(k - 1))
                pe.wait_ge(q["absent_ready"], at(k - 1))
                pe.wait_ge(q["onehot_ready"], at(k))
                pe.wait_ge(q["last3_ready"], at(k))
                for u in range(U):
                    ins = t.matmul(psM[sl][:, u * (M3 + 1):(u + 1) * (M3 + 1)], top(onehot[sl][:, u, :]), top(last3[:, u, :]),
                                   start=True, stop=True)
                ins.then_inc(q["nodemax_done"], 1)
                pe.wait_ge(q["out_ready"], at(k - 3))
                pe.wait_ge(q["weighted"], at(k - 1))
                sums(range(early))
                if relational:
                    queries(2, k + 1, nx)
                    queries(3, k + 1, nx)
                pe.wait_ge(q["refsum"], at(k - 1))
                pe.wait_ge(q["m3_ready"], at(k))
                for u in range(U):
                    ins = t.matmul(psR[sl][:, u * M3:(u + 1) * M3], top_of(onehotT[sl][:, cut(u)]), top(m3[sl][:, :]),
                                   start=True, stop=True)
                ins.then_inc(q["refmax_done"], 1)
                if not relational:
                    turn(k + 1, nx)
                if AU:
                    pe.wait_ge(q["weighted_act"], at(k - 1))
                sums(range(early, U)).then_inc(q["aggregated"], 1)
                ahead(k + 2, pv)
            passes(pe, body)
    s.close()


def edgeconv_stage(nc, d, r, tag):
    s = Stage(nc, tag)
    NG, NB = 4, U // 2
    idx = [s.sb(f"idx{j}", [P, U], I32) for j in range(SL)]
    G = [s.sb(f"G{j}", [P, U, D]) for j in range(SL)]
    firstrow = [s.sb(f"firstrow{j}", [P, CHUNK], BF16) for j in range(SL)]
    onehot = [s.sb(f"onehot{j}", [P, U, P]) for j in range(SL)]
    scanned = [[s.sb(f"scanned{j}_{h}", [P, CHUNK]) for h in range(2)] for j in range(SL)]
    back = [s.sb(f"back{j}", [P, U, XW]) for j in range(SL)]
    outw = [s.sb(f"outw{j}", [P, XW]) for j in range(SL)]
    psT = [s.ps(f"psT{i}", [P, 512]) for i in range(4)]
    psB = [s.ps(f"psB{i}", [P, 512]) for i in range(3)]
    psO = s.ps("psO", [P, 512])
    ready = s.sem("ready")
    gathered = [[nc.alloc_semaphore(f"{tag}_gathered{j}_{u}") for u in range(U)] for j in range(SL)]
    firstrow_in = [s.sem(f"firstrow_in{j}") for j in range(SL)]
    out_stored = [s.sem(f"out_stored{j}") for j in range(SL)]
    idx_ready, onehot_ready, selected, out_ready = (s.sem(n) for n in (
        "idx_ready", "onehot_ready", "selected", "out_ready"))
    turned, scan_done, back_done, back_ready = (s.sem(n) for n in ("turned", "scan_done", "back_done", "back_ready"))
    buffers_zero, all_stored = s.sem("buffers_zero"), s.sem("all_stored")
    store_due = s.sem("store_due")
    at = lambda k: k + SL
    at4 = lambda k: NG * (k + SL)
    rowi = lambda k: bass.ds(k, 1)
    loaded = lambda i, j: 16 * (i + 1 + j // SL)

    def passes(eng, body):
        nit = eng.value_load(r["nits_i"][0:1, 0:1], min_val=1, max_val=NIT)
        with eng.Fori(0, NIT) as i:
            with eng.If(i < nit):
                for j in range(SL):
                    body(i, SL * i + j + 1, (j + 1) % SL, j)
        return nit

    with nc.Block() as block:
        @block.gpsimd
        def _(pool):
            for x in (onehot_ready, selected, out_ready):
                pool.sem_inc(x, SL)
            for x in (turned, scan_done, back_done, back_ready):
                pool.sem_inc(x, NG * SL)
            pool.sem_inc(ready, 1)

            def body(i, k, sl, j):
                pool.wait_ge(ready, 1)
                mine = pool.snap(at(k - SL))
                pool.wait_ge(turned, at4(k - SL))
                nc.gpsimd.tensor_copy(idx[sl][:, :], r["src_pass"][:, rowi(k), :].rearrange(
                    "p a u -> p (a u)")).then_inc(idx_ready, 1)
                pool.wait_ge(ready, 1)
                pool.wait_ge(idx_ready, mine)
                for u in range(U):
                    nc.gpsimd.indirect_dma_start(
                        G[sl][:, u, :], None, d["bx"],
                        bass.IndirectOffsetOnAxis(ap=idx[sl][:, u:u + 1], axis=0)).then_inc(gathered[sl][u], 16)
            passes(pool, body)

        @block.sync
        def _(sp):
            prime(sp, outw, out_stored, 16, r)

            def load(k, sl):
                sp.dma_start(firstrow[sl][:, :], bcast(d["firstrow"][rowi(k), :], [P, CHUNK])).then_inc(firstrow_in[sl], 16)

            load(1, 1)
            sp.wait_ge(ready, 1)

            def body(i, k, sl, j):
                sp.wait_ge(scan_done, at4(k - 2))
                load(k + 1, (sl + 1) % SL)
                n0 = sp.value_load(r["n0_i"][0:1, bass.ds(k + 2, 1)], min_val=0, max_val=N)
                before = 16 * (i + (2 if j else 1))
                sp.wait_ge(out_stored[(sl - 1) % SL], before)
                sp.sem_inc(store_due, 1)
                sp.wait_ge(out_ready, at(k))
                sp.sem_inc(store_due, 1)
                sp.dma_start(d["aggx"][bass.ds(n0, P), :], outw[sl][:, :]).then_inc(out_stored[sl], 16)
            nit = passes(sp, body)
            seen = sp.snap(16 * (nit + 1))
            sp.wait_ge(ready, 1)
            for j in range(SL):
                sp.wait_ge(out_stored[j], seen)
            sp.wait_ge(firstrow_in[1], seen)
            sp.sem_inc(all_stored, 1)

        @block.vector
        def _(dve):
            v = nc.vector
            for j in range(SL):
                v.memset(back[j][:, :, D:XW], 1.0)
            for h in range(2):
                v.memset(scanned[0][h][:, :], 0.0).then_inc(buffers_zero, 1)
            dve.wait_ge(ready, 1)
            dve.wait_ge(buffers_zero, 2)

            def body(i, k, sl, j):
                pv = (sl - 1) % SL
                dve.wait_ge(selected, at(k - SL))
                loc = r["lastloc"][:, rowi(k), :].rearrange("p a u -> p (a u)").unsqueeze(2)
                v.tensor_tensor(onehot[sl][:, :, :], bcast(loc, [P, U, P]),
                                bcast(r["iota_row"][:, :].unsqueeze(1), [P, U, P]), ALU.is_equal).then_inc(onehot_ready, 1)
                dve.wait_ge(firstrow_in[sl], loaded(i, j))
                dve.wait_ge(back_done, at4(k - SL))
                for n in range(NG):
                    a, h = n // 2, n % 2
                    cols = slice(a * 512, (a + 1) * 512)
                    start = scanned[sl][h][:, 511:512] if a else scanned[pv][h][:, CHUNK - 1:CHUNK]
                    dve.wait_ge(scan_done, at4(k - 1) + n - 1)
                    dve.wait_ge(turned, at4(k - 1) + n + 1)
                    v.tensor_tensor_scan(scanned[sl][h][:, cols], firstrow[sl][:, cols], psT[n][:, :], start,
                                         ALU.add, ALU.max).then_inc(scan_done, 1)
            passes(dve, body)

        @block.scalar
        def _(act):
            for j in range(SL):
                act.wait_ge(out_stored[j], 16)
            act.wait_ge(ready, 1)

            def body(i, k, sl, j):
                act.wait_ge(selected, at(k - SL))
                for n in range(NB):
                    act.wait_ge(back_done, at4(k - 1) + n + 1)
                    nc.scalar.copy(back[sl][:, 2 * n:2 * n + 2, 0:D],
                                   psB[(NB * j + n) % 3][:, :].rearrange("p (u n) -> p u n", u=2)).then_inc(back_ready, 1)
                act.wait_ge(out_stored[sl], 16 * (i + 1))
                act.wait_ge(selected, at(k))
                nc.scalar.copy(outw[sl][:, :], psO[:, 0:XW]).then_inc(out_ready, 1)
            passes(act, body)

        @block.tensor
        def _(pe):
            t = nc.tensor
            pe.wait_ge(ready, 1)
            pe.wait_ge(buffers_zero, 2)

            def body(i, k, sl, j):
                for u in range(U):
                    pe.wait_ge(gathered[sl][u], 16 * (i + 1))
                for n in range(NG):
                    a, h = n // 2, n % 2
                    pe.wait_ge(ready, 1)
                    pe.wait_ge(scan_done, at4(k - 1) + n + 1 - NG)
                    for u in range(4):
                        ins = t.transpose(psT[n][:, u * P:(u + 1) * P], G[sl][:, 4 * a + u, h * P:(h + 1) * P],
                                          r["ident"][:, :])
                    ins.then_inc(turned, 1)
                for n in range(NB):
                    pe.wait_ge(ready, 1)
                    pe.wait_ge(back_ready, at4(k - 1) + n + 1 - 3)
                    pe.wait_ge(scan_done, at4(k - 1) + 2 * (n // 2) + 2)
                    for u in (2 * n, 2 * n + 1):
                        for h in range(2):
                            ins = t.transpose(psB[(NB * j + n) % 3][:, (u - 2 * n) * D + h * P:(u - 2 * n) * D + (h + 1) * P],
                                              scanned[sl][h][:, u * P:(u + 1) * P], r["ident"][:, :])
                    ins.then_inc(back_done, 1)
                pe.wait_ge(out_ready, at(k - 1))
                pe.wait_ge(onehot_ready, at(k))
                pe.wait_ge(back_ready, at4(k))
                for u in range(U):
                    ins = t.matmul(psO[:, 0:XW], onehot[sl][:, u, :], back[sl][:, u, :], start=(u == 0), stop=(u == U - 1))
                ins.then_inc(selected, 1)
            passes(pe, body)
    s.close()


def coefficient_stage(nc, d, r, tag, kind, ca, cs):
    s = Stage(nc, tag)
    T4 = [P, TILES, H]
    aux = s.sb("aux", [P, TILES, 2 * H])
    own = s.sb("own", [P, TILES, 2 * H])
    tmp = [s.sb(f"tmp{i}", T4) for i in range(4)]
    loaded, dve_step, ex_in, ex_out = s.sem("loaded"), s.sem("dve_step"), s.sem("ex_in"), s.sem("ex_out")
    tiles = lambda dram: dram.rearrange("(t p) w -> p t w", p=P)
    with nc.Block() as block:
        @block.sync
        def _(sp):
            sp.dma_start(aux[:, :, :], tiles(d["agg"])[:, :, D:AW]).then_inc(loaded, 16)
            if kind != "relational":
                sp.dma_start(own[:, :, :], tiles(d["h"])[:, :, D:GW]).then_inc(loaded, 16)

        @block.scalar
        def _(act):
            if kind != "relational":
                act.wait_ge(ex_in, 2)
                nc.scalar.activation(tmp[0][:, :, :], tmp[0][:, :, :], ACT.Exp)
                nc.scalar.activation(tmp[1][:, :, :], tmp[1][:, :, :], ACT.Exp).then_inc(ex_out, 1)

        @block.vector
        def _(dve):
            v, c = nc.vector, Chain(dve, dve_step)
            den, mx = aux[:, :, 0:H], aux[:, :, H:2 * H]
            ea, es, empty, x = (t[:, :, :] for t in tmp)
            dve.wait_ge(loaded, 16 if kind == "relational" else 32)
            c.do(v.tensor_scalar(empty, den, 0.0, None, ALU.is_equal))
            if kind == "relational":
                c.do(v.tensor_tensor(den, den, empty, ALU.add))
                c.do(v.reciprocal(ca[:, :, :], den))
                c.do(v.tensor_copy(cs[:, :, :], empty))
                return
            c.do(v.tensor_tensor(x, own[:, :, 0:H], own[:, :, H:2 * H], ALU.add))
            c.do(v.scalar_tensor_tensor(es, x, 0.2, x, ALU.mult, ALU.max))
            c.do(v.tensor_tensor(x, mx, es, ALU.max))
            v.tensor_tensor(ea, mx, x, ALU.subtract).then_inc(ex_in, 1)
            v.tensor_tensor(es, es, x, ALU.subtract).then_inc(ex_in, 1)
            dve.wait_ge(ex_out, 1)
            c.do(v.tensor_tensor(x, den, ea, ALU.mult))
            c.do(v.tensor_tensor(x, x, es, ALU.add))
            if kind == "relu":
                c.do(v.tensor_scalar(x, x, 1e-16, None, ALU.add))
            c.do(v.reciprocal(x, x))
            c.do(v.tensor_tensor(ca[:, :, :], ea, x, ALU.mult))
            c.do(v.tensor_tensor(cs[:, :, :], es, x, ALU.mult))
    s.close()


def stats_stage(nc, r, tag, mv):
    s = Stage(nc, tag)
    dve_step, var_ready, root_ready = s.sem("dve_step"), s.sem("var_ready"), s.sem("root_ready")
    with nc.Block() as block:
        @block.vector
        def _(dve):
            v, c = nc.vector, Chain(dve, dve_step)
            c.do(v.tensor_copy(r["mean"][:, :], mv[:, :, 0]))
            v.tensor_scalar(r["rstd"][:, :], mv[:, :, 1], EPS, None, ALU.add).then_inc(var_ready, 1)
            dve.wait_ge(root_ready, 1)
            c.do(v.reciprocal(r["rstd"][:, :], r["rstd"][:, :]))

        @block.scalar
        def _(act):
            act.wait_ge(var_ready, 1)
            nc.scalar.activation(r["rstd"][:, :], r["rstd"][:, :], ACT.Sqrt).then_inc(root_ready, 1)
    s.close()


def waves(steps, tiles):
    for w in range(tiles + len(steps) - 1):
        for lag in reversed(range(len(steps))):
            if 0 <= w - lag < tiles:
                steps[lag](w - lag)


def statistics(dve, v, i, y, mv, st, mvt, ready, q, at, B):
    def stats(b):
        t = i * B + b
        dve.wait_ge(ready, 1)
        dve.wait_ge(q["y_ready"], at(t))
        v.bn_stats(st[b % NB][:, :], y[:, bass.ds(t * D, D)]).then_inc(q["stats_ready"], 1)

    def aggregate(b):
        dve.wait_ge(ready, 1)
        dve.wait_ge(q["stats_ready"], at(i * B + b))
        v.bn_aggr(mvt[:, b, :], st[b % NB][:, :]).then_inc(q["aggr_ready"], 1)

    def keep():
        dve.wait_ge(q["aggr_ready"], at(i * B + B - 1))
        v.tensor_scalar(mv[:, bass.ds(i * B, B), :], mvt[:, :, :], 1.0, None, ALU.mult).then_inc(q["mv_kept"], 1)
        dve.wait_ge(q["mv_kept"], i + 2)
    return stats, aggregate, keep


def combine_stage(nc, d, r, y, tag, kind, ca, cs, mv, bias):
    s = Stage(nc, tag)
    B = 10
    IT = TILES // B
    att = kind != "conv"
    dram_a, wa = (d["agg"], D) if att else (d["aggx"], XW)
    dram_h = {"relu": d["h"][:, 0:D], "elu": d["h"][:, 0:D], "relational": d["kv"][:, D:2 * D], "conv": d["ax"]}[kind]
    acc = [s.sb(f"acc{b}", [P, wa]) for b in range(NB)]
    hv = [s.sb(f"hv{b}", [P, D]) for b in range(NB)]
    xt = [s.sb(f"xt{b}", [P, D]) for b in range(NB)]
    hs = [s.sb(f"hs{b}", [P, D]) for b in range(NB)]
    ta = [s.sb(f"ta{b}", [P, D]) for b in range(NB)]
    tb = [s.sb(f"tb{b}", [P, D]) for b in range(NB)]
    st = [s.sb(f"st{b}", [P, 6]) for b in range(NB)]
    mvt = s.sb("mvt", [P, B, 2])
    psT = [s.ps(f"psT{b}", [P, 512]) for b in range(2)]
    psW = [s.ps(f"psW{b}", [P, 512]) for b in range(2)]
    loaded = [s.sem(f"loaded{b}") for b in range(NB)]
    ready = s.sem("ready")
    names = ["own_scaled", "own_ready", "x_ready", "scaled", "summed", "exp_ready", "relu_ready", "turned", "xT_ready",
             "product_done", "half_done", "y_ready", "stats_ready", "aggr_ready"]
    q = {n: s.sem(n) for n in names}
    q["mv_kept"] = s.sem("mv_kept")
    at = lambda t: t + 1 + NB
    loads = lambda i, b: 48 * (i * (B // NB) + b // NB + 1)
    heads = lambda ap: ap.rearrange("p (h c) -> p h c", c=C)
    coef = lambda c, t: bcast(c[:, bass.ds(t, 1), :].rearrange("p a h -> p (a h)").unsqueeze(2), [P, H, C])
    with nc.Block() as block:
        @block.sync
        def _(sp):
            sp.wait_ge(ready, 1)
            with sp.Fori(0, IT) as i:
                for b in range(B):
                    t, n = i * B + b, b % NB
                    sp.wait_ge(q["y_ready"], at(t - NB))
                    rows = bass.ds(t * P, P)
                    sp.dma_start(acc[n][:, :], dram_a[rows, 0:wa]).then_inc(loaded[n], 16)
                    sp.dma_start(hv[n][:, :], dram_h[rows, :]).then_inc(loaded[n], 16)
                    sp.dma_start(xt[n][:, :], d["x"][rows, :]).then_inc(loaded[n], 16)

        @block.gpsimd
        def _(pool):
            for n, x in q.items():
                pool.sem_inc(x, 1 if n == "mv_kept" else NB)
            pool.sem_inc(ready, 1)
            g = nc.gpsimd
            with pool.Fori(0, IT) as i:
                def own(b):
                    t, n = i * B + b, b % NB
                    pool.wait_ge(ready, 1)
                    pool.wait_ge(q["y_ready"], at(t - NB))
                    pool.wait_ge(loaded[n], loads(i, b))
                    if not att:
                        g.tensor_tensor(hs[n][:, :], hv[n][:, :], acc[n][:, 0:D], ALU.add).then_inc(q["own_ready"], 1)
                        return
                    done = q["own_ready" if kind == "relational" else "own_scaled"]
                    g.tensor_tensor(heads(hs[n][:, :]), heads(hv[n][:, :]), coef(cs, t), ALU.mult).then_inc(done, 1)
                    if kind == "relational":
                        g.tensor_tensor(xt[n][:, :], xt[n][:, :], bias, ALU.add).then_inc(q["x_ready"], 1)

                def add_bias(b):
                    t, n = i * B + b, b % NB
                    pool.wait_ge(ready, 1)
                    pool.wait_ge(q["own_scaled"], at(t))
                    g.tensor_tensor(hs[n][:, :], hs[n][:, :], bias, ALU.add).then_inc(q["own_ready"], 1)
                waves([own, add_bias] if kind in ("relu", "elu") else [own], B)

        @block.vector
        def _(dve):
            v = nc.vector
            dve.wait_ge(ready, 1)
            with dve.Fori(0, IT) as i:
                def scale(b):
                    t, n = i * B + b, b % NB
                    dve.wait_ge(q["y_ready"], at(t - NB))
                    if kind == "relational":
                        dve.wait_ge(q["turned"], at(t - NB))
                    dve.wait_ge(loaded[n], loads(i, b))
                    v.tensor_tensor(heads(ta[n][:, :]), heads(acc[n][:, :]), coef(ca, t), ALU.mult).then_inc(q["scaled"], 1)

                def add_own(b):
                    t, n = i * B + b, b % NB
                    dve.wait_ge(q["own_ready"], at(t))
                    dve.wait_ge(q["scaled"], at(t))
                    v.tensor_tensor(ta[n][:, :], ta[n][:, :], hs[n][:, :], ALU.add).then_inc(q["summed"], 1)

                def clip(b):
                    t, n = i * B + b, b % NB
                    dve.wait_ge(q["y_ready"], at(t - NB))
                    dve.wait_ge(q["own_ready"], at(t))
                    v.tensor_scalar(ta[n][:, :], hs[n][:, :], 0.0, acc[n][:, D:XW], ALU.max, ALU.mult).then_inc(q["summed"], 1)

                def elu(b):
                    t, n = i * B + b, b % NB
                    dve.wait_ge(q["relu_ready"], at(t))
                    v.scalar_tensor_tensor(tb[n][:, :], tb[n][:, :], 1.0, ta[n][:, :], ALU.min, ALU.add).then_inc(
                        q["half_done"], 1)

                def residual(b):
                    t, n = i * B + b, b % NB
                    yt = y[:, bass.ds(t * D, D)]
                    if kind == "relu":
                        dve.wait_ge(q["summed"], at(t))
                        ins = v.scalar_tensor_tensor(yt, ta[n][:, :], 0.0, xt[n][:, :], ALU.max, ALU.add)
                    elif kind == "elu":
                        dve.wait_ge(q["half_done"], at(t))
                        ins = v.scalar_tensor_tensor(yt, tb[n][:, :], -1.0, xt[n][:, :], ALU.add, ALU.add)
                    elif kind == "relational":
                        dve.wait_ge(q["x_ready"], at(t))
                        dve.wait_ge(q["product_done"], at(t))
                        ins = v.tensor_tensor(yt, psW[b % 2][:, 0:D], xt[n][:, :], ALU.add)
                    else:
                        dve.wait_ge(q["summed"], at(t))
                        ins = v.tensor_tensor(yt, ta[n][:, :], xt[n][:, :], ALU.add)
                    ins.then_inc(q["y_ready"], 1)

                stats, aggregate, keep = statistics(dve, v, i, y, mv, st, mvt, ready, q, at, B)
                nothing = lambda b: None
                waves({"relu": [scale, add_own, residual], "elu": [scale, add_own, nothing, elu, residual],
                       "relational": [scale, add_own, nothing, nothing, residual], "conv": [clip, residual]}[kind]
                      + [stats, aggregate], B)
                keep()

        @block.scalar
        def _(act):
            act.wait_ge(ready, 1)
            if kind in ("elu", "relational"):
                with act.Fori(0, IT) as i:
                    for b in range(B):
                        t, n = i * B + b, b % NB
                        if kind == "elu":
                            act.wait_ge(q["y_ready"], at(t - NB))
                            act.wait_ge(q["summed"], at(t))
                            nc.scalar.activation(tb[n][:, :], ta[n][:, :], ACT.Exp).then_inc(q["exp_ready"], 1)
                            act.wait_ge(q["exp_ready"], at(t))
                            nc.scalar.activation(ta[n][:, :], ta[n][:, :], ACT.Relu).then_inc(q["relu_ready"], 1)
                        else:
                            act.wait_ge(q["product_done"], at(t - NB))
                            act.wait_ge(q["turned"], at(t))
                            nc.scalar.copy(tb[n][:, :], psT[b % 2][:, 0:D]).then_inc(q["xT_ready"], 1)

        @block.tensor
        def _(pe):
            pe.wait_ge(ready, 1)
            if kind == "relational":
                w = r["wo"]
                with pe.Fori(0, IT) as i:
                    def turn(b):
                        t, x = i * B + b, ta[b % NB]
                        pe.wait_ge(ready, 1)
                        pe.wait_ge(q["xT_ready"], at(t - 2))
                        pe.wait_ge(q["summed"], at(t))
                        nc.tensor.transpose(psT[b % 2][:, 0:P], x[:, 0:P], r["ident"][:, :])
                        nc.tensor.transpose(psT[b % 2][:, P:D], x[:, P:D], r["ident"][:, :]).then_inc(q["turned"], 1)

                    def multiply(b):
                        t, x = i * B + b, tb[b % NB]
                        pe.wait_ge(q["y_ready"], at(t - 2))
                        pe.wait_ge(q["xT_ready"], at(t))
                        nc.tensor.matmul(psW[b % 2][:, 0:D], x[:, 0:P], w[:, 0, :], start=True, stop=False)
                        nc.tensor.matmul(psW[b % 2][:, 0:D], x[:, P:D], w[:, 1, :], start=False,
                                         stop=True).then_inc(q["product_done"], 1)
                    waves([turn, lambda b: None, multiply], B)
    s.close()


def affine_stage(nc, d, r, y, tag, mv):
    s = Stage(nc, tag)
    B = 10
    IT = TILES // B
    xt = [s.sb(f"xt{b}", [P, D]) for b in range(NB)]
    z = [s.sb(f"z{b}", [P, D]) for b in range(NB)]
    st = [s.sb(f"st{b}", [P, 6]) for b in range(NB)]
    mvt = s.sb("mvt", [P, B, 2])
    loaded = [s.sem(f"loaded{b}") for b in range(NB)]
    ready = s.sem("ready")
    q = {n: s.sem(n) for n in ("xb_ready", "z_ready", "zg_ready", "y_ready", "stats_ready", "aggr_ready")}
    q["mv_kept"] = s.sem("mv_kept")
    at = lambda t: t + 1 + NB
    with nc.Block() as block:
        @block.sync
        def _(sp):
            sp.wait_ge(ready, 1)
            with sp.Fori(0, IT) as i:
                for b in range(B):
                    t = i * B + b
                    sp.wait_ge(q["y_ready"], at(t - NB))
                    sp.dma_start(xt[b % NB][:, :], d["x"][bass.ds(t * P, P), :]).then_inc(loaded[b % NB], 16)

        @block.gpsimd
        def _(pool):
            for n, x in q.items():
                pool.sem_inc(x, 1 if n == "mv_kept" else NB)
            pool.sem_inc(ready, 1)
            with pool.Fori(0, IT) as i:
                for b in range(B):
                    x = xt[b % NB]
                    pool.wait_ge(ready, 1)
                    pool.wait_ge(loaded[b % NB], 16 * (i * (B // NB) + b // NB + 1))
                    nc.gpsimd.tensor_tensor(x[:, :], x[:, :], r["beta"][:, :], ALU.add).then_inc(q["xb_ready"], 1)

        @block.vector
        def _(dve):
            v = nc.vector
            dve.wait_ge(ready, 1)
            with dve.Fori(0, IT) as i:
                def normalize(b):
                    t = i * B + b
                    dve.wait_ge(q["y_ready"], at(t - NB))
                    v.tensor_scalar(z[b % NB][:, :], y[:, bass.ds(t * D, D)], r["mean"][:, bass.ds(t, 1)],
                                    r["rstd"][:, bass.ds(t, 1)], ALU.subtract, ALU.mult).then_inc(q["z_ready"], 1)

                def times_gamma(b):
                    zb = z[b % NB]
                    dve.wait_ge(q["z_ready"], at(i * B + b))
                    v.tensor_tensor(zb[:, :], zb[:, :], r["gamma"][:, :], ALU.mult).then_inc(q["zg_ready"], 1)

                def residual(b):
                    t = i * B + b
                    dve.wait_ge(q["xb_ready"], at(t))
                    dve.wait_ge(q["zg_ready"], at(t))
                    v.tensor_tensor(y[:, bass.ds(t * D, D)], z[b % NB][:, :], xt[b % NB][:, :], ALU.add).then_inc(
                        q["y_ready"], 1)

                stats, aggregate, keep = statistics(dve, v, i, y, mv, st, mvt, ready, q, at, B)
                waves([normalize, times_gamma, residual, stats, aggregate], B)
                keep()
    s.close()


def output_stage(nc, d, r, y, out):
    s = Stage(nc, "output")
    B = 5
    xo = [s.sb(f"xo{b}", [P, D]) for b in range(B)]
    stored = [s.sem(f"stored{b}") for b in range(B)]
    norm_done, ready = s.sem("norm_done"), s.sem("ready")
    at = lambda t: t + 1
    with nc.Block() as block:
        @block.sync
        def _(sp):
            prime(sp, xo, stored, 16, r)
            with sp.Fori(0, TILES // B) as i:
                for b in range(B):
                    t = i * B + b
                    sp.wait_ge(norm_done, at(t))
                    sp.dma_start(out[bass.ds(t * P, P), :], xo[b][:, :]).then_inc(stored[b], 16)
            for b in range(B):
                sp.wait_ge(stored[b], 16 * (1 + TILES // B))

        @block.vector
        def _(dve):
            with dve.Fori(0, TILES // B) as i:
                for b in range(B):
                    t = i * B + b
                    dve.wait_ge(stored[b], 16 * (i + 1))
                    nc.vector.tensor_scalar(xo[b][:, :], y[:, bass.ds(t * D, D)], r["mean"][:, bass.ds(t, 1)],
                                            r["rstd"][:, bass.ds(t, 1)], ALU.subtract, ALU.mult).then_inc(norm_done, 1)
    s.close()


def load_x_stage(nc, r, y):
    s = Stage(nc, "loadx")
    loaded = s.sem("loaded")
    with nc.Block() as block:
        @block.sync
        def _(sp):
            sp.dma_start(y[:, :].rearrange("p (t n) -> p t n", n=D),
                         r["x_dram"].rearrange("(t p) n -> p t n", p=P)).then_inc(loaded, 16)
            sp.wait_ge(loaded, 16)
    s.close()


def graph_layers(nc, d, out):
    dram = lambda name, shape, dt=F32: nc.dram_tensor(name, shape, dt, kind="Internal").ap()
    d["x"] = dram("x_kept", (ROWS, D))
    d["h"] = dram("h_table", (ROWS, GW))
    d["kv"] = dram("kv_table", (ROWS, 2 * D))
    d["q"] = dram("q_table", (ROWS, D))
    d["bx"] = dram("source_table", (ROWS, D))
    d["ax"] = dram("destination_table", (ROWS, D))
    d["agg"] = dram("aggregates", (ROWS, AW))
    d["aggx"] = dram("maxima", (ROWS, XW))
    d["dstrow"] = dram("dstrow", (NK, CHUNK), BF16)
    d["firstrow"] = dram("firstrow", (NK, CHUNK), BF16)
    d["firstrow4"] = dram("firstrow4", (NK, H * CHUNK), BF16)
    d["typrow"] = dram("typrow", (NK, CHUNK), BF16)
    ctx = ExitStack()
    with ctx:
        def sb(name, shape, dt=F32):
            return ctx.enter_context(nc.sbuf_tensor(name, shape, dt))
        r = {"x_dram": d["x_in"]}
        for name, shape in (("iota_row", [P, P]), ("iota_col", [P, 1]), ("ident", [P, P]), ("dstloc", [P, NK, U]),
                            ("islast", [P, NK, U]), ("lastloc", [P, NK, U]), ("delta", [P, NK]), ("rowneg", [P, NK]), ("w0", [P, 2, GW]),
                            ("w2", [P, 2, GW]), ("wkvq", [P, 2, 3 * D]), ("wo", [P, 2, D]), ("w3", [P, 2, 2 * D]),
                            ("relw", [NREL, 3, C]), ("b0", [P, D]), ("b1", [P, 3 * D]), ("b2", [P, D]), ("b3", [P, 2 * D]),
                            ("bo", [P, D]), ("gamma", [P, D]), ("beta", [P, D]),
                            ("mean", [P, TILES]), ("rstd", [P, TILES])):
            r[name] = sb(name, shape)
        r["iota_i"] = sb("iota_i", [P, P + NK + 1], I32)
        r["src_pass"] = sb("src_pass", [P, NK, U], I32)
        r["n0_i"] = sb("n0_i", [1, NK + 2], I32)
        r["nits_i"] = sb("nits_i", [1, 1], I32)
        setup_stage(nc, d, r)

        def project(y, layer):
            if layer in (0, 2):
                project_stage(nc, d, r, y, f"project{layer}", r[f"w{layer}"], None, GW, [(0, GW, d["h"])])
            elif layer == 1:
                project_stage(nc, d, r, y, "project1", r["wkvq"], r["b1"][:, :], 3 * D,
                              [(0, 2 * D, d["kv"]), (2 * D, 3 * D, d["q"])])
            else:
                project_stage(nc, d, r, y, "project3", r["w3"], r["b3"][:, :], 2 * D,
                              [(0, D, d["bx"]), (D, 2 * D, d["ax"])])

        with nc.sbuf_tensor("y_in", [P, TILES * D], F32) as y:
            load_x_stage(nc, r, y)
            project(y, 0)
        for layer, kind in enumerate(("relu", "relational", "elu", "conv")):
            if kind == "conv":
                edgeconv_stage(nc, d, r, "edges3")
            else:
                edge_stage(nc, d, r, f"edges{layer}", kind == "relational")
            with ExitStack() as nodes:
                y = nodes.enter_context(nc.sbuf_tensor(f"y{layer}", [P, TILES * D], F32))
                mv = nodes.enter_context(nc.sbuf_tensor(f"mv{layer}", [P, TILES, 2], F32))
                ca = nodes.enter_context(nc.sbuf_tensor(f"ca{layer}", [P, TILES, H], F32))
                cs = nodes.enter_context(nc.sbuf_tensor(f"cs{layer}", [P, TILES, H], F32))
                if kind != "conv":
                    coefficient_stage(nc, d, r, f"coef{layer}", kind, ca, cs)
                bias = {"relu": r["b0"], "relational": r["bo"], "elu": r["b2"], "conv": r["b0"]}[kind][:, :]
                combine_stage(nc, d, r, y, f"combine{layer}", kind, ca, cs, mv, bias)
                stats_stage(nc, r, f"stats{layer}", mv)
                if kind == "relational":
                    affine_stage(nc, d, r, y, "affine", mv)
                    stats_stage(nc, r, "stats_affine", mv)
                if kind == "conv":
                    output_stage(nc, d, r, y, out)
                else:
                    project(y, layer + 1)


def kernel(**inputs):
    import numpy as np
    import concourse.bacc as bacc
    from concourse.bass_utils import run_bass_kernel_spmd

    arr = {k: np.asarray(v) for k, v in inputs.items()}
    x = np.zeros((ROWS, D), np.float32)
    x[:N] = arr["x"]
    dst = np.full(1 + NCH * CHUNK + 1, PAD_DST, np.int32)
    dst[0] = -1
    dst[1:1 + E] = arr["dst"]
    src = np.zeros(NCH * CHUNK, np.int32)
    src[:E] = arr["src"]
    typ = np.zeros(NCH * CHUNK, np.int32)
    typ[:E] = arr["edge_type_64"]
    feeds = {
        "x_in": x, "dst": dst, "src": src.reshape(NCH, CHUNK), "typ": typ.reshape(NCH, CHUNK),
        "W0": arr["L0_gnn_W"], "as0": arr["L0_gnn_att_src"], "ad0": arr["L0_gnn_att_dst"], "b0": arr["L0_gnn_bias"],
        "W2": arr["L2_gnn_W"], "as2": arr["L2_gnn_att_src"], "ad2": arr["L2_gnn_att_dst"], "b2": arr["L2_gnn_bias"],
        "query": arr["L1_gnn_query_emb"], "Wq": arr["L1_gnn_Wq"], "bq": arr["L1_gnn_bq"], "Wk": arr["L1_gnn_Wk"],
        "bk": arr["L1_gnn_bk"], "Wv": arr["L1_gnn_Wv"], "bv": arr["L1_gnn_bv"], "rel": arr["L1_gnn_rel_w"],
        "Wo": arr["L1_gnn_Wo"], "bo": arr["L1_gnn_bo"], "gamma": arr["L1_gnn_gamma"], "beta": arr["L1_gnn_beta"],
        "thetaT": np.ascontiguousarray(arr["L3_gnn_theta_w"].T), "theta_b": arr["L3_gnn_theta_b"],
        "phiT": np.ascontiguousarray(arr["L3_gnn_phi_w"].T), "phi_b": arr["L3_gnn_phi_b"],
    }
    nc = bacc.Bacc("TRN2", target_bir_lowering=False, num_devices=1)
    d, given = {}, {}
    for name, a in feeds.items():
        a = np.ascontiguousarray(a)
        given[f"in_{name}"] = a
        d[name] = nc.dram_tensor(f"in_{name}", a.shape, mybir.dt.from_np(a.dtype), kind="ExternalInput").ap()
    out = nc.dram_tensor("out", (ROWS, D), F32, kind="ExternalOutput").ap()
    graph_layers(nc, d, out)
    result = run_bass_kernel_spmd(nc, [given], core_ids=[0])
    return result.results[0]["out"][:N]
```
